# Optimizing a Trainium2 kernel written in Bass

```python
import numpy as np
import jax
import jax.numpy as jnp

def _softmax(x, axis=-1):
    return jax.nn.softmax(x, axis=axis)

def _gelu(x):
    return jax.nn.gelu(x, approximate=True)

def _silu(x):
    return jax.nn.silu(x)

def _sigmoid(x):
    return jax.nn.sigmoid(x)

def _layernorm(x, axis=-1, eps=1e-05):
    m = jnp.mean(x, axis=axis, keepdims=True)
    v = jnp.var(x, axis=axis, keepdims=True)
    return (x - m) / jnp.sqrt(v + eps)

def _scatter_add(tgt, idx, src, axis=0):
    return tgt.at[idx].add(src)

def _segment_sum(src, seg, n):
    return jax.ops.segment_sum(src, seg, n)
kernel_name = 'mk_xattn_seq_d2_seqx_r8_76de83'

def setup_inputs(seed: int=0):
    np.random.seed(seed)
    _w = jnp.asarray

    def _rec_inputs():
        import jax
        import jax.numpy as jnp
        _rk = jax.random.key(seed)
        x = -0.0002928 + 1 * jax.random.normal(jax.random.fold_in(_rk, 1), (16, 64, 256), jnp.float32)
        _lenS = 64 - jax.random.randint(jax.random.fold_in(_rk, 7), (16,), 0, max(1, 64 // 4) + 1, jnp.int32)
        _lenS2 = 64 - jax.random.randint(jax.random.fold_in(_rk, 8), (16,), 0, max(1, 64 // 4) + 1, jnp.int32)
        _ctx_2048P = jax.random.normal(jax.random.fold_in(_rk, 11), (16, 16, 256), jnp.float32)
        _ctx_2048c = jax.random.dirichlet(jax.random.fold_in(_rk, 511), 0.3 * jnp.ones((16,), jnp.float32), (16, 64))
        _ctx_2048t = jnp.einsum('bsk,bkd->bsd', _ctx_2048c, _ctx_2048P)
        _ctx_2048t = _ctx_2048t * jax.lax.rsqrt(jnp.mean(jnp.square(_ctx_2048t)) + 1e-12) * 0.953939
        ctx_2048 = -1.39393e-06 + 0.999914 * (_ctx_2048t + 0.3 * jax.random.normal(jax.random.fold_in(_rk, 611), (16, 64, 256), jnp.float32))
        _validS = jnp.arange(64)[None, :] < _lenS[:, None]
        _validS2 = jnp.arange(64)[None, :] < _lenS2[:, None]
        _causal = jnp.tril(jnp.ones((64, 64), dtype=bool))
        mask_1x1xSxS2_fc1 = jnp.where(jnp.broadcast_to(_validS2[0:1, None, None, :], (1, 1, 64, 64)), 1.0, 0.0).astype(jnp.float32)
        mask_Bx1xSxS2_ff1 = jnp.where(jnp.ones((16, 1, 64, 64), dtype=bool), 1.0, 0.0).astype(jnp.float32)
        return (x, ctx_2048, mask_1x1xSxS2_fc1, mask_Bx1xSxS2_ff1)
    x, ctx_2048, mask_1x1xSxS2_fc1, mask_Bx1xSxS2_ff1 = _rec_inputs()

    def _L0_xattn_setup():
        import jax, jax.numpy as jnp
        import numpy as np
        H = 256
        NH = 16
        HD = H // NH
        EPS = 1e-05

        def gelu(x):
            return 0.5 * x * (1.0 + jnp.tanh(0.7978845608028654 * x * (1.0 + 0.044715 * x * x)))

        def layernorm(x, scale, bias):
            m = jnp.mean(x, axis=-1, keepdims=True)
            v = jnp.mean(jnp.square(x - m), axis=-1, keepdims=True)
            return (x - m) * jax.lax.rsqrt(v + EPS) * scale + bias

        def split_heads(x):
            b, s, _ = x.shape
            return x.reshape(b, s, NH, HD).transpose(0, 2, 1, 3)

        def merge_heads(x):
            b, nh, s, hd = x.shape
            return x.transpose(0, 2, 1, 3).reshape(b, s, nh * hd)

        def attention(q, k, v, mask):
            scores = jnp.einsum('bhqd,bhkd->bhqk', q, k) / jnp.sqrt(jnp.float32(HD))
            scores = scores * mask - 10000.0 * (1.0 - mask)
            probs = jax.nn.softmax(scores, axis=-1)
            return jnp.einsum('bhqk,bhkd->bhqd', probs, v)
        key = jax.random.key(seed)
        ks = jax.random.split(key, 16)
        b, s, t = (2, 128, 128)
        w = lambda k, i, o: jax.random.normal(k, (i, o), jnp.float32) * 0.02
        inp = {'hidden_states': jax.random.normal(ks[0], (b, s, H), jnp.float32), 'encoder_states': jax.random.normal(ks[1], (b, t, H), jnp.float32), 'ltor_mask': jnp.tril(jnp.ones((1, 1, s, s), jnp.float32)), 'cross_mask': jnp.ones((b, 1, s, t), jnp.float32), 'ln1_s': jnp.ones((H,), jnp.float32), 'ln1_b': jnp.zeros((H,), jnp.float32), 'w_qkv': w(ks[2], H, 3 * H), 'b_qkv': jnp.zeros((3 * H,), jnp.float32), 'w_ao': w(ks[3], H, H), 'b_ao': jnp.zeros((H,), jnp.float32), 'ln2_s': jnp.ones((H,), jnp.float32), 'ln2_b': jnp.zeros((H,), jnp.float32), 'w_q': w(ks[4], H, H), 'b_q': jnp.zeros((H,), jnp.float32), 'w_kv': w(ks[5], H, 2 * H), 'b_kv': jnp.zeros((2 * H,), jnp.float32), 'w_co': w(ks[6], H, H), 'b_co': jnp.zeros((H,), jnp.float32), 'ln3_s': jnp.ones((H,), jnp.float32), 'ln3_b': jnp.zeros((H,), jnp.float32), 'w1': w(ks[7], H, 4 * H), 'b1': jnp.zeros((4 * H,), jnp.float32), 'w2': w(ks[8], 4 * H, H), 'b2': jnp.zeros((H,), jnp.float32)}
        return inp
    _L0_xattn_all = _L0_xattn_setup()
    _L0_xattn_in = {k: v for k, v in _L0_xattn_all.items() if k in ('ln1_s', 'ln1_b', 'w_qkv', 'b_qkv', 'w_ao', 'b_ao', 'ln2_s', 'ln2_b', 'w_q', 'b_q', 'w_kv', 'b_kv', 'w_co', 'b_co', 'ln3_s', 'ln3_b', 'w1', 'b1', 'w2', 'b2')}
    del _L0_xattn_all

    def _L1_xattn_setup():
        import jax, jax.numpy as jnp
        import numpy as np
        E, H, L, B = (256, 32, 128, 4)
        S = E // H
        DM, DD = (32, 64)

        def _ln(x, w, b, eps=1e-05):
            m = x.mean(-1, keepdims=True)
            v = ((x - m) ** 2).mean(-1, keepdims=True)
            return (x - m) / jnp.sqrt(v + eps) * w + b

        def _block(x, state, ln1_w, ln1_b, ln2_w, ln2_b, maa_x, maa_w1, maa_w2, maa_stack, time_decay, td_w1, td_w2, u, Wr, Wk, Wv, Wg, Wo, gn_w, gn_b, ffn_maa_k, ffn_maa_r, Wfk, Wfr, Wfv):
            b, l, e = x.shape
            h = u.shape[0]
            s_ = e // h
            xa = _ln(x, ln1_w, ln1_b)
            sx = jnp.concatenate([state[:, 1:2] - xa[:, :1], xa[:, :-1] - xa[:, 1:]], axis=1)
            xxx = jnp.tanh((xa + sx * maa_x) @ maa_w1).reshape(b, l, 5, DM)
            xxx = jnp.einsum('blfd,fde->blfe', xxx, maa_w2)
            xm = xa[:, :, None] + sx[:, :, None] * (maa_stack + xxx)
            xk, xw, xv, xr, xg = (xm[:, :, j] for j in range(5))
            w = jnp.exp(-jnp.exp(time_decay + jnp.tanh(xw @ td_w1) @ td_w2)).reshape(b, l, h, s_)
            r = (xr @ Wr.T).reshape(b, l, h, s_)
            k = (xk @ Wk.T).reshape(b, l, h, s_)
            v = (xv @ Wv.T).reshape(b, l, h, s_)
            g = jax.nn.silu(xg @ Wg.T)
            s0 = state[:, 2:2 + s_].reshape(b, h, s_, s_)

            def step(s, rkvw):
                r_t, k_t, v_t, w_t = rkvw
                a = k_t[..., :, None] * v_t[..., None, :]
                out = jnp.einsum('bhi,bhij->bhj', r_t, u * a + s)
                s = a + w_t[..., :, None] * s
                return (s, out)
            rkvw = tuple((jnp.moveaxis(t, 1, 0) for t in (r, k, v, w)))
            _, out = jax.lax.scan(step, s0, rkvw)
            out = jnp.moveaxis(out, 0, 1).reshape(b, l, e)
            og = out.reshape(b, l, h, s_)
            m = og.mean(-1, keepdims=True)
            va = ((og - m) ** 2).mean(-1, keepdims=True)
            og = ((og - m) / jnp.sqrt(va + 1e-05)).reshape(b, l, e) * gn_w + gn_b
            x1 = x + og * g @ Wo.T
            xc = _ln(x1, ln2_w, ln2_b)
            sx2 = jnp.concatenate([state[:, 0:1] - xc[:, :1], xc[:, :-1] - xc[:, 1:]], axis=1)
            xk2 = xc + sx2 * ffn_maa_k
            xr2 = xc + sx2 * ffn_maa_r
            rr = jax.nn.sigmoid(xr2 @ Wfr.T)
            kk = jnp.square(jax.nn.relu(xk2 @ Wfk.T))
            return x1 + rr * (kk @ Wfv.T)
        key = jax.random.key(seed)
        ks = jax.random.split(key, 24)
        sc = 0.02
        d = {'x': jax.random.normal(ks[0], (B, L, E), jnp.float32), 'state': jax.random.normal(ks[1], (B, 2 + S, E), jnp.float32) * 0.1, 'ln1_w': jnp.ones((E,), jnp.float32), 'ln1_b': jnp.zeros((E,), jnp.float32), 'ln2_w': jnp.ones((E,), jnp.float32), 'ln2_b': jnp.zeros((E,), jnp.float32), 'maa_x': jax.random.normal(ks[2], (E,), jnp.float32) * 0.1, 'maa_w1': jax.random.normal(ks[3], (E, 5 * DM), jnp.float32) * sc, 'maa_w2': jax.random.normal(ks[4], (5, DM, E), jnp.float32) * sc, 'maa_stack': jax.random.normal(ks[5], (1, 5, E), jnp.float32) * 0.1, 'time_decay': jax.random.normal(ks[6], (E,), jnp.float32) * 0.5, 'td_w1': jax.random.normal(ks[7], (E, DD), jnp.float32) * sc, 'td_w2': jax.random.normal(ks[8], (DD, E), jnp.float32) * sc, 'u': jax.random.normal(ks[9], (H, S, 1), jnp.float32) * 0.1, 'Wr': jax.random.normal(ks[10], (E, E), jnp.float32) * sc, 'Wk': jax.random.normal(ks[11], (E, E), jnp.float32) * sc, 'Wv': jax.random.normal(ks[12], (E, E), jnp.float32) * sc, 'Wg': jax.random.normal(ks[13], (E, E), jnp.float32) * sc, 'Wo': jax.random.normal(ks[14], (E, E), jnp.float32) * sc, 'gn_w': jnp.ones((E,), jnp.float32), 'gn_b': jnp.zeros((E,), jnp.float32), 'ffn_maa_k': jax.random.normal(ks[15], (E,), jnp.float32) * 0.1, 'ffn_maa_r': jax.random.normal(ks[16], (E,), jnp.float32) * 0.1, 'Wfk': jax.random.normal(ks[17], (E, E), jnp.float32) * sc, 'Wfr': jax.random.normal(ks[18], (E, E), jnp.float32) * sc, 'Wfv': jax.random.normal(ks[19], (E, E), jnp.float32) * sc}
        return d
    _L1_xattn_all = _L1_xattn_setup()
    _L1_xattn_in = {k: v for k, v in _L1_xattn_all.items() if k in ('ln1_w', 'ln1_b', 'ln2_w', 'ln2_b', 'maa_x', 'maa_w1', 'maa_w2', 'maa_stack', 'time_decay', 'td_w1', 'td_w2', 'u', 'Wr', 'Wk', 'Wv', 'Wg', 'Wo', 'gn_w', 'gn_b', 'ffn_maa_k', 'ffn_maa_r', 'Wfk', 'Wfr', 'Wfv')}
    del _L1_xattn_all
    return {'x': x, 'ctx_2048': ctx_2048, 'mask_1x1xSxS2_fc1': mask_1x1xSxS2_fc1, 'mask_Bx1xSxS2_ff1': mask_Bx1xSxS2_ff1, 'L0_xattn_ln1_s': _L0_xattn_in['ln1_s'], 'L0_xattn_ln1_b': _L0_xattn_in['ln1_b'], 'L0_xattn_w_qkv': _L0_xattn_in['w_qkv'], 'L0_xattn_b_qkv': _L0_xattn_in['b_qkv'], 'L0_xattn_w_ao': _L0_xattn_in['w_ao'], 'L0_xattn_b_ao': _L0_xattn_in['b_ao'], 'L0_xattn_ln2_s': _L0_xattn_in['ln2_s'], 'L0_xattn_ln2_b': _L0_xattn_in['ln2_b'], 'L0_xattn_w_q': _L0_xattn_in['w_q'], 'L0_xattn_b_q': _L0_xattn_in['b_q'], 'L0_xattn_w_kv': _L0_xattn_in['w_kv'], 'L0_xattn_b_kv': _L0_xattn_in['b_kv'], 'L0_xattn_w_co': _L0_xattn_in['w_co'], 'L0_xattn_b_co': _L0_xattn_in['b_co'], 'L0_xattn_ln3_s': _L0_xattn_in['ln3_s'], 'L0_xattn_ln3_b': _L0_xattn_in['ln3_b'], 'L0_xattn_w1': _L0_xattn_in['w1'], 'L0_xattn_b1': _L0_xattn_in['b1'], 'L0_xattn_w2': _L0_xattn_in['w2'], 'L0_xattn_b2': _L0_xattn_in['b2'], 'L1_xattn_ln1_w': _L1_xattn_in['ln1_w'], 'L1_xattn_ln1_b': _L1_xattn_in['ln1_b'], 'L1_xattn_ln2_w': _L1_xattn_in['ln2_w'], 'L1_xattn_ln2_b': _L1_xattn_in['ln2_b'], 'L1_xattn_maa_x': _L1_xattn_in['maa_x'], 'L1_xattn_maa_w1': _L1_xattn_in['maa_w1'], 'L1_xattn_maa_w2': _L1_xattn_in['maa_w2'], 'L1_xattn_maa_stack': _L1_xattn_in['maa_stack'], 'L1_xattn_time_decay': _L1_xattn_in['time_decay'], 'L1_xattn_td_w1': _L1_xattn_in['td_w1'], 'L1_xattn_td_w2': _L1_xattn_in['td_w2'], 'L1_xattn_u': _L1_xattn_in['u'], 'L1_xattn_Wr': _L1_xattn_in['Wr'], 'L1_xattn_Wk': _L1_xattn_in['Wk'], 'L1_xattn_Wv': _L1_xattn_in['Wv'], 'L1_xattn_Wg': _L1_xattn_in['Wg'], 'L1_xattn_Wo': _L1_xattn_in['Wo'], 'L1_xattn_gn_w': _L1_xattn_in['gn_w'], 'L1_xattn_gn_b': _L1_xattn_in['gn_b'], 'L1_xattn_ffn_maa_k': _L1_xattn_in['ffn_maa_k'], 'L1_xattn_ffn_maa_r': _L1_xattn_in['ffn_maa_r'], 'L1_xattn_Wfk': _L1_xattn_in['Wfk'], 'L1_xattn_Wfr': _L1_xattn_in['Wfr'], 'L1_xattn_Wfv': _L1_xattn_in['Wfv']}

def reference(x, ctx_2048, mask_1x1xSxS2_fc1, mask_Bx1xSxS2_ff1, L0_xattn_ln1_s, L0_xattn_ln1_b, L0_xattn_w_qkv, L0_xattn_b_qkv, L0_xattn_w_ao, L0_xattn_b_ao, L0_xattn_ln2_s, L0_xattn_ln2_b, L0_xattn_w_q, L0_xattn_b_q, L0_xattn_w_kv, L0_xattn_b_kv, L0_xattn_w_co, L0_xattn_b_co, L0_xattn_ln3_s, L0_xattn_ln3_b, L0_xattn_w1, L0_xattn_b1, L0_xattn_w2, L0_xattn_b2, L1_xattn_ln1_w, L1_xattn_ln1_b, L1_xattn_ln2_w, L1_xattn_ln2_b, L1_xattn_maa_x, L1_xattn_maa_w1, L1_xattn_maa_w2, L1_xattn_maa_stack, L1_xattn_time_decay, L1_xattn_td_w1, L1_xattn_td_w2, L1_xattn_u, L1_xattn_Wr, L1_xattn_Wk, L1_xattn_Wv, L1_xattn_Wg, L1_xattn_Wo, L1_xattn_gn_w, L1_xattn_gn_b, L1_xattn_ffn_maa_k, L1_xattn_ffn_maa_r, L1_xattn_Wfk, L1_xattn_Wfr, L1_xattn_Wfv):
    import jax
    import jax.numpy as jnp

    def _L0_xattn_ref(hidden_states, encoder_states, ltor_mask, cross_mask, ln1_s, ln1_b, w_qkv, b_qkv, w_ao, b_ao, ln2_s, ln2_b, w_q, b_q, w_kv, b_kv, w_co, b_co, ln3_s, ln3_b, w1, b1, w2, b2):
        import jax, jax.numpy as jnp
        import numpy as np
        H = 256
        NH = 16
        HD = H // NH
        EPS = 1e-05

        def gelu(x):
            return 0.5 * x * (1.0 + jnp.tanh(0.7978845608028654 * x * (1.0 + 0.044715 * x * x)))

        def layernorm(x, scale, bias):
            m = jnp.mean(x, axis=-1, keepdims=True)
            v = jnp.mean(jnp.square(x - m), axis=-1, keepdims=True)
            return (x - m) * jax.lax.rsqrt(v + EPS) * scale + bias

        def split_heads(x):
            b, s, _ = x.shape
            return x.reshape(b, s, NH, HD).transpose(0, 2, 1, 3)

        def merge_heads(x):
            b, nh, s, hd = x.shape
            return x.transpose(0, 2, 1, 3).reshape(b, s, nh * hd)

        def attention(q, k, v, mask):
            scores = jnp.einsum('bhqd,bhkd->bhqk', q, k) / jnp.sqrt(jnp.float32(HD))
            scores = scores * mask - 10000.0 * (1.0 - mask)
            probs = jax.nn.softmax(scores, axis=-1)
            return jnp.einsum('bhqk,bhkd->bhqd', probs, v)
        ln_out = layernorm(hidden_states, ln1_s, ln1_b)
        qkv = ln_out @ w_qkv + b_qkv
        q, k, v = jnp.split(qkv, 3, axis=-1)
        ctx = merge_heads(attention(split_heads(q), split_heads(k), split_heads(v), ltor_mask))
        attn_out = ctx @ w_ao + b_ao
        x = hidden_states + attn_out
        ln_out = layernorm(x, ln2_s, ln2_b)
        q = ln_out @ w_q + b_q
        kv = encoder_states @ w_kv + b_kv
        k, v = jnp.split(kv, 2, axis=-1)
        ctx = merge_heads(attention(split_heads(q), split_heads(k), split_heads(v), cross_mask))
        cross_out = ctx @ w_co + b_co
        x = x + cross_out
        ln_out = layernorm(x, ln3_s, ln3_b)
        mlp_out = gelu(ln_out @ w1 + b1) @ w2 + b2
        return x + mlp_out

    def _L1_xattn_ref(x, state, ln1_w, ln1_b, ln2_w, ln2_b, maa_x, maa_w1, maa_w2, maa_stack, time_decay, td_w1, td_w2, u, Wr, Wk, Wv, Wg, Wo, gn_w, gn_b, ffn_maa_k, ffn_maa_r, Wfk, Wfr, Wfv):
        import jax, jax.numpy as jnp
        import numpy as np
        E, H, L, B = (256, 32, 128, 4)
        S = E // H
        DM, DD = (32, 64)

        def _ln(x, w, b, eps=1e-05):
            m = x.mean(-1, keepdims=True)
            v = ((x - m) ** 2).mean(-1, keepdims=True)
            return (x - m) / jnp.sqrt(v + eps) * w + b

        def _block(x, state, ln1_w, ln1_b, ln2_w, ln2_b, maa_x, maa_w1, maa_w2, maa_stack, time_decay, td_w1, td_w2, u, Wr, Wk, Wv, Wg, Wo, gn_w, gn_b, ffn_maa_k, ffn_maa_r, Wfk, Wfr, Wfv):
            b, l, e = x.shape
            h = u.shape[0]
            s_ = e // h
            xa = _ln(x, ln1_w, ln1_b)
            sx = jnp.concatenate([state[:, 1:2] - xa[:, :1], xa[:, :-1] - xa[:, 1:]], axis=1)
            xxx = jnp.tanh((xa + sx * maa_x) @ maa_w1).reshape(b, l, 5, DM)
            xxx = jnp.einsum('blfd,fde->blfe', xxx, maa_w2)
            xm = xa[:, :, None] + sx[:, :, None] * (maa_stack + xxx)
            xk, xw, xv, xr, xg = (xm[:, :, j] for j in range(5))
            w = jnp.exp(-jnp.exp(time_decay + jnp.tanh(xw @ td_w1) @ td_w2)).reshape(b, l, h, s_)
            r = (xr @ Wr.T).reshape(b, l, h, s_)
            k = (xk @ Wk.T).reshape(b, l, h, s_)
            v = (xv @ Wv.T).reshape(b, l, h, s_)
            g = jax.nn.silu(xg @ Wg.T)
            s0 = state[:, 2:2 + s_].reshape(b, h, s_, s_)

            def step(s, rkvw):
                r_t, k_t, v_t, w_t = rkvw
                a = k_t[..., :, None] * v_t[..., None, :]
                out = jnp.einsum('bhi,bhij->bhj', r_t, u * a + s)
                s = a + w_t[..., :, None] * s
                return (s, out)
            rkvw = tuple((jnp.moveaxis(t, 1, 0) for t in (r, k, v, w)))
            _, out = jax.lax.scan(step, s0, rkvw)
            out = jnp.moveaxis(out, 0, 1).reshape(b, l, e)
            og = out.reshape(b, l, h, s_)
            m = og.mean(-1, keepdims=True)
            va = ((og - m) ** 2).mean(-1, keepdims=True)
            og = ((og - m) / jnp.sqrt(va + 1e-05)).reshape(b, l, e) * gn_w + gn_b
            x1 = x + og * g @ Wo.T
            xc = _ln(x1, ln2_w, ln2_b)
            sx2 = jnp.concatenate([state[:, 0:1] - xc[:, :1], xc[:, :-1] - xc[:, 1:]], axis=1)
            xk2 = xc + sx2 * ffn_maa_k
            xr2 = xc + sx2 * ffn_maa_r
            rr = jax.nn.sigmoid(xr2 @ Wfr.T)
            kk = jnp.square(jax.nn.relu(xk2 @ Wfk.T))
            return x1 + rr * (kk @ Wfv.T)
        return _block(x, state, ln1_w, ln1_b, ln2_w, ln2_b, maa_x, maa_w1, maa_w2, maa_stack, time_decay, td_w1, td_w2, u, Wr, Wk, Wv, Wg, Wo, gn_w, gn_b, ffn_maa_k, ffn_maa_r, Wfk, Wfr, Wfv)
    x = _L0_xattn_ref(x, ctx_2048, mask_1x1xSxS2_fc1, mask_Bx1xSxS2_ff1, L0_xattn_ln1_s, L0_xattn_ln1_b, L0_xattn_w_qkv, L0_xattn_b_qkv, L0_xattn_w_ao, L0_xattn_b_ao, L0_xattn_ln2_s, L0_xattn_ln2_b, L0_xattn_w_q, L0_xattn_b_q, L0_xattn_w_kv, L0_xattn_b_kv, L0_xattn_w_co, L0_xattn_b_co, L0_xattn_ln3_s, L0_xattn_ln3_b, L0_xattn_w1, L0_xattn_b1, L0_xattn_w2, L0_xattn_b2)
    x = _L1_xattn_ref(x, ctx_2048, L1_xattn_ln1_w, L1_xattn_ln1_b, L1_xattn_ln2_w, L1_xattn_ln2_b, L1_xattn_maa_x, L1_xattn_maa_w1, L1_xattn_maa_w2, L1_xattn_maa_stack, L1_xattn_time_decay, L1_xattn_td_w1, L1_xattn_td_w2, L1_xattn_u, L1_xattn_Wr, L1_xattn_Wk, L1_xattn_Wv, L1_xattn_Wg, L1_xattn_Wo, L1_xattn_gn_w, L1_xattn_gn_b, L1_xattn_ffn_maa_k, L1_xattn_ffn_maa_r, L1_xattn_Wfk, L1_xattn_Wfr, L1_xattn_Wfv)
    return x

_drawn_inputs = setup_inputs


def setup_inputs(seed=0):
    import zlib

    import numpy as np

    out = dict(_drawn_inputs(seed))
    spreads = {'L0_xattn_ln1_s': (1.0, 0.6),
     'L0_xattn_ln1_b': (0.0, 0.758),
     'L0_xattn_b_qkv': (0.0, 0.269),
     'L0_xattn_b_ao': (0.0, 0.1),
     'L0_xattn_ln2_s': (1.0, 0.6),
     'L0_xattn_ln2_b': (0.0, 2.0),
     'L0_xattn_b_q': (0.0, 2.0),
     'L0_xattn_b_kv': (0.0, 0.28),
     'L0_xattn_b_co': (0.0, 0.1),
     'L0_xattn_ln3_s': (1.0, 0.6),
     'L0_xattn_ln3_b': (0.0, 0.649),
     'L0_xattn_b1': (0.0, 0.1),
     'L0_xattn_b2': (0.0, 0.1),
     'L1_xattn_ln1_w': (1.0, 0.593),
     'L1_xattn_ln1_b': (0.0, 0.573),
     'L1_xattn_ln2_w': (1.0, 0.6),
     'L1_xattn_ln2_b': (0.0, 0.8),
     'L1_xattn_gn_w': (1.0, 0.6),
     'L1_xattn_gn_b': (0.0, 0.8)}
    factors = {'L0_xattn_w_qkv': 3.088,
     'L0_xattn_w_q': 8.0,
     'L1_xattn_maa_x': 8.0,
     'L1_xattn_maa_w1': 7.95,
     'L1_xattn_maa_w2': 7.921,
     'L1_xattn_maa_stack': 2.933,
     'L1_xattn_time_decay': 2.811,
     'L1_xattn_td_w1': 8.0,
     'L1_xattn_td_w2': 8.0,
     'L1_xattn_u': 5.944,
     'L1_xattn_ffn_maa_k': 8.0,
     'L1_xattn_ffn_maa_r': 8.0,
     'L1_xattn_Wfk': 2.879,
     'L1_xattn_Wfr': 8.0,
     'L1_xattn_Wfv': 2.681}
    for name, (base, spread) in spreads.items():
        noise = np.random.default_rng([zlib.crc32(name.encode()), seed]).standard_normal(out[name].shape)
        drawn = base * np.exp(spread * noise) if base else spread * noise
        out[name] = jnp.asarray(drawn.astype(out[name].dtype))
    for name, factor in factors.items():
        out[name] = (out[name] * factor).astype(out[name].dtype)
    return out
```

```python
from contextlib import ExitStack

import concourse.bass as bass
from concourse import mybir

P = 128
E = 256
HALF = E // P
NB, SEQ = 16, 64
GB = 4
GROUPS = NB // GB
T = GB * SEQ
TT = T // P
NH, HD = 16, 16
HP = NH // 2
RG = P // 32
F1 = 4 * E
H2, S2 = 32, 8
HH = P // S2
MIX, DM, DD = 5, 32, 64
EPS = 1e-5

F32 = mybir.dt.float32
I32 = mybir.dt.int32
ALU = mybir.AluOpType
ACT = mybir.ActivationFunctionType
AX_X = mybir.AxisListType.X

WEIGHTS = [("w_qkv", 2, 3 * E), ("w_ao", 2, E), ("w_q", 2, E), ("w_kv", 2, 2 * E), ("w_co", 2, E),
           ("w1", 2, F1), ("w2", 8, E),
           ("maa_w1", 2, MIX * DM), ("maa_w2", 1, E), ("maa_w2_last", 1, E), ("td_w1", 2, DD), ("td_w2", 1, E),
           ("Wk", 2, E), ("Wv", 2, E), ("Wr", 2, E), ("Wg", 2, E), ("Wo", 2, E),
           ("Wfk", 2, E), ("Wfr", 2, E), ("Wfv", 2, E)]
W_AT, W_COLS = {}, 0
for _name, _kt, _n in WEIGHTS:
    W_AT[_name] = (W_COLS, _kt, _n)
    W_COLS += _kt * _n
W_PIECES = ["w_qkv", "w_ao", "w1", "maa_w1", "Wk", "Wo"]

VECTORS = [("ln1_s", 2), ("ln1_b", 2), ("ln2_s", 2), ("ln2_b", 2), ("ln3_s", 2), ("ln3_b", 2),
           ("b_qkv", 6), ("b_q", 2), ("b_kv", 4), ("b1", 8),
           ("r_ln1_w", 2), ("r_ln1_b", 2), ("r_ln2_w", 2), ("r_ln2_b", 2),
           ("maa_x", 2), ("maa_stack", 2 * MIX), ("time_decay", 2), ("u", 2), ("mix_k", 2), ("mix_r", 2)]
V_AT, V_COLS = {}, 0
for _name, _n in VECTORS:
    V_AT[_name] = V_COLS
    V_COLS += _n

ROWS = ["b_ao", "b_co", "b2", "gn_w", "gn_b"]

C_IDENT, C_SEL, C_HEADS, C_ONES, C_PAR = 0, P, P + S2 * P, P + S2 * P + HH, 2 * P + S2 * P + HH
C_COLS = C_PAR + 2

L0_USES = ([("ln1", "l0_h", 1, 3), ("q1", "q_ev", 1, 2), ("k1", "k_ev", 1, 2), ("v1", "v_ev", 1, 2)]
           + [(f"sc1_{r}", "masked", r + 1, 8) for r in range(4)]
           + [("k2", "k_ev", 2, 2), ("v2", "v_ev", 2, 2)]
           + [(f"pt1_{r}", "pt_ev", r + 1, 8) for r in range(4)]
           + [("pv1_0", "o_norm", 1, 4), ("pv1_1", "o_norm", 2, 4), ("ot1", "oT_ev", 1, 2), ("ao", "x_res", 1, 3),
              ("ln2", "l0_h", 2, 3), ("q2", "q_ev", 2, 2)]
           + [(f"sc2_{r}", "masked", r + 5, 8) for r in range(4)]
           + [(f"pt2_{r}", "pt_ev", r + 5, 8) for r in range(4)]
           + [("pv2_0", "o_norm", 3, 4), ("pv2_1", "o_norm", 4, 4), ("ot2", "oT_ev", 2, 2), ("co", "x_res", 2, 3),
              ("ln3", "l0_h", 3, 3)]
           + [(f"h{m}", "gelu", m + 1, 4) for m in range(4)] + [("w2", "x_res", 3, 3), None, None])
L1_USES = ([("ln4", "l1_h", 1, 2), ("xl0", "xl_ev", 1, 2), ("xl1", "xl_ev", 2, 2)]
           + [(f"mix{i}", "mixed", i + 1, MIX) for i in range(MIX)]
           + [("td1", "td_ev", 1, 1), ("td2", "decay", 1, 2), ("k", "rkv_ev", 1, 3), ("v", "rkv_ev", 2, 3), ("r", "rkv_ev", 3, 3),
              ("g", "gate", 1, 1), ("bonus", "bonus_v", 1, 1)]
           + [("vb0", "kv", 1, 8), ("wkv", "centred", 1, 1), ("vb1", "kv", 2, 8)]
           + [use for j in (2, 4, 6) for use in ((f"vb{j}", "kv", j + 1, 8), None, (f"vb{j + 1}", "kv", j + 2, 8))]
           + [("yT", "yT_ev", 1, 1), ("wo", "x1_done", 1, 1), ("ln5", "l1_h", 2, 2),
              ("fk", "fk_ev", 1, 1), ("fr", "fr_ev", 1, 1), ("fv", "fv_ev", 1, 1)])
L0_BANKS, L1_BANKS = 5, 3
assert len(L0_USES) % L0_BANKS == 0 and len(L1_USES) % L1_BANKS == 0, (len(L0_USES), len(L1_USES))


def ring(uses, banks, first_bank):
    out = {}
    for i, use in enumerate(uses):
        if use is None:
            continue
        j = i - banks
        while uses[j] is None:
            j -= banks
        out[use[0]] = (first_bank + i % banks, uses[j], j < 0)
    return out


BANK = {**ring(L0_USES, L0_BANKS, 0), **ring(L1_USES, L1_BANKS, L0_BANKS)}

L0 = (["ln1", "qkv1"] + [f"scores1"] + [f"soft1_{r}" for r in range(4)] + ["kv2"] + [f"pt1_{r}" for r in range(4)]
      + ["pv1", "ao", "ln2", "q2", "scores2"] + [f"soft2_{r}" for r in range(4)] + [f"pt2_{r}" for r in range(4)]
      + ["pv2", "co", "ln3", "mlp_up", "mlp_down"])
L1 = (["ln4", "mixin"] + [f"mix{i}" for i in range(MIX)] + ["decay", "rkv", "gate", "bonus"]
      + [f"wkv{j}" for j in range(S2)] + ["norm", "wo", "ln5", "ffn"])
MIX_ORDER = [1, 0, 2, 3, 4]


def merged():
    out, a, b = [], 0, 0
    while a < len(L0) or b < len(L1):
        if b < len(L1) and (a == len(L0) or b * len(L0) <= a * len(L1)):
            out.append((1, L1[b]))
            b += 1
        else:
            out.append((0, L0[a]))
            a += 1
    return out


def build(nc, x, ctxT, s0, state01, self_mask, cross_mask, weights, vectors, rows, consts, out):
    with ExitStack() as ctx:
        def sb(name, *shape):
            return ctx.enter_context(nc.sbuf_tensor(name, list(shape), F32))

        def sem(name):
            return ctx.enter_context(nc.semaphore(name))

        s_x_loaded = sem("x_loaded")
        s_ctx_loaded = sem("ctx_loaded")
        s_c_loaded = sem("c_loaded")
        s_v_loaded = sem("v_loaded")
        s_s_loaded = sem("s_loaded")
        s_out_stored = sem("out_stored")
        s_init_g = sem("init_g")
        s_init_v = sem("init_v")
        s_l0_var = sem("l0_var")
        s_l0_rstd = sem("l0_rstd")
        s_l0_norm = sem("l0_norm")
        s_l0_normT = sem("l0_normT")
        s_l0_h = sem("l0_h")
        s_q_mm = sem("q_mm")
        s_k_mm = sem("k_mm")
        s_v_mm = sem("v_mm")
        s_q_ev = sem("q_ev")
        s_k_ev = sem("k_ev")
        s_v_ev = sem("v_ev")
        s_sc_mm = sem("sc_mm")
        s_masked = sem("masked")
        s_biased = sem("biased")
        s_shifted = sem("shifted")
        s_exped = sem("exped")
        s_pt_mm = sem("pt_mm")
        s_pt_ev = sem("pt_ev")
        s_pv_mm = sem("pv_mm")
        s_o_norm = sem("o_norm")
        s_oT_mm = sem("oT_mm")
        s_oT_ev = sem("oT_ev")
        s_ao_mm = sem("ao_mm")
        s_x_res = sem("x_res")
        s_x_biased = sem("x_biased")
        s_mlp_mm = sem("mlp_mm")
        s_gelu = sem("gelu")
        s_w2_mm = sem("w2_mm")
        s_l1_var = sem("l1_var")
        s_l1_rstd = sem("l1_rstd")
        s_l1_norm = sem("l1_norm")
        s_l1_normT = sem("l1_normT")
        s_l1_h = sem("l1_h")
        s_l1_edge = sem("l1_edge")
        s_l1_in = sem("l1_in")
        s_xl_mm = sem("xl_mm")
        s_xl_ev = sem("xl_ev")
        s_mix_mm = sem("mix_mm")
        s_mixed = sem("mixed")
        s_mix_done = sem("mix_done")
        s_td1_mm = sem("td1_mm")
        s_td_ev = sem("td_ev")
        s_td2_mm = sem("td2_mm")
        s_decay = sem("decay")
        s_rkv_mm = sem("rkv_mm")
        s_rkv_ev = sem("rkv_ev")
        s_g_mm = sem("g_mm")
        s_g_tanh = sem("g_tanh")
        s_gate = sem("gate")
        s_rk = sem("rk")
        s_bonus_mm = sem("bonus_mm")
        s_bonus_v = sem("bonus_v")
        s_vb_mm = sem("vb_mm")
        s_s0_in = sem("s0_in")
        s_kv = sem("kv")
        s_scanned = sem("scanned")
        s_prod = sem("prod")
        s_wkv_mm = sem("wkv_mm")
        s_centred = sem("centred")
        s_squared = sem("squared")
        s_normed = sem("normed")
        s_gn_out = sem("gn_out")
        s_y = sem("y")
        s_yT_mm = sem("yT_mm")
        s_yT_ev = sem("yT_ev")
        s_wo_mm = sem("wo_mm")
        s_x1_done = sem("x1_done")
        s_shift2 = sem("shift2")
        s_fk_mm = sem("fk_mm")
        s_fk_ev = sem("fk_ev")
        s_kk = sem("kk")
        s_fr_mm = sem("fr_mm")
        s_fr_ev = sem("fr_ev")
        s_fv_mm = sem("fv_mm")
        s_fv_ev = sem("fv_ev")
        s_result = sem("result")
        s_chain_v = sem("chain_v")
        s_chain_a = sem("chain_a")
        s_w_loaded = [sem(f"w_loaded{i}") for i in range(len(W_PIECES))]
        banks = [ctx.enter_context(nc.psum_tensor(f"bank{i}", [P, 512], F32)) for i in range(8)]

        W = sb("W", P, W_COLS)
        V = sb("V", P, V_COLS)
        R = sb("R", P, len(ROWS), E)
        C = sb("C", P, C_COLS)
        ident = C[:, C_IDENT:C_IDENT + P]
        heads = C[:, C_HEADS:C_HEADS + HH]
        head_ones = C[:, C_ONES:C_ONES + P]
        mask1 = sb("mask1", P, SEQ)
        mask1b = sb("mask1b", P, SEQ)
        mask2 = sb("mask2", P, GROUPS * TT, SEQ)
        mask2b = sb("mask2b", P, GROUPS * TT, SEQ)
        key_bias = sb("key_bias", P, 2, HALF, 2)
        minus_half = sb("minus_half", P, TT)
        u_heads = sb("u_heads", P, HALF, P)

        x_in = sb("x_in", P, TT, E)
        x_res = sb("x_res", P, TT, E)
        x_mid = sb("x_mid", P, TT, E)
        x_bias = sb("x_bias", P, TT, E)
        ctx_in = sb("ctx_in", P, HALF, T)
        stats = sb("stats", P, 2, TT, 6)
        moments = sb("moments", P, 2, TT, 2)
        var_eps = sb("var_eps", P, 2, TT)
        rstd = sb("rstd", P, 2, TT)
        xn = sb("xn", P, 2, TT, E)
        hT = sb("hT", P, HALF, T)
        qT = sb("qT", P, HALF, T)
        k_bd = sb("k_bd", P, 2, HALF, 2, T)
        v_bd = sb("v_bd", P, 2, GB, HP, 2, HD + 1)
        probs = sb("probs", P, RG, 8, SEQ)
        row_max = sb("row_max", P, RG, 8)
        probsT = sb("probsT", P, RG, 4, P)
        rden = sb("rden", P, TT, NH)
        o_tok = sb("o_tok", P, TT, E)
        oT = sb("oT", P, HALF, T)
        hidden = sb("hidden", P, F1 // P, T)

        xe = sb("xe", P, 2, HALF * GB, SEQ + 1)
        edge = sb("edge", P, 2, HALF, NB)
        sx = sb("sx", P, HALF, T)
        xl = sb("xl", P, HALF, T)
        lora = sb("lora", P, T)
        lora_last = sb("lora_last", DM, T)
        xm = sb("xm", P, MIX, HALF, T)
        td_h = sb("td_h", DD, T)
        dec_e = sb("dec_e", P, HALF * GB, SEQ)
        dec = sb("dec", P, HALF * GB, SEQ)
        kT = sb("kT", P, HALF, T)
        vT = sb("vT", P, HALF, T)
        rT = sb("rT", P, HALF, T)
        rk = sb("rk", P, HALF, T)
        g_t = sb("g_t", P, TT, E)
        gate = sb("gate", P, TT, E)
        s0_sb = sb("s0_sb", P, GROUPS, S2, HALF * GB)
        wkv = sb("wkv", P, S2, HALF * GB, SEQ)
        head_sum = sb("head_sum", P, TT * H2)
        centred = sb("centred", P, TT * H2, S2)
        nw = sb("nw", P, 4, TT * H2)
        y_tok = sb("y_tok", P, TT, E)
        yT = sb("yT", P, HALF, T)
        x1 = sb("x1", P, TT, E)
        xk = sb("xk", P, HALF, T)
        xr = sb("xr", P, HALF, T)
        kk = sb("kk", P, HALF, T)
        fr_t = sb("fr_t", P, TT, E)
        result = sb("result", P, TT, E)

        block = ctx.enter_context(nc.Block())

        def w(name, kt, a, b, rows_=slice(0, P)):
            at, _, n = W_AT[name]
            return W[rows_, at + kt * n + a:at + kt * n + b]

        def vec(name, i):
            return V[:, V_AT[name] + i:V_AT[name] + i + 1]

        def row(name):
            return R[:, ROWS.index(name), :].unsqueeze(1).broadcast_to([P, TT, E])

        def later(n):
            return not (isinstance(n, int) and n == 0)

        def tok(n):
            return bass.ds(n * T, T)

        def tokens(ap):
            return ap.rearrange("p h (b t) -> p (h b) t", t=SEQ)

        def mask_of(a, n, own, cross):
            if a == 0:
                return own[:, :].unsqueeze(1).unsqueeze(1).broadcast_to([P, TT, 4, SEQ])
            return cross[:, bass.ds(n * TT, TT), :].unsqueeze(2).broadcast_to([P, TT, 4, SEQ])

        read = {"bonus_v": s_bonus_v, "centred": s_centred, "decay": s_decay, "fk_ev": s_fk_ev, "fr_ev": s_fr_ev, "fv_ev": s_fv_ev, "gate": s_gate, "gelu": s_gelu, "k_ev": s_k_ev, "kv": s_kv, "l0_h": s_l0_h, "l1_h": s_l1_h, "masked": s_masked, "mixed": s_mixed, "oT_ev": s_oT_ev, "o_norm": s_o_norm, "pt_ev": s_pt_ev, "q_ev": s_q_ev, "rkv_ev": s_rkv_ev, "td_ev": s_td_ev, "v_ev": s_v_ev, "x1_done": s_x1_done, "x_res": s_x_res, "xl_ev": s_xl_ev, "yT_ev": s_yT_ev}

        @block.sync
        def _(sp):
            def load(n):
                if later(n):
                    sp.wait_ge(s_x_biased, 3 * n - 2)
                if later(n):
                    sp.wait_ge(s_l0_norm, 3 * n - 2)
                sp.dma_start(x_in[:, :, :], x[tok(n), :].rearrange("(t p) d -> p t d", p=P)).then_inc(s_x_loaded, 16)
                if later(n):
                    sp.wait_ge(s_v_mm, 2 * n)
                sp.dma_start(ctx_in[:, :, :], ctxT[:, :, tok(n)]).then_inc(s_ctx_loaded, 16)

            def store(n):
                sp.wait_ge(s_result, n + 1)
                sp.dma_start(out[tok(n), :].rearrange("(t p) d -> p t d", p=P), result[:, :, :]).then_inc(s_out_stored, 16)

            load(0)
            sp.dma_start(V[:, :], vectors).then_inc(s_v_loaded, 16)
            sp.dma_start(mask1[0:SEQ, :], self_mask).then_inc(s_v_loaded, 16)
            sp.dma_start(mask1[SEQ:P, :], self_mask).then_inc(s_v_loaded, 16)
            sp.dma_start(mask2[:, :, :], cross_mask.rearrange("(t b) q k -> (b q) t k", b=2)).then_inc(s_v_loaded, 16)
            sp.dma_start(R[:, :, :], rows.partition_broadcast(P)).then_inc(s_v_loaded, 16)
            sp.dma_start(s0_sb[:, :, :, :], s0).then_inc(s_s_loaded, 16)
            sp.dma_start(edge[:, :, :, :], state01).then_inc(s_s_loaded, 16)
            for n in range(GROUPS):
                if n + 1 < GROUPS:
                    load(n + 1)
                if n:
                    store(n - 1)
            store(GROUPS - 1)
            sp.wait_ge(s_out_stored, 16 * GROUPS)

        @block.tensor
        def _(pe):
            def claim(use, n):
                bank, (_, signal, k, per), before = BANK[use]
                if later(n) or not before:
                    pe.wait_ge(read[signal], per * n + (k - per if before else k))
                return banks[bank]

            def mm(o, lhsT, rhs, start=True, stop=True, **kw):
                return nc.tensor.matmul(o, lhsT, rhs, start=start, stop=stop, **kw)

            def to_features(use, n, src):
                ps = claim(use, n)[:, :].rearrange("p (h t) -> p h t", h=HALF)
                for h in range(HALF):
                    for t in range(TT):
                        last = nc.tensor.transpose(ps[:, h, t * P:(t + 1) * P], src[:, t, h * P:(h + 1) * P], ident)
                return last

            def features_out(use, n, weight, a, src, kt=HALF):
                ps = claim(use, n)[:, :].rearrange("p (h t) -> p h t", h=HALF)
                for m in range(HALF):
                    for k in range(kt):
                        last = mm(ps[:, m, :], w(weight, k, a + m * P, a + (m + 1) * P), src[:, k, :], k == 0, k == kt - 1)
                return last

            def tokens_out(use, n, weight, src, kt=HALF):
                ps = claim(use, n)[:, :].rearrange("p (t d) -> p t d", t=TT)
                for t in range(TT):
                    for k in range(kt):
                        last = mm(ps[:, t, :], src[:, k, t * P:(t + 1) * P], w(weight, k, 0, E), k == 0, k == kt - 1)
                return last

            def values(a, n, weight, at, src):
                ps = claim(f"v{a + 1}", n)[:, :].rearrange("p (t d) -> p t d", t=TT)
                for t in range(TT):
                    for k in range(HALF):
                        last = mm(ps[:, t, :], src[:, k, t * P:(t + 1) * P], w(weight, k, at, at + E), k == 0, k == HALF - 1)
                last.then_inc(s_v_mm, 1)

            def norm0(i, n):
                pe.wait_ge(s_l0_norm, 3 * n + i + 1)
                to_features(f"ln{i + 1}", n, xn[:, 0]).then_inc(s_l0_normT, 1)

            def scores(a, n):
                pe.wait_ge(s_q_ev, 2 * n + a + 1)
                pe.wait_ge(s_k_ev, 2 * n + a + 1)
                ps = [claim(f"sc{a + 1}_{r}", n)[:, :].rearrange("p (c k) -> p c k", k=SEQ) for r in range(RG)]
                for t in range(TT):
                    for b in range(2):
                        for h in range(HALF):
                            for r in range(RG):
                                at = slice(t * P + b * SEQ, t * P + (b + 1) * SEQ)
                                last = mm(ps[r][b * SEQ:(b + 1) * SEQ, 4 * t + 2 * h:4 * t + 2 * h + 2, :],
                                          qT[32 * r:32 * r + 32, h, at], k_bd[32 * r:32 * r + 32, a, h, :, at])
                                if t == TT - 1 and b == 1 and h == HALF - 1:
                                    last.then_inc(s_sc_mm, 1)

            def probs_turn(a, r, n):
                pe.wait_ge(s_exped, 8 * n + 4 * a + r + 1)
                ps = claim(f"pt{a + 1}_{r}", n)
                for c in range(4):
                    last = nc.tensor.transpose(ps[:, c * P:(c + 1) * P],
                                               probs[:, r, 2 * c:2 * c + 2, :].rearrange("p c k -> p (c k)"), ident)
                last.then_inc(s_pt_mm, 1)

            def weigh(a, n):
                pe.wait_ge(s_v_ev, 2 * n + a + 1)
                ps = [claim(f"pv{a + 1}_{t}", n) for t in range(TT)]
                for r in range(RG):
                    pe.wait_ge(s_pt_ev, 8 * n + 4 * a + r + 1)
                    for t in range(TT):
                        for b in range(2):
                            for h in range(HALF):
                                hp = h * RG + r
                                last = mm(ps[t][b * SEQ:(b + 1) * SEQ, hp * 34:(hp + 1) * 34],
                                          probsT[:, r, 2 * t + h, b * SEQ:(b + 1) * SEQ],
                                          v_bd[:, a, 2 * t + b, hp, :, :].rearrange("p q d -> p (q d)"))
                last.then_inc(s_pv_mm, 1)

            def attend_out(a, n):
                pe.wait_ge(s_o_norm, 4 * n + 2 * a + 2)
                to_features(f"ot{a + 1}", n, o_tok).then_inc(s_oT_mm, 1)
                pe.wait_ge(s_oT_ev, 2 * n + a + 1)
                use, weight = (("ao", "w_ao"), ("co", "w_co"))[a]
                tokens_out(use, n, weight, oT).then_inc(s_ao_mm, 1)

            def l0(stage, n):
                if stage == "ln1":
                    norm0(0, n)
                elif stage == "qkv1":
                    pe.wait_ge(s_l0_h, 3 * n + 1)
                    features_out("q1", n, "w_qkv", 0, hT).then_inc(s_q_mm, 1)
                    features_out("k1", n, "w_qkv", E, hT).then_inc(s_k_mm, 1)
                    values(0, n, "w_qkv", 2 * E, hT)
                elif stage in ("scores1", "scores2"):
                    scores(int(stage[-1]) - 1, n)
                elif stage == "kv2":
                    pe.wait_ge(s_ctx_loaded, 16 * n + 16)
                    features_out("k2", n, "w_kv", 0, ctx_in).then_inc(s_k_mm, 1)
                    values(1, n, "w_kv", E, ctx_in)
                elif stage[:2] == "pt":
                    probs_turn(int(stage[2]) - 1, int(stage[4]), n)
                elif stage in ("pv1", "pv2"):
                    weigh(int(stage[-1]) - 1, n)
                elif stage in ("ao", "co"):
                    attend_out(int(stage == "co"), n)
                elif stage == "ln2":
                    norm0(1, n)
                elif stage == "q2":
                    pe.wait_ge(s_l0_h, 3 * n + 2)
                    features_out("q2", n, "w_q", 0, hT).then_inc(s_q_mm, 1)
                elif stage == "ln3":
                    norm0(2, n)
                elif stage == "mlp_up":
                    pe.wait_ge(s_l0_h, 3 * n + 3)
                    for m in range(F1 // E):
                        features_out(f"h{m}", n, "w1", m * E, hT).then_inc(s_mlp_mm, 1)
                elif stage == "mlp_down":
                    pe.wait_ge(s_gelu, 4 * n + 4)
                    tokens_out("w2", n, "w2", hidden, F1 // P).then_inc(s_w2_mm, 1)

            def l1(stage, n):
                if stage in ("ln4", "ln5"):
                    i = int(stage == "ln5")
                    pe.wait_ge(s_l1_norm, 2 * n + i + 1)
                    to_features(stage, n, xn[:, 1]).then_inc(s_l1_normT, 1)
                elif stage == "mixin":
                    pe.wait_ge(s_l1_in, n + 1)
                    ps = claim("xl0", n)
                    for k in range(HALF):
                        last = mm(ps[:, 0:T], w("maa_w1", k, 0, P), xl[:, k, :], k == 0, k == HALF - 1)
                    last.then_inc(s_xl_mm, 1)
                    ps = claim("xl1", n)
                    for k in range(HALF):
                        last = mm(ps[0:DM, 0:T], w("maa_w1", k, P, P + DM), xl[:, k, :], k == 0, k == HALF - 1)
                    last.then_inc(s_xl_mm, 1)
                elif stage[:3] == "mix":
                    i = int(stage[3])
                    f = MIX_ORDER[i]
                    pe.wait_ge(s_xl_ev, 2 * n + 2)
                    ps = claim(f"mix{i}", n)
                    at, weight, src = (32 * f, "maa_w2", lora) if f < 4 else (0, "maa_w2_last", lora_last)
                    for m in range(HALF):
                        last = mm(ps[:, m * T:(m + 1) * T], w(weight, 0, m * P, (m + 1) * P, slice(at, at + DM)), src[at:at + DM, :])
                    last.then_inc(s_mix_mm, 1)
                elif stage == "decay":
                    pe.wait_ge(s_mix_done, 5 * n + 1)
                    ps = claim("td1", n)
                    for k in range(HALF):
                        last = mm(ps[0:DD, 0:T], w("td_w1", k, 0, DD), xm[:, 1, k, :], k == 0, k == HALF - 1)
                    last.then_inc(s_td1_mm, 1)
                    pe.wait_ge(s_td_ev, n + 1)
                    ps = claim("td2", n)
                    for m in range(HALF):
                        last = mm(ps[:, m * T:(m + 1) * T], w("td_w2", 0, m * P, (m + 1) * P, slice(0, DD)), td_h[:, :])
                    last.then_inc(s_td2_mm, 1)
                elif stage == "rkv":
                    for i, (use, weight, f) in enumerate((("k", "Wk", 0), ("v", "Wv", 2), ("r", "Wr", 3))):
                        pe.wait_ge(s_mix_done, 5 * n + MIX_ORDER.index(f) + 1)
                        features_out(use, n, weight, 0, xm[:, f]).then_inc(s_rkv_mm, 1)
                elif stage == "gate":
                    pe.wait_ge(s_mix_done, 5 * n + 5)
                    tokens_out("g", n, "Wg", xm[:, 4]).then_inc(s_g_mm, 1)
                elif stage == "bonus":
                    pe.wait_ge(s_rk, n + 1)
                    ps = claim("bonus", n)
                    for m in range(HALF):
                        last = mm(ps[:, m * T:(m + 1) * T], u_heads[:, m, :], rk[:, m, :])
                    last.then_inc(s_bonus_mm, 1)
                elif stage[:3] == "wkv":
                    j = int(stage[3])

                    def spread(i):
                        pe.wait_ge(s_rkv_ev, 3 * n + 2)
                        ps_ = claim(f"vb{i}", n)
                        for m_ in range(HALF):
                            last_ = mm(ps_[:, m_ * T:(m_ + 1) * T], C[:, C_SEL + i * P:C_SEL + (i + 1) * P], vT[:, m_, :])
                        last_.then_inc(s_vb_mm, 1)

                    acc = banks[BANK["wkv"][0]][:, :].rearrange("p (t h d) -> p t h d", t=TT, h=HALF)
                    if j == 0:
                        spread(0)
                        pe.wait_ge(s_bonus_v, n + 1)
                        claim("wkv", n)
                        for t in range(TT):
                            for m in range(HALF):
                                mm(acc[:, t, m, :], rk[:, m, t * P:(t + 1) * P], ident, t == 0 and m == 0, False, skip_group_check=True)
                    if j + 1 < S2:
                        spread(j + 1)
                    pe.wait_ge(s_prod, 8 * n + j + 1)
                    for t in range(TT):
                        for m in range(HALF):
                            last = mm(acc[:, t, m, :].rearrange("p (h j) -> p h j", j=S2)[:, :, j],
                                      wkv[:, j, m * GB + 2 * t:m * GB + 2 * t + 2, :].rearrange("p b t -> p (b t)"), heads,
                                      False, j == S2 - 1, skip_group_check=True)
                    last.then_inc(s_wkv_mm, 1)
                elif stage == "norm":
                    pe.wait_ge(s_y, n + 1)
                    to_features("yT", n, y_tok).then_inc(s_yT_mm, 1)
                elif stage == "wo":
                    pe.wait_ge(s_yT_ev, n + 1)
                    tokens_out("wo", n, "Wo", yT).then_inc(s_wo_mm, 1)
                elif stage == "ffn":
                    pe.wait_ge(s_shift2, n + 1)
                    features_out("fk", n, "Wfk", 0, xk).then_inc(s_fk_mm, 1)
                    tokens_out("fr", n, "Wfr", xr).then_inc(s_fr_mm, 1)
                    pe.wait_ge(s_kk, n + 1)
                    tokens_out("fv", n, "Wfv", kk).then_inc(s_fv_mm, 1)

            pe.wait_ge(s_c_loaded, 16)
            pe.wait_ge(s_w_loaded[0], 16)
            for stage in L0:
                if stage == "kv2":
                    pe.wait_ge(s_w_loaded[1], 16)
                if stage == "mlp_up":
                    pe.wait_ge(s_w_loaded[2], 16)
                l0(stage, 0)
            for piece in (3, 4, 5):
                pe.wait_ge(s_w_loaded[piece], 16)
            pe.wait_ge(s_init_v, 1)
            for n in range(1, GROUPS):
                for which, stage in merged():
                    if which:
                        l1(stage, n - 1)
                    else:
                        l0(stage, n)
            for stage in L1:
                l1(stage, GROUPS - 1)

        @block.scalar
        def _(act):
            A = nc.scalar.activation
            def bank(use):
                return banks[BANK[use][0]]

            def halves(use):
                return bank(use)[:, :].rearrange("p (h t) -> p h t", h=HALF)

            def hT_free(i, n):
                if i == 0:
                    if later(n):
                        act.wait_ge(s_mlp_mm, 4 * n)
                elif i == 1:
                    act.wait_ge(s_v_mm, 2 * n + 1)
                else:
                    act.wait_ge(s_q_mm, 2 * n + 2)

            def queries(a, n):
                act.wait_ge(s_q_mm, 2 * n + a + 1)
                if a:
                    act.wait_ge(s_sc_mm, 8 * n + 4)
                else:
                    if later(n):
                        act.wait_ge(s_sc_mm, 8 * n)
                name = ("b_qkv", "b_q")[a]
                for h in range(HALF):
                    last = A(qT[:, h, :], halves(f"q{a + 1}")[:, h, :], ACT.Identity, bias=vec(name, h))
                last.then_inc(s_q_ev, 1)

            def keys(a, n):
                act.wait_ge(s_k_mm, 2 * n + a + 1)
                if later(n):
                    act.wait_ge(s_sc_mm, 8 * n - 8 + 4 * a + 4)
                for h in range(HALF):
                    for q in range(2):
                        last = A(k_bd[:, a, h, q, :], halves(f"k{a + 1}")[:, h, :], ACT.Identity,
                                 scale=C[:, C_PAR + q:C_PAR + q + 1], bias=key_bias[:, a, h, q:q + 1])
                last.then_inc(s_k_ev, 1)

            def values(a, n):
                if later(n):
                    act.wait_ge(s_pv_mm, 2 * n - 2 + a + 1)
                act.wait_ge(s_v_mm, 2 * n + a + 1)
                src = bank(f"v{a + 1}")[:, :].rearrange("p (t h q d) -> p t h q d", t=TT, h=HP, q=2)
                dst = v_bd[:, a].rearrange("p (t b) h q d -> p t b h q d", b=2)
                for b in range(2):
                    for q in range(2):
                        last = A(dst[q * SEQ:(q + 1) * SEQ, :, b, :, q, 0:HD], src[b * SEQ:(b + 1) * SEQ, :, :, q, :], ACT.Copy)
                last.then_inc(s_v_ev, 1)

            def exps(a, r, n):
                act.wait_ge(s_shifted, 8 * n + 4 * a + r + 1)
                A(probs[:, r], probs[:, r], ACT.Exp).then_inc(s_exped, 1)

            def probs_out(a, r, n):
                act.wait_ge(s_pt_mm, 8 * n + 4 * a + r + 1)
                if a:
                    act.wait_ge(s_pv_mm, 2 * n + 1)
                else:
                    if later(n):
                        act.wait_ge(s_pv_mm, 2 * n)
                A(probsT[:, r].rearrange("p c q -> p (c q)"), bank(f"pt{a + 1}_{r}")[:, :], ACT.Copy).then_inc(s_pt_ev, 1)

            def attended(a, n):
                act.wait_ge(s_oT_mm, 2 * n + a + 1)
                if a:
                    act.wait_ge(s_ao_mm, 2 * n + 1)
                else:
                    if later(n):
                        act.wait_ge(s_ao_mm, 2 * n)
                name, at = (("b_qkv", 4), ("b_kv", 2))[a]
                for h in range(HALF):
                    last = A(oT[:, h, :], halves(f"ot{a + 1}")[:, h, :], ACT.Identity, bias=vec(name, at + h))
                last.then_inc(s_oT_ev, 1)

            def l0(stage, n):
                if stage in ("ln1", "ln2", "ln3"):
                    i = int(stage[-1]) - 1
                    hT_free(i, n)
                    act.wait_ge(s_l0_normT, 3 * n + i + 1)
                    for h in range(HALF):
                        last = A(hT[:, h, :], halves(stage)[:, h, :], ACT.Identity,
                                 scale=vec(f"{stage}_s", h), bias=vec(f"{stage}_b", h))
                    last.then_inc(s_l0_h, 1)
                elif stage == "qkv1":
                    queries(0, n)
                    keys(0, n)
                    values(0, n)
                elif stage == "kv2":
                    keys(1, n)
                    values(1, n)
                elif stage == "q2":
                    queries(1, n)
                elif stage[:4] == "soft":
                    exps(int(stage[4]) - 1, int(stage[6]), n)
                elif stage[:2] == "pt":
                    probs_out(int(stage[2]) - 1, int(stage[4]), n)
                elif stage in ("ao", "co"):
                    attended(int(stage == "co"), n)
                elif stage == "mlp_up":
                    if later(n):
                        act.wait_ge(s_w2_mm, n)
                    for m in range(F1 // E):
                        act.wait_ge(s_mlp_mm, 4 * n + m + 1)
                        for h in range(HALF):
                            last = A(hidden[:, 2 * m + h, :], halves(f"h{m}")[:, h, :], ACT.Gelu_apprx_tanh, bias=vec("b1", 2 * m + h))
                        last.then_inc(s_gelu, 1)

            def l1(stage, n):
                if stage in ("ln4", "ln5"):
                    i = int(stage == "ln5")
                    act.wait_ge(s_l1_normT, 2 * n + i + 1)
                    if i == 0:
                        if later(n):
                            act.wait_ge(s_mixed, 5 * n)
                        if later(n):
                            act.wait_ge(s_mix_done, 5 * n)
                    else:
                        if later(n):
                            act.wait_ge(s_shift2, n)
                    ln = ("r_ln1", "r_ln2")[i]
                    for h in range(HALF):
                        last = A(xe[:, i, h * GB:(h + 1) * GB, 1:], tokens(halves(stage))[:, h * GB:(h + 1) * GB, :], ACT.Identity,
                                 scale=vec(f"{ln}_w", h), bias=vec(f"{ln}_b", h))
                    last.then_inc(s_l1_h, 1)
                elif stage == "mixin":
                    if later(n):
                        act.wait_ge(s_mix_mm, 5 * n)
                    act.wait_ge(s_xl_mm, 2 * n + 1)
                    A(lora[:, :], bank("xl0")[:, 0:T], ACT.Tanh).then_inc(s_xl_ev, 1)
                    act.wait_ge(s_xl_mm, 2 * n + 2)
                    A(lora_last[:, :], bank("xl1")[0:DM, 0:T], ACT.Tanh).then_inc(s_xl_ev, 1)
                elif stage == "decay":
                    act.wait_ge(s_td1_mm, n + 1)
                    if later(n):
                        act.wait_ge(s_td2_mm, n)
                    A(td_h[:, :], bank("td1")[0:DD, 0:T], ACT.Tanh).then_inc(s_td_ev, 1)
                    act.wait_ge(s_td2_mm, n + 1)
                    if later(n):
                        act.wait_ge(s_decay, 2 * n)
                    for h in range(HALF):
                        last = A(dec_e[:, h * GB:(h + 1) * GB, :], tokens(halves("td2"))[:, h * GB:(h + 1) * GB, :], ACT.Exp,
                                 bias=vec("time_decay", h))
                    last.then_inc(s_decay, 1)
                    act.wait_ge(s_decay, 2 * n + 1)
                    if later(n):
                        act.wait_ge(s_scanned, 8 * n)
                    act.wait_ge(s_init_g, 1)
                    A(dec[:, :, 1:], dec_e[:, :, 0:SEQ - 1], ACT.Exp, scale=-1.0).then_inc(s_decay, 1)
                elif stage == "rkv":
                    for i, (use, dst) in enumerate((("k", kT), ("v", vT), ("r", rT))):
                        act.wait_ge(s_rkv_mm, 3 * n + i + 1)
                        if i == 0:
                            if later(n):
                                act.wait_ge(s_kv, 8 * n)
                            if later(n):
                                act.wait_ge(s_rk, n)
                        if i == 1:
                            if later(n):
                                act.wait_ge(s_vb_mm, 8 * n)
                            if later(n):
                                act.wait_ge(s_bonus_v, n)
                        if i == 2:
                            if later(n):
                                act.wait_ge(s_prod, 8 * n)
                        A(dst[:, :, :], halves(use), ACT.Copy).then_inc(s_rkv_ev, 1)
                elif stage == "gate":
                    act.wait_ge(s_g_mm, n + 1)
                    if later(n):
                        act.wait_ge(s_gate, n)
                    A(g_t[:, :, :].rearrange("p t d -> p (t d)"), bank("g")[:, :], ACT.Tanh, scale=0.5).then_inc(s_g_tanh, 1)
                elif stage == "norm":
                    act.wait_ge(s_centred, n + 1)
                    if later(n):
                        act.wait_ge(s_y, n)
                    A(y_tok[:, :, :].rearrange("p t d -> p (t d)"), centred[:, :, :].rearrange("p h d -> p (h d)"), ACT.Square).then_inc(s_squared, 1)
                    act.wait_ge(s_yT_mm, n + 1)
                    if later(n):
                        act.wait_ge(s_wo_mm, n)
                    A(yT[:, :, :], halves("yT"), ACT.Copy).then_inc(s_yT_ev, 1)
                elif stage == "ffn":
                    act.wait_ge(s_fk_mm, n + 1)
                    if later(n):
                        act.wait_ge(s_fv_mm, n)
                    A(kk[:, :, :], halves("fk"), ACT.Relu).then_inc(s_fk_ev, 1)
                    act.wait_ge(s_fk_ev, n + 1)
                    A(kk[:, :, :], kk[:, :, :], ACT.Square).then_inc(s_kk, 1)
                    act.wait_ge(s_fr_mm, n + 1)
                    if later(n):
                        act.wait_ge(s_fv_ev, n)
                    A(fr_t[:, :, :].rearrange("p t d -> p (t d)"), bank("fr")[:, :], ACT.Tanh, scale=0.5).then_inc(s_fr_ev, 1)

            def piece(i):
                a = W_AT[W_PIECES[i]][0]
                b = W_AT[W_PIECES[i + 1]][0] if i + 1 < len(W_PIECES) else W_COLS
                act.dma_start(W[:, a:b], weights[:, a:b]).then_inc(s_w_loaded[i], 16)

            act.dma_start(C[:, :], consts).then_inc(s_c_loaded, 16)
            for i in range(len(W_PIECES)):
                piece(i)
            act.wait_ge(s_v_loaded, 5 * 16)
            act.wait_ge(s_init_g, 1)
            act.wait_ge(s_init_v, 1)
            for stage in L0:
                l0(stage, 0)
            for n in range(1, GROUPS):
                for which, stage in merged():
                    if which:
                        l1(stage, n - 1)
                    else:
                        l0(stage, n)
            for stage in L1:
                l1(stage, GROUPS - 1)

        @block.vector
        def _(dve):
            v = nc.vector
            chain = [0]

            def link(ins):
                chain[0] += 1
                ins.then_inc(s_chain_v, 1)
                dve.wait_ge(s_chain_v, chain[0])

            def bank(use):
                return banks[BANK[use][0]]

            def flat(ap):
                return ap.rearrange("p t d -> p (t d)")

            def layer_norm(src, which, i, per, n, s_var, s_rstd, s_norm, s_normT):
                for t in range(TT):
                    last = v.bn_stats(stats[:, which, t, :], src[:, t, :])
                link(last)
                for t in range(TT):
                    last = v.bn_aggr(moments[:, which, t, :], stats[:, which, t, :])
                link(last)
                if i == 0 and later(n):
                    dve.wait_ge(s_rstd, per * n)
                v.tensor_scalar(var_eps[:, which, :], moments[:, which, :, 1], EPS, None, ALU.add).then_inc(s_var, 1)
                dve.wait_ge(s_rstd, per * n + i + 1)
                if i or later(n):
                    dve.wait_ge(s_normT, per * n + i)
                for t in range(TT):
                    last = v.tensor_scalar(xn[:, which, t, :], src[:, t, :], moments[:, which, t, 0:1], rstd[:, which, t:t + 1],
                                           ALU.subtract, ALU.mult)
                last.then_inc(s_norm, 1)

            def softmax(a, r, n):
                i = 4 * a + r + 1
                dve.wait_ge(s_sc_mm, 8 * n + i)
                if a:
                    dve.wait_ge(s_pt_mm, 8 * n + r + 1)
                else:
                    if later(n):
                        dve.wait_ge(s_pt_mm, 8 * n - 8 + 4 + r + 1)
                ps = bank(f"sc{a + 1}_{r}")[:, :].rearrange("p (t c k) -> p t c k", t=TT, c=4)
                pr = probs[:, r].rearrange("p (t c) k -> p t c k", t=TT)
                v.tensor_tensor(pr, ps, mask_of(a, n, mask1, mask2), ALU.mult).then_inc(s_masked, 1)
                dve.wait_ge(s_biased, 8 * n + i)
                link(v.tensor_reduce(row_max[:, r, :], probs[:, r], AX_X, ALU.max))
                v.tensor_tensor(probs[:, r], probs[:, r], row_max[:, r, :].unsqueeze(2).broadcast_to([P, 8, SEQ]),
                                ALU.subtract).then_inc(s_shifted, 1)

            def divide(a, n):
                dve.wait_ge(s_pv_mm, 2 * n + a + 1)
                if a:
                    dve.wait_ge(s_oT_mm, 2 * n + 1)
                else:
                    if later(n):
                        dve.wait_ge(s_oT_mm, 2 * n)
                ps = [bank(f"pv{a + 1}_{t}")[:, 0:NH * (HD + 1)].rearrange("p (h d) -> p h d", h=NH) for t in range(TT)]
                for t in range(TT):
                    last = v.reciprocal(rden[:, t, :], ps[t][:, :, HD])
                link(last)
                for t in range(TT):
                    v.tensor_tensor(o_tok[:, t, :].rearrange("p (h d) -> p h d", h=NH), ps[t][:, :, 0:HD],
                                    rden[:, t, :].unsqueeze(2).broadcast_to([P, NH, HD]), ALU.mult).then_inc(s_o_norm, 1)

            def residual(i, n):
                if i == 2:
                    dve.wait_ge(s_w2_mm, n + 1)
                    if later(n):
                        dve.wait_ge(s_x1_done, n)
                    if later(n):
                        dve.wait_ge(s_l1_norm, 2 * n - 1)
                else:
                    dve.wait_ge(s_ao_mm, 2 * n + i + 1)
                dve.wait_ge(s_x_biased, 3 * n + i + 1)
                use, dst = (("ao", x_res), ("co", x_res), ("w2", x_mid))[i]
                v.tensor_tensor(flat(dst[:, :, :]), bank(use)[:, :], flat(x_bias[:, :, :]), ALU.add).then_inc(s_x_res, 1)

            def l0(stage, n):
                if stage == "ln1":
                    dve.wait_ge(s_x_loaded, 16 * n + 16)
                    layer_norm(x_in, 0, 0, 3, n, s_l0_var, s_l0_rstd, s_l0_norm, s_l0_normT)
                elif stage in ("ln2", "ln3"):
                    i = int(stage[-1]) - 1
                    dve.wait_ge(s_x_res, 3 * n + i)
                    layer_norm(x_res, 0, i, 3, n, s_l0_var, s_l0_rstd, s_l0_norm, s_l0_normT)
                elif stage[:4] == "soft":
                    softmax(int(stage[4]) - 1, int(stage[6]), n)
                elif stage in ("pv1", "pv2"):
                    divide(int(stage[-1]) - 1, n)
                elif stage in ("ao", "co", "mlp_down"):
                    residual(("ao", "co", "mlp_down").index(stage), n)

            def shift(i):
                link(v.tensor_tensor(tokens(sx[:, :, :]), xe[:, i, :, 0:SEQ], xe[:, i, :, 1:], ALU.subtract))

            def lerp(dst, i, name):
                for h in range(HALF):
                    at = slice(h * GB, (h + 1) * GB)
                    last = v.scalar_tensor_tensor(tokens(dst)[:, at, :], tokens(sx[:, :, :])[:, at, :], vec(name, h),
                                                  xe[:, i, at, 1:], ALU.mult, ALU.add)
                return last

            def rsqrt_heads(n):
                y, q, t, h = (nw[:, i, :] for i in range(4))
                link(v.tensor_scalar(t.bitcast(I32), q.bitcast(I32), 1, None, ALU.logical_shift_right))
                link(v.tensor_scalar(y.bitcast(I32), t.bitcast(I32), -1.0, float(0x5F3759DF), ALU.mult, ALU.add))
                link(v.tensor_scalar(h, q, -0.5, None, ALU.mult))
                for _ in range(3):
                    link(v.tensor_tensor(t, y, y, ALU.mult))
                    link(v.tensor_tensor(t, t, h, ALU.mult))
                    link(v.scalar_tensor_tensor(y, t, 1.5, y, ALU.add, ALU.mult))

            def l1(stage, n):
                if stage == "ln4":
                    dve.wait_ge(s_x_res, 3 * n + 3)
                    layer_norm(x_mid, 1, 0, 2, n, s_l1_var, s_l1_rstd, s_l1_norm, s_l1_normT)
                elif stage == "mixin":
                    dve.wait_ge(s_l1_h, 2 * n + 1)
                    dve.wait_ge(s_l1_edge, 2 * n + 1)
                    if later(n):
                        dve.wait_ge(s_xl_mm, 2 * n)
                    shift(0)
                    lerp(xl[:, :, :], 0, "maa_x").then_inc(s_l1_in, 1)
                elif stage[:3] == "mix":
                    i = int(stage[3])
                    f = MIX_ORDER[i]
                    dve.wait_ge(s_mix_mm, 5 * n + i + 1)
                    if f == 1:
                        if later(n):
                            dve.wait_ge(s_td1_mm, n)
                    elif f == 4:
                        if later(n):
                            dve.wait_ge(s_g_mm, n)
                    else:
                        if later(n):
                            dve.wait_ge(s_rkv_mm, 3 * n)
                    ps = bank(f"mix{i}")[:, :].rearrange("p (h t) -> p h t", h=HALF)
                    for h in range(HALF):
                        last = v.scalar_tensor_tensor(xm[:, f, h, :], ps[:, h, :], vec("maa_stack", 2 * f + h), sx[:, h, :],
                                                      ALU.add, ALU.mult)
                    last.then_inc(s_mixed, 1)
                elif stage == "gate":
                    dve.wait_ge(s_g_tanh, n + 1)
                    if later(n):
                        dve.wait_ge(s_y, n)
                    v.scalar_tensor_tensor(flat(gate[:, :, :]), flat(g_t[:, :, :]), 1.0, bank("g")[:, :], ALU.add, ALU.mult).then_inc(s_gate, 1)
                elif stage == "bonus":
                    dve.wait_ge(s_bonus_mm, n + 1)
                    v.tensor_tensor(rk[:, :, :], bank("bonus")[:, :].rearrange("p (h t) -> p h t", h=HALF), vT[:, :, :],
                                    ALU.mult).then_inc(s_bonus_v, 1)
                elif stage[:3] == "wkv":
                    j = int(stage[3])
                    if j == 0:
                        dve.wait_ge(s_s0_in, n + 1)
                        dve.wait_ge(s_decay, 2 * n + 2)
                        dve.wait_ge(s_rkv_ev, 3 * n + 3)
                    dve.wait_ge(s_vb_mm, 8 * n + j + 1)
                    vb = bank(f"vb{j}")[:, :].rearrange("p (c t) -> p c t", t=SEQ)
                    v.tensor_tensor(wkv[:, j, :, 1:], vb[:, :, 0:SEQ - 1], tokens(kT[:, :, :])[:, :, 0:SEQ - 1], ALU.mult).then_inc(s_kv, 1)
                    dve.wait_ge(s_kv, 8 * n + j + 1)
                    line = wkv[:, j, :, :].rearrange("p c t -> p (c t)")
                    v.tensor_tensor_scan(line, dec[:, :, :].rearrange("p c t -> p (c t)"), line, 0.0, ALU.mult, ALU.add).then_inc(s_scanned, 1)
                    dve.wait_ge(s_scanned, 8 * n + j + 1)
                    v.tensor_tensor(wkv[:, j, :, :], wkv[:, j, :, :], tokens(rT[:, :, :]), ALU.mult).then_inc(s_prod, 1)
                elif stage == "norm":
                    dve.wait_ge(s_wkv_mm, 8 * n + 8)
                    ps = bank("wkv")[:, :].rearrange("p (h d) -> p h d", d=S2)
                    link(v.tensor_reduce(head_sum[:, :], ps, AX_X, ALU.add))
                    v.scalar_tensor_tensor(centred[:, :, :], head_sum[:, :].unsqueeze(2).broadcast_to([P, TT * H2, S2]), -1.0 / S2,
                                           ps, ALU.mult, ALU.add).then_inc(s_centred, 1)
                    dve.wait_ge(s_squared, n + 1)
                    link(v.tensor_reduce(nw[:, 2, :], y_tok[:, :, :].rearrange("p t (h d) -> p (t h) d", d=S2), AX_X, ALU.add))
                    link(v.tensor_scalar(nw[:, 1, :], nw[:, 2, :], 1.0 / S2, EPS, ALU.mult, ALU.add))
                    rsqrt_heads(n)
                    dve.wait_ge(s_centred, n + 1)
                    v.tensor_tensor(centred[:, :, :], centred[:, :, :], nw[:, 0, :].unsqueeze(2).broadcast_to([P, TT * H2, S2]),
                                    ALU.mult).then_inc(s_normed, 1)
                    dve.wait_ge(s_gn_out, 2 * n + 2)
                    v.scalar_tensor_tensor(flat(y_tok[:, :, :]), centred[:, :, :].rearrange("p h d -> p (h d)"), 0.5, flat(gate[:, :, :]),
                                           ALU.mult, ALU.mult).then_inc(s_y, 1)
                elif stage == "wo":
                    dve.wait_ge(s_wo_mm, n + 1)
                    if later(n):
                        dve.wait_ge(s_fv_ev, n)
                    v.tensor_tensor(flat(x1[:, :, :]), bank("wo")[:, :], flat(x_mid[:, :, :]), ALU.add).then_inc(s_x1_done, 1)
                elif stage == "ln5":
                    dve.wait_ge(s_x1_done, n + 1)
                    layer_norm(x1, 1, 1, 2, n, s_l1_var, s_l1_rstd, s_l1_norm, s_l1_normT)
                elif stage == "ffn":
                    dve.wait_ge(s_l1_h, 2 * n + 2)
                    dve.wait_ge(s_l1_edge, 2 * n + 2)
                    shift(1)
                    if later(n):
                        dve.wait_ge(s_fk_mm, n)
                    if later(n):
                        dve.wait_ge(s_fr_mm, n)
                    lerp(xk[:, :, :], 1, "mix_k")
                    lerp(xr[:, :, :], 1, "mix_r").then_inc(s_shift2, 1)
                    dve.wait_ge(s_fv_mm, n + 1)
                    dve.wait_ge(s_fr_ev, n + 1)
                    if later(n):
                        dve.wait_ge(s_out_stored, 16 * n)
                    v.scalar_tensor_tensor(flat(result[:, :, :]), flat(fr_t[:, :, :]), 1.0, bank("fv")[:, :], ALU.add, ALU.mult).then_inc(s_fv_ev, 1)
                    dve.wait_ge(s_fv_ev, n + 1)
                    v.scalar_tensor_tensor(flat(result[:, :, :]), flat(result[:, :, :]), 0.5, flat(x1[:, :, :]), ALU.mult, ALU.add).then_inc(s_result, 1)

            dve.wait_ge(s_v_loaded, 5 * 16)
            dve.wait_ge(s_c_loaded, 16)
            v.tensor_scalar(mask1b[:, :], mask1[:, :], -1.0, 10000.0, ALU.add, ALU.mult)
            v.tensor_scalar(mask2b[:, :, :], mask2[:, :, :], -1.0, 10000.0, ALU.add, ALU.mult)
            for a, (name, at) in enumerate((("b_qkv", 2), ("b_kv", 0))):
                for h in range(HALF):
                    v.tensor_scalar(key_bias[:, a, h, :], C[:, C_PAR:C_PAR + 2], vec(name, at + h), None, ALU.mult)
            for h in range(HALF):
                last = v.tensor_scalar(u_heads[:, h, :], head_ones, vec("u", h), None, ALU.mult)
            last.then_inc(s_init_v, 1)
            for stage in L0:
                l0(stage, 0)
            for n in range(1, GROUPS):
                for which, stage in merged():
                    if which:
                        l1(stage, n - 1)
                    else:
                        l0(stage, n)
            for stage in L1:
                l1(stage, GROUPS - 1)

        @block.gpsimd
        def _(pool):
            g = nc.gpsimd

            def rsqrt(which, i, per, n, s_var, s_rstd, s_norm):
                pool.wait_ge(s_var, per * n + i + 1)
                if i or later(n):
                    pool.wait_ge(s_norm, per * n + i)
                g.tensor_tensor(rstd[:, which, :], var_eps[:, which, :], minus_half[:, :], ALU.pow).then_inc(s_rstd, 1)

            def bias_residual(i, src, n):
                if i:
                    pool.wait_ge(s_x_res, 3 * n + i)
                else:
                    pool.wait_ge(s_x_loaded, 16 * n + 16)
                    if later(n):
                        pool.wait_ge(s_x_res, 3 * n)
                last = g.tensor_tensor(x_bias[:, :, :], src[:, :, :], row(("b_ao", "b_co", "b2")[i]), ALU.add)
                last.then_inc(s_x_biased, 1)

            def l0(stage, n):
                if stage in ("ln1", "ln2", "ln3"):
                    i = int(stage[-1]) - 1
                    rsqrt(0, i, 3, n, s_l0_var, s_l0_rstd, s_l0_norm)
                    bias_residual(i, x_in if i == 0 else x_res, n)
                elif stage[:4] == "soft":
                    a, r = int(stage[4]) - 1, int(stage[6])
                    pool.wait_ge(s_masked, 8 * n + 4 * a + r + 1)
                    pr = probs[:, r].rearrange("p (t c) k -> p t c k", t=TT)
                    g.tensor_tensor(pr, pr, mask_of(a, n, mask1b, mask2b), ALU.add).then_inc(s_biased, 1)

            def edge_in(i, n):
                if i == 0:
                    if later(n):
                        pool.wait_ge(s_l1_in, n)
                else:
                    if later(n):
                        pool.wait_ge(s_shift2, n)
                g.tensor_copy(xe[:, i, :, 0].rearrange("p (h b) -> p h b", h=HALF), edge[:, i, :, bass.ds(n * GB, GB)]).then_inc(s_l1_edge, 1)

            def l1(stage, n):
                if stage in ("ln4", "ln5"):
                    i = int(stage == "ln5")
                    rsqrt(1, i, 2, n, s_l1_var, s_l1_rstd, s_l1_norm)
                    edge_in(i, n)
                elif stage[:3] == "mix" and stage != "mixin":
                    i = int(stage[3])
                    f = MIX_ORDER[i]
                    pool.wait_ge(s_mixed, 5 * n + i + 1)
                    g.tensor_tensor(tokens(xm[:, f]), tokens(xm[:, f]), xe[:, 0, :, 1:], ALU.add).then_inc(s_mix_done, 1)
                elif stage == "rkv":
                    if later(n):
                        pool.wait_ge(s_wkv_mm, 8 * n)
                    pool.wait_ge(s_rkv_ev, 3 * n + 3)
                    g.tensor_tensor(rk[:, :, :], kT[:, :, :], rT[:, :, :], ALU.mult).then_inc(s_rk, 1)
                    g.tensor_copy(wkv[:, :, :, 0], s0_sb[:, n, :, :]).then_inc(s_s0_in, 1)
                elif stage == "norm":
                    pool.wait_ge(s_normed, n + 1)
                    c = centred[:, :, :].rearrange("p (t h) d -> p t (h d)", t=TT)
                    g.tensor_tensor(c, c, row("gn_w"), ALU.mult).then_inc(s_gn_out, 1)
                    pool.wait_ge(s_gn_out, 2 * n + 1)
                    g.tensor_tensor(c, c, row("gn_b"), ALU.add).then_inc(s_gn_out, 1)

            g.memset(v_bd[:, :, :, :, :, :], 0.0)
            g.memset(dec[:, :, 0:1], 0.0)
            g.memset(minus_half[:, :], -0.5)
            g.drain()
            for q in range(2):
                last = g.memset(v_bd[q * SEQ:(q + 1) * SEQ, :, :, :, q, HD:HD + 1], 1.0)
            last.then_inc(s_init_g, 1)
            pool.wait_ge(s_init_g, 1)
            pool.wait_ge(s_v_loaded, 5 * 16)
            pool.wait_ge(s_init_v, 1)
            pool.wait_ge(s_s_loaded, 2 * 16)
            for stage in L0:
                l0(stage, 0)
            for n in range(1, GROUPS):
                for which, stage in merged():
                    if which:
                        l1(stage, n - 1)
                    else:
                        l0(stage, n)
            for stage in L1:
                l1(stage, GROUPS - 1)


def kernel(**inputs):
    import numpy as np
    import concourse.bacc as bacc
    from concourse.bass_utils import run_bass_kernel_spmd as run

    def a(name):
        return np.asarray(inputs[name])

    l0 = {k[len("L0_xattn_"):]: np.asarray(v) for k, v in inputs.items() if k.startswith("L0_xattn_")}
    l1 = {k[len("L1_xattn_"):]: np.asarray(v) for k, v in inputs.items() if k.startswith("L1_xattn_")}

    src = {n: l0[n] for n in ("w_qkv", "w_ao", "w_q", "w_kv", "w_co", "w1", "w2")}
    src |= {n: l1[n] for n in ("maa_w1", "td_w1", "td_w2")}
    src |= {n: l1[n].T for n in ("Wk", "Wv", "Wr", "Wg", "Wo", "Wfk", "Wfr", "Wfv")}
    src["maa_w2"] = l1["maa_w2"][:4].reshape(4 * DM, E)
    src["maa_w2_last"] = l1["maa_w2"][4]
    W = np.zeros((P, W_COLS), np.float32)
    for name, (at, kt, n) in W_AT.items():
        m = src[name]
        for k in range(kt):
            part = m[k * P:(k + 1) * P]
            W[:part.shape[0], at + k * n:at + (k + 1) * n] = part

    vsrc = {n: l0[n] for n in ("ln1_s", "ln1_b", "ln2_s", "ln2_b", "ln3_s", "ln3_b", "b_qkv", "b_q", "b_kv", "b1")}
    vsrc |= {"r_ln1_w": l1["ln1_w"], "r_ln1_b": l1["ln1_b"], "r_ln2_w": l1["ln2_w"], "r_ln2_b": l1["ln2_b"],
             "maa_x": l1["maa_x"], "maa_stack": l1["maa_stack"], "time_decay": l1["time_decay"], "u": l1["u"],
             "mix_k": l1["ffn_maa_k"], "mix_r": l1["ffn_maa_r"]}
    V = np.concatenate([vsrc[name].reshape(n, P).T for name, n in VECTORS], axis=1)
    R = np.stack([l0["b_ao"], l0["b_co"], l0["b2"], l1["gn_w"], l1["gn_b"]])

    C = np.zeros((P, C_COLS), np.float32)
    at = np.arange(P)
    C[at, C_IDENT + at] = 1
    for j in range(S2):
        for i in range(S2):
            C[at[::S2] + j, C_SEL + j * P + at[::S2] + i] = 1
    C[at, C_HEADS + at // S2] = 1
    C[:, C_ONES:C_ONES + P] = at[:, None] // S2 == at[None, :] // S2
    for q in range(2):
        C[:, C_PAR + q] = (at // HD % 2 == q) * HD ** -0.5

    ctx = a("ctx_2048")
    s0 = ctx[:, 2:2 + S2].reshape(GROUPS, GB, HALF, P, S2).transpose(3, 0, 4, 2, 1).reshape(P, GROUPS, S2, HALF * GB)
    state01 = ctx[:, 1::-1].reshape(NB, 2, HALF, P).transpose(3, 1, 2, 0)
    arrays = {
        "x_in_dram": a("x").reshape(NB * SEQ, E),
        "ctxT_dram": ctx.reshape(NB * SEQ, HALF, P).transpose(2, 1, 0),
        "s0_dram": s0,
        "state01_dram": state01,
        "self_mask_dram": a("mask_1x1xSxS2_fc1").reshape(SEQ, SEQ),
        "cross_mask_dram": a("mask_Bx1xSxS2_ff1").reshape(NB, SEQ, SEQ),
        "weights_dram": W, "vectors_dram": V, "rows_dram": R, "consts_dram": C,
    }
    arrays = {k: np.ascontiguousarray(v) for k, v in arrays.items()}
    nc = bacc.Bacc("TRN2", target_bir_lowering=False, num_devices=1)
    args = [nc.dram_tensor(k, v.shape, F32, kind="ExternalInput").ap() for k, v in arrays.items()]
    args.append(nc.dram_tensor("out_dram", (NB * SEQ, E), F32, kind="ExternalOutput").ap())
    build(nc, *args)
    r = run(nc, [arrays], core_ids=[0])
    return r.results[0]["out_dram"].reshape(NB, SEQ, E)
```

```python
from contextlib import ExitStack

import concourse.bass as bass
from concourse import mybir

P = 128
E = 256
HALF = E // P
NB, SEQ = 16, 64
GB = 4
GROUPS = NB // GB
T = GB * SEQ
TT = T // P
NH, HD = 16, 16
HP = NH // 2
RG = P // 32
F1 = 4 * E
H2, S2 = 32, 8
HH = P // S2
MIX, DM, DD = 5, 32, 64
EPS = 1e-5

F32 = mybir.dt.float32
I32 = mybir.dt.int32
ALU = mybir.AluOpType
ACT = mybir.ActivationFunctionType
AX_X = mybir.AxisListType.X

WEIGHTS = [("w_qkv", 2, 3 * E), ("w_ao", 2, E), ("w_q", 2, E), ("w_kv", 2, 2 * E), ("w_co", 2, E),
           ("w1", 2, F1), ("w2", 8, E),
           ("maa_w1", 2, MIX * DM), ("maa_w2", 1, E), ("maa_w2_last", 1, E), ("td_w1", 2, DD), ("td_w2", 1, E),
           ("Wk", 2, E), ("Wv", 2, E), ("Wr", 2, E), ("Wg", 2, E), ("Wo", 2, E),
           ("Wfk", 2, E), ("Wfr", 2, E), ("Wfv", 2, E)]
W_AT, W_COLS = {}, 0
for _name, _kt, _n in WEIGHTS:
    W_AT[_name] = (W_COLS, _kt, _n)
    W_COLS += _kt * _n
W_PIECES = ["w_qkv", "w_ao", "w1", "maa_w1", "Wk", "Wo"]

VECTORS = [("ln1_s", 2), ("ln1_b", 2), ("ln2_s", 2), ("ln2_b", 2), ("ln3_s", 2), ("ln3_b", 2),
           ("b_qkv", 6), ("b_q", 2), ("b_kv", 4), ("b1", 8),
           ("r_ln1_w", 2), ("r_ln1_b", 2), ("r_ln2_w", 2), ("r_ln2_b", 2),
           ("maa_x", 2), ("maa_stack", 2 * MIX), ("time_decay", 2), ("u", 2), ("mix_k", 2), ("mix_r", 2)]
V_AT, V_COLS = {}, 0
for _name, _n in VECTORS:
    V_AT[_name] = V_COLS
    V_COLS += _n

ROWS = ["b_ao", "b_co", "b2", "gn_w", "gn_b"]

C_IDENT, C_PAR, C_HEADS, C_ONES, C_SEL = 0, P, P + 2, P + 2 + HH, 2 * P + 2 + HH
C_COLS = C_SEL + S2 * P

MIX_ORDER = [1, 0, 2, 3, 4]

ORDER = {
    "pe": """
    norm_turn.0.0:0 key.0.0:1 query.0.0:2 value.0.0:3 scores.0.0:4567 key.1.0:0 value.1.0:1 probs_turn.0.0:2
    probs_turn.1.0:3 weigh.0.0:45 probs_turn.2.0:6 weigh.1.0 probs_turn.3.0:0 weigh.2.0 weigh.3.0 attended_turn.0.0:7
    attention_out.0.0:1 norm_turn.1.0:2 query.1.0:3 scores.1.0:6045 probs_turn.4.0:7 weigh.4.0:12 probs_turn.5.0:3
    probs_turn.6.0:6 weigh.5.0 probs_turn.7.0:0 weigh.6.0 weigh.7.0 attended_turn.1.0:4 attention_out.1.0:5 norm_turn.2.0:7
    mlp_up.0.0:3 norm_turn.0.1:6 mlp_up.1.0:0 mlp_up.2.0:1 mlp_up.3.0:2 key.0.1:4 query.0.1:5 value.0.1:7 scores.0.1:3016
    mlp_down.0.0:2 probs_turn.0.1:4 key.1.1:5 probs_turn.1.1:7 weigh.0.1:30 probs_turn.2.1:1 value.1.1:6 weigh.1.1
    probs_turn.3.1:2 weigh.2.1 norm_turn.3.0:4 weigh.3.1 attended_turn.0.1:5 lora_in.0.0:7 attention_out.0.1:1 mix.0.0:6
    mix.1.0:2 mix.2.0:4 mix.3.0:0 norm_turn.1.1:3 decay_in.0.0:5 mix.4.0:7 query.1.1:1 kvr.0.0:6 scores.1.1:2430 kvr.1.0:5
    decay_out.0.0:7 kvr.2.0:1 spread.0.0:6 gate_in.0.0:2 probs_turn.4.1:4 spread.1.0:3 probs_turn.5.1:5 weigh.4.1:70
    spread.2.0:1 probs_turn.6.1:6 weigh.5.1 spread.3.0:4 weigh.6.1 probs_turn.7.1:5 spread.4.0:3 wkv_sum.0.0:6 weigh.7.1
    spread.5.0:1 wkv_sum.1.0 spread.6.0:2 wkv_sum.2.0 spread.7.0:5 wkv_sum.3.0 attended_turn.1.1:4 wkv_sum.4.0 bonus.0.0:3
    attention_out.1.1:0 wkv_sum.5.0 wkv_sum.6.0 wkv_sum.7.0 wkv_bonus.0.0 norm_turn.2.1:7 mlp_up.0.1:1 mlp_up.1.1:4
    mlp_up.2.1:2 norm_turn.0.2:3 mlp_up.3.1:0 y_turn.0.0:5 key.0.2:6 query.0.2:7 value.0.2:1 scores.0.2:4230 mlp_down.0.1:5
    probs_turn.0.2:6 wkv_out.0.0:7 probs_turn.1.2:1 weigh.0.2:42 probs_turn.2.2:3 weigh.1.2 probs_turn.3.2:0 weigh.2.2
    key.1.2:6 weigh.3.2 norm_turn.4.0:7 value.1.2:1 attended_turn.0.2:5 norm_turn.3.1:3 ffn_key.0.0:0 attention_out.0.2:6
    ffn_gate.0.0:2 lora_in.0.1:4 ffn_value.0.0:7 norm_turn.1.2:1 mix.0.1:5 mix.1.1:3 query.1.2:0 mix.2.1:6 decay_in.0.1:2
    scores.1.2:4715 kvr.0.1:3 mix.3.1:0 kvr.1.1:6 decay_out.0.1:2 probs_turn.4.2:4 spread.0.1:7 mix.4.1:1 spread.1.1:3
    probs_turn.5.2:5 weigh.4.2:60 probs_turn.6.2:2 weigh.5.2 probs_turn.7.2:4 weigh.6.2 kvr.2.1:1 weigh.7.2 spread.2.1:5
    gate_in.0.1:2 spread.3.1:4 wkv_sum.0.1:1 attended_turn.1.2:7 spread.4.1:0 bonus.0.1:6 attention_out.1.2:3 spread.5.1:7
    wkv_sum.1.1 spread.6.1:2 wkv_sum.2.1 spread.7.1:5 wkv_sum.3.1 wkv_sum.4.1 norm_turn.2.2:6 mlp_up.0.2:3 wkv_sum.5.1
    mlp_up.1.2:4 norm_turn.0.3:0 mlp_up.2.2:6 wkv_sum.6.1 mlp_up.3.2:7 wkv_sum.7.1 wkv_bonus.0.1 key.0.3:2 query.0.3:3
    value.0.3:4 scores.0.3:5607 mlp_down.0.2:1 probs_turn.0.3:2 y_turn.0.1:3 probs_turn.1.3:4 key.1.3:5 weigh.0.3:60
    probs_turn.2.3:7 weigh.1.3 probs_turn.3.3:2 weigh.2.3 wkv_out.0.1:3 weigh.3.3 value.1.3:4 attended_turn.0.3:5
    norm_turn.4.1:7 attention_out.0.3:2 norm_turn.3.2:3 ffn_key.0.1:0 ffn_gate.0.1:6 lora_in.0.2:1 norm_turn.1.3:4
    ffn_value.0.1:5 query.1.3:7 mix.0.2:3 mix.1.2:2 scores.1.3:0614 mix.2.2:5 kvr.0.2:7 mix.3.2:3 decay_in.0.2:2 mix.4.2:0
    kvr.1.2:6 decay_out.0.2:5 kvr.2.2:7 spread.0.2:3 probs_turn.4.3:2 spread.1.2:1 probs_turn.5.3:4 spread.2.2:6
    weigh.4.3:05 probs_turn.6.3:7 weigh.5.3 probs_turn.7.3:2 spread.3.2:3 weigh.6.3 spread.4.2:4 weigh.7.3 spread.5.2:1
    wkv_sum.0.2:7 spread.6.2:2 wkv_sum.1.2 spread.7.2:6 attended_turn.1.3:3 wkv_sum.2.2 bonus.0.2:4 attention_out.1.3:0
    wkv_sum.3.2 gate_in.0.2:5 wkv_sum.4.2 wkv_sum.5.2 wkv_sum.6.2 wkv_sum.7.2 wkv_bonus.0.2 norm_turn.2.3:1 mlp_up.0.3:3
    mlp_up.1.3:2 mlp_up.2.3:4 mlp_up.3.3:0 y_turn.0.2:6 mlp_down.0.3:5 wkv_out.0.2:7 norm_turn.4.2:1 norm_turn.3.3:3
    ffn_key.0.2:2 lora_in.0.3:4 ffn_gate.0.2:0 mix.0.3:6 ffn_value.0.2:7 mix.1.3:5 decay_in.0.3:1 mix.2.3:3 decay_out.0.3:2
    mix.3.3:4 kvr.0.3:0 mix.4.3:6 kvr.1.3:7 kvr.2.3:5 spread.0.3:1 gate_in.0.3:3 spread.1.3:4 wkv_sum.0.3:2 spread.2.3:0
    bonus.0.3:6 spread.3.3:7 wkv_sum.1.3 spread.4.3:5 spread.5.3:1 wkv_sum.2.3 spread.6.3:3 spread.7.3:4 wkv_sum.3.3
    wkv_sum.4.3 wkv_sum.5.3 wkv_sum.6.3 wkv_sum.7.3 wkv_bonus.0.3 y_turn.0.3:6 wkv_out.0.3:0 norm_turn.4.3:7 ffn_key.0.3:5
    ffn_gate.0.3:1 ffn_value.0.3:3""",
    "act": """
    normed.0.0 key_out.0.0 query_out.0.0 value_out.0.0 key_out.1.0 value_out.1.0 probs_exp.0.0 probs_exp.1.0 probs_out.0.0
    probs_exp.2.0 probs_out.1.0 probs_exp.3.0 probs_out.2.0 probs_out.3.0 attended.0.0 normed.1.0 query_out.1.0
    probs_exp.4.0 probs_out.4.0 probs_exp.5.0 probs_exp.6.0 probs_out.5.0 probs_exp.7.0 probs_out.6.0 probs_out.7.0
    attended.1.0 normed.2.0 gelu.0.0 gelu.1.0 gelu.2.0 normed.0.1 gelu.3.0 key_out.0.1 query_out.0.1 value_out.0.1
    probs_exp.0.1 probs_exp.1.1 probs_exp.2.1 probs_out.0.1 probs_exp.3.1 key_out.1.1 probs_out.1.1 probs_out.2.1
    value_out.1.1 probs_out.3.1 normed.3.0 attended.0.1 lora_out.0.0 normed.1.1 decay_tanh.0.0 query_out.1.1 kvr_out.0.0
    kvr_out.1.0 decay_exp.0.0 probs_exp.4.1 kvr_out.2.0 probs_exp.5.1 gate_tanh.0.0 probs_out.4.1 probs_out.5.1
    probs_exp.6.1 probs_out.6.1 probs_exp.7.1 probs_out.7.1 attended.1.1 normed.2.1 square.0.0 gelu.0.1 gelu.1.1 gelu.2.1
    normed.0.2 gelu.3.1 y_out.0.0 key_out.0.2 query_out.0.2 value_out.0.2 probs_exp.0.2 probs_exp.1.2 probs_exp.2.2
    probs_out.0.2 probs_exp.3.2 probs_out.1.2 probs_out.2.2 probs_out.3.2 key_out.1.2 normed.4.0 value_out.1.2 attended.0.2
    normed.3.1 ffn_square.0.0 ffn_tanh.0.0 lora_out.0.1 normed.1.2 query_out.1.2 decay_tanh.0.1 kvr_out.0.1 probs_exp.4.2
    kvr_out.1.1 decay_exp.0.1 probs_exp.5.2 probs_out.4.2 probs_exp.6.2 probs_out.5.2 probs_exp.7.2 probs_out.6.2
    probs_out.7.2 kvr_out.2.1 gate_tanh.0.1 attended.1.2 normed.2.2 gelu.0.2 gelu.1.2 gelu.2.2 normed.0.3 gelu.3.2
    square.0.1 key_out.0.3 query_out.0.3 value_out.0.3 probs_exp.0.3 probs_exp.1.3 probs_exp.2.3 probs_out.0.3 y_out.0.1
    probs_out.1.3 probs_exp.3.3 key_out.1.3 probs_out.2.3 probs_out.3.3 value_out.1.3 attended.0.3 normed.4.1 normed.3.2
    ffn_square.0.1 ffn_tanh.0.1 lora_out.0.2 normed.1.3 query_out.1.3 kvr_out.0.2 probs_exp.4.3 decay_tanh.0.2 probs_exp.5.3
    kvr_out.1.2 decay_exp.0.2 probs_exp.6.3 kvr_out.2.2 probs_exp.7.3 probs_out.4.3 probs_out.5.3 probs_out.6.3
    probs_out.7.3 attended.1.3 gate_tanh.0.2 normed.2.3 square.0.2 gelu.0.3 gelu.1.3 gelu.2.3 gelu.3.3 y_out.0.2 normed.4.2
    normed.3.3 ffn_square.0.2 lora_out.0.3 ffn_tanh.0.2 decay_tanh.0.3 decay_exp.0.3 kvr_out.0.3 kvr_out.1.3 kvr_out.2.3
    gate_tanh.0.3 square.0.3 y_out.0.3 normed.4.3 ffn_square.0.3 ffn_tanh.0.3""",
    "dve": """
    norm_stats.0.0 init_keys.0.0 norm.0.0 init_masks.0.0 masking.0.0 masking.1.0 masking.2.0 shifting.0.0 masking.3.0
    shifting.1.0 shifting.2.0 init_heads.0.0 shifting.3.0 attended_norm.0.0 residual.0.0 norm_stats.1.0 norm.1.0 masking.4.0
    masking.5.0 masking.6.0 shifting.4.0 masking.7.0 shifting.5.0 shifting.6.0 shifting.7.0 attended_norm.1.0 residual.1.0
    norm_stats.2.0 norm.2.0 norm_stats.0.1 norm.0.1 masking.0.1 masking.1.1 masking.2.1 shifting.0.1 masking.3.1
    shifting.1.1 shifting.2.1 residual.2.0 shifting.3.1 norm_stats.3.0 norm.3.0 attended_norm.0.1 shift.0.0 residual.0.1
    norm_stats.1.1 mixing.0.0 norm.1.1 mixing.1.0 mixing.2.0 mixing.3.0 mixing.4.0 masking.4.1 masking.5.1 masking.6.1
    shifting.4.1 masking.7.1 shifting.5.1 recur.0.0 shifting.6.1 recur.1.0 shifting.7.1 recur.2.0 gating.0.0 recur.3.0
    recur.4.0 attended_norm.1.1 recur.5.0 recur.6.0 bonus_value.0.0 residual.1.1 recur.7.0 norm_stats.2.1 norm.2.1
    centre.0.0 norm_stats.0.2 head_norm.0.0 norm.0.2 gated.0.0 masking.0.2 masking.1.2 masking.2.2 shifting.0.2 masking.3.2
    shifting.1.2 shifting.2.2 shifting.3.2 wkv_residual.0.0 residual.2.1 norm_stats.4.0 norm.4.0 norm_stats.3.1
    attended_norm.0.2 norm.3.1 shift.1.0 shift.0.1 residual.0.2 norm_stats.1.2 norm.1.2 finish.0.0 mixing.0.1 mixing.1.1
    mixing.2.1 masking.4.2 masking.5.2 masking.6.2 shifting.4.2 masking.7.2 shifting.5.2 mixing.3.1 shifting.6.2 mixing.4.1
    shifting.7.2 recur.0.1 attended_norm.1.2 recur.1.1 gating.0.1 recur.2.1 bonus_value.0.1 residual.1.2 recur.3.1
    norm_stats.2.2 recur.4.1 norm.2.2 recur.5.1 norm_stats.0.3 recur.6.1 norm.0.3 recur.7.1 centre.0.1 head_norm.0.1
    gated.0.1 masking.0.3 masking.1.3 masking.2.3 shifting.0.3 masking.3.3 shifting.1.3 shifting.2.3 shifting.3.3
    wkv_residual.0.1 norm_stats.4.1 attended_norm.0.3 residual.2.2 norm.4.1 norm_stats.3.2 norm.3.2 shift.1.1 residual.0.3
    shift.0.2 norm_stats.1.3 norm.1.3 finish.0.1 mixing.0.2 mixing.1.2 masking.4.3 masking.5.3 mixing.2.2 shifting.4.3
    mixing.3.2 masking.6.3 shifting.5.3 masking.7.3 mixing.4.2 shifting.6.3 shifting.7.3 recur.0.2 recur.1.2 recur.2.2
    recur.3.2 recur.4.2 attended_norm.1.3 recur.5.2 recur.6.2 bonus_value.0.2 residual.1.3 recur.7.2 norm_stats.2.3
    gating.0.2 norm.2.3 centre.0.2 head_norm.0.2 gated.0.2 wkv_residual.0.2 norm_stats.4.2 residual.2.3 norm.4.2
    norm_stats.3.3 norm.3.3 shift.1.2 shift.0.3 mixing.0.3 finish.0.2 mixing.1.3 mixing.2.3 mixing.3.3 mixing.4.3 recur.0.3
    gating.0.3 recur.1.3 bonus_value.0.3 recur.2.3 recur.3.3 recur.4.3 recur.5.3 recur.6.3 recur.7.3 centre.0.3
    head_norm.0.3 gated.0.3 wkv_residual.0.3 norm_stats.4.3 norm.4.3 shift.1.3 finish.0.3""",
    "pool": """
    rsqrt.0.0 bias_residual.0.0 mask_bias.0.0 mask_bias.1.0 edge_in.0.0 state_in.0.0 mask_bias.2.0 edge_in.1.0 mask_bias.3.0
    bias_residual.1.0 rsqrt.1.0 mask_bias.4.0 mask_bias.5.0 mask_bias.6.0 mask_bias.7.0 bias_residual.2.0 rsqrt.2.0
    rsqrt.0.1 mask_bias.0.1 mask_bias.1.1 mask_bias.2.1 mask_bias.3.1 bias_residual.0.1 rsqrt.3.0 edge_in.0.1
    bias_residual.1.1 rsqrt.1.1 mix_add.0.0 mix_add.1.0 mix_add.2.0 mix_add.3.0 mix_add.4.0 mask_bias.4.1 mask_bias.5.1
    mask_bias.6.1 mask_bias.7.1 rk_product.0.0 bias_residual.2.1 state_in.0.1 rsqrt.2.1 rsqrt.0.2 group_norm.0.0
    mask_bias.0.2 mask_bias.1.2 mask_bias.2.2 mask_bias.3.2 bias_residual.0.2 rsqrt.4.0 rsqrt.3.1 edge_in.1.1 edge_in.0.2
    bias_residual.1.2 rsqrt.1.2 mix_add.0.1 mix_add.1.1 mix_add.2.1 mask_bias.4.2 mask_bias.5.2 mask_bias.6.2 mask_bias.7.2
    mix_add.3.1 mix_add.4.1 rk_product.0.1 bias_residual.2.2 rsqrt.2.2 rsqrt.0.3 state_in.0.2 group_norm.0.1 mask_bias.0.3
    mask_bias.1.3 mask_bias.2.3 mask_bias.3.3 rsqrt.4.1 bias_residual.0.3 rsqrt.3.2 edge_in.1.2 bias_residual.1.3
    edge_in.0.3 rsqrt.1.3 mix_add.0.2 mix_add.1.2 mask_bias.4.3 mask_bias.5.3 mix_add.2.2 mix_add.3.2 mask_bias.6.3
    mask_bias.7.3 mix_add.4.2 rk_product.0.2 bias_residual.2.3 rsqrt.2.3 state_in.0.3 group_norm.0.2 rsqrt.4.2 rsqrt.3.3
    edge_in.1.3 mix_add.0.3 mix_add.1.3 mix_add.2.3 mix_add.3.3 mix_add.4.3 rk_product.0.3 group_norm.0.3 rsqrt.4.3""",
}


def order(engine):
    for word in ORDER[engine].split():
        step, _, given = word.partition(":")
        name, i, n = step.split(".")
        yield name, int(i), int(n), [int(bank) for bank in given]


def bank_uses():
    named = {"norm_turn": "norm{}", "query": "query{}", "key": "key{}", "value": "value{}", "scores": "scores{}",
             "probs_turn": "probsT{}", "attended_turn": "oT{}", "attention_out": "attention_out{}", "mlp_up": "hidden{}",
             "mlp_down": "mlp_down", "lora_in": "lora", "mix": "mix{}", "decay_in": "decay_in", "decay_out": "decay_out",
             "kvr": "kvr{}", "gate_in": "gate", "bonus": "bonus", "spread": "spread{}", "wkv_sum": "wkv", "y_turn": "yT",
             "wkv_out": "wkv_out", "ffn_key": "ffn_key", "ffn_gate": "ffn_gate", "ffn_value": "ffn_value"}
    out = {}
    for name, i, n, given in order("pe"):
        if name == "weigh" and given:
            out[f"weighed{i // RG}", n] = given
        elif given:
            out[named[name].format(i), n] = given
    return out


BANKS = bank_uses()


def build(nc, x, ctxT, s0, state01, self_mask, cross_mask, weights, vectors, rows, consts, out):
    with ExitStack() as ctx:
        def sb(name, *shape):
            return ctx.enter_context(nc.sbuf_tensor(name, list(shape), F32))

        def sem(name):
            return ctx.enter_context(nc.semaphore(name))

        s_l0_norm = sem("l0_norm")
        s_l0_normT = sem("l0_normT")
        s_l1_norm = sem("l1_norm")
        s_l1_normT = sem("l1_normT")
        s_l0_h = sem("l0_h")
        s_q_mm = sem("q_mm")
        s_ctx_loaded = sem("ctx_loaded")
        s_k_mm = sem("k_mm")
        s_v_mm = sem("v_mm")
        s_q_ev = sem("q_ev")
        s_k_ev = sem("k_ev")
        s_sc_mm = sem("sc_mm")
        s_exped = sem("exped")
        s_pt_mm = sem("pt_mm")
        s_v_ev = sem("v_ev")
        s_pt_ev = sem("pt_ev")
        s_pv_mm = sem("pv_mm")
        s_o_norm = sem("o_norm")
        s_oT_mm = sem("oT_mm")
        s_oT_ev = sem("oT_ev")
        s_ao_mm = sem("ao_mm")
        s_mlp_mm = sem("mlp_mm")
        s_gelu = sem("gelu")
        s_w2_mm = sem("w2_mm")
        s_l1_in = sem("l1_in")
        s_xl_mm = sem("xl_mm")
        s_xl_ev = sem("xl_ev")
        s_mix_mm = sem("mix_mm")
        s_mix_done = sem("mix_done")
        s_td1_mm = sem("td1_mm")
        s_td_ev = sem("td_ev")
        s_td2_mm = sem("td2_mm")
        s_kv = sem("kv")
        s_kvr_mm = sem("kvr_mm")
        s_g_mm = sem("g_mm")
        s_init_heads = sem("init_heads")
        s_rk = sem("rk")
        s_bonus_mm = sem("bonus_mm")
        s_consts_loaded = sem("consts_loaded")
        s_kvr_ev = sem("kvr_ev")
        s_vb_mm = sem("vb_mm")
        s_prod = sem("prod")
        s_wkv_mm = sem("wkv_mm")
        s_bonus_v = sem("bonus_v")
        s_bonus_in = sem("bonus_in")
        s_y = sem("y")
        s_yT_mm = sem("yT_mm")
        s_yT_ev = sem("yT_ev")
        s_wo_mm = sem("wo_mm")
        s_shift2 = sem("shift2")
        s_fk_mm = sem("fk_mm")
        s_fr_mm = sem("fr_mm")
        s_kk = sem("kk")
        s_fv_mm = sem("fv_mm")
        s_ident_loaded = sem("ident_loaded")
        s_l1_h = sem("l1_h")
        s_init_keys = sem("init_keys")
        s_init_g = sem("init_g")
        s_shifted = sem("shifted")
        s_decay = sem("decay")
        s_scanned = sem("scanned")
        s_gate = sem("gate")
        s_g_tanh = sem("g_tanh")
        s_centred = sem("centred")
        s_squared = sem("squared")
        s_fk_ev = sem("fk_ev")
        s_fv_ev = sem("fv_ev")
        s_fr_ev = sem("fr_ev")
        s_v_loaded = sem("v_loaded")
        s_chain_v = sem("chain_v")
        s_x_loaded = sem("x_loaded")
        s_x_res = sem("x_res")
        s_x1_done = sem("x1_done")
        s_l1_rstd = sem("l1_rstd")
        s_l1_var = sem("l1_var")
        s_l0_rstd = sem("l0_rstd")
        s_l0_var = sem("l0_var")
        s_masks_loaded = sem("masks_loaded")
        s_masked = sem("masked")
        s_biased = sem("biased")
        s_x_biased = sem("x_biased")
        s_l1_edge = sem("l1_edge")
        s_mixed = sem("mixed")
        s_s0_in = sem("s0_in")
        s_normed = sem("normed")
        s_gn_out = sem("gn_out")
        s_result = sem("result")
        s_out_stored = sem("out_stored")
        s_init_masks = sem("init_masks")
        s_rows_loaded = sem("rows_loaded")
        s_s_loaded = sem("s_loaded")
        s_w_loaded = [sem(f"w_loaded{i}") for i in range(len(W_PIECES))]
        banks = [ctx.enter_context(nc.psum_tensor(f"bank{i}", [P, 512], F32)) for i in range(8)]

        W = sb("W", P, W_COLS)
        V = sb("V", P, V_COLS)
        R = sb("R", P, len(ROWS), E)
        C = sb("C", P, C_COLS)
        ident = C[:, C_IDENT:C_IDENT + P]
        heads = C[:, C_HEADS:C_HEADS + HH]
        head_ones = C[:, C_ONES:C_ONES + P]
        mask1 = sb("mask1", P, SEQ)
        mask1b = sb("mask1b", P, SEQ)
        mask2 = sb("mask2", P, GROUPS * TT, SEQ)
        mask2b = sb("mask2b", P, GROUPS * TT, SEQ)
        key_bias = sb("key_bias", P, 2, HALF, 2)
        minus_half = sb("minus_half", P, TT)
        u_heads = sb("u_heads", P, HALF, P)

        x_in = sb("x_in", P, TT, E)
        x_res = sb("x_res", P, TT, E)
        x_mid = sb("x_mid", P, TT, E)
        x_bias = sb("x_bias", P, TT, E)
        ctx_in = sb("ctx_in", P, HALF, T)
        stats = sb("stats", P, 2, TT, 6)
        moments = sb("moments", P, 2, TT, 2)
        var_eps = sb("var_eps", P, 2, TT)
        rstd = sb("rstd", P, 2, TT)
        xn = sb("xn", P, 2, TT, E)
        hT = sb("hT", P, HALF, T)
        qT = sb("qT", P, HALF, T)
        k_bd = sb("k_bd", P, 2, HALF, 2, T)
        v_bd = sb("v_bd", P, 2, GB, HP, 2, HD + 1)
        probs = sb("probs", P, RG, 8, SEQ)
        row_max = sb("row_max", P, RG, 8)
        probsT = sb("probsT", P, RG, 4, P)
        rden = sb("rden", P, TT, NH)
        o_tok = sb("o_tok", P, TT, E)
        oT = sb("oT", P, HALF, T)
        hidden = sb("hidden", P, F1 // P, T)

        xe = sb("xe", P, 2, HALF * GB, SEQ + 1)
        edge = sb("edge", P, 2, HALF, NB)
        sx = sb("sx", P, 2, HALF, T)
        xl = sb("xl", P, HALF, T)
        lora = sb("lora", P, T)
        lora_last = sb("lora_last", DM, T)
        xm = sb("xm", P, MIX, HALF, T)
        td_h = sb("td_h", DD, T)
        dec_e = sb("dec_e", P, HALF * GB, SEQ)
        dec = sb("dec", P, HALF * GB, SEQ)
        kT = sb("kT", P, HALF, T)
        vT = sb("vT", P, HALF, T)
        rT = sb("rT", P, HALF, T)
        rk = sb("rk", P, HALF, T)
        g_t = sb("g_t", P, TT, E)
        gate = sb("gate", P, TT, E)
        s0_sb = sb("s0_sb", P, GROUPS, S2, HALF * GB)
        wkv = sb("wkv", P, S2, HALF * GB, SEQ)
        head_sum = sb("head_sum", P, TT * H2)
        centred = sb("centred", P, TT * H2, S2)
        nw = sb("nw", P, 4, TT * H2)
        y_tok = sb("y_tok", P, TT, E)
        yT = sb("yT", P, HALF, T)
        x1 = sb("x1", P, TT, E)
        xk = sb("xk", P, HALF, T)
        xr = sb("xr", P, HALF, T)
        kk = sb("kk", P, HALF, T)
        fr_t = sb("fr_t", P, TT, E)
        result = sb("result", P, TT, E)

        block = ctx.enter_context(nc.Block())

        def w(name, kt, a, b, rows_=slice(0, P)):
            at, _, n = W_AT[name]
            return W[rows_, at + kt * n + a:at + kt * n + b]

        def vec(name, i):
            return V[:, V_AT[name] + i:V_AT[name] + i + 1]

        def row(name):
            return R[:, ROWS.index(name), :].unsqueeze(1).broadcast_to([P, TT, E])

        def tok(n):
            return bass.ds(n * T, T)

        def tokens(ap):
            return ap.rearrange("p h (b t) -> p (h b) t", t=SEQ)

        def mask_of(a, n, own, cross):
            if a == 0:
                return own[:, :].unsqueeze(1).unsqueeze(1).broadcast_to([P, TT, 4, SEQ])
            return cross[:, bass.ds(n * TT, TT), :].unsqueeze(2).broadcast_to([P, TT, 4, SEQ])

        freed_by = {"lora": (s_xl_ev, 1, 1), "decay_in": (s_td_ev, 1, 1), "decay_out": (s_decay, 2, 1), "gate": (s_gate, 1, 1),
                    "bonus": (s_bonus_v, 1, 1), "wkv": (s_centred, 1, 1), "yT": (s_yT_ev, 1, 1), "wkv_out": (s_x1_done, 1, 1),
                    "ffn_key": (s_fk_ev, 1, 1), "ffn_gate": (s_fr_ev, 1, 1), "ffn_value": (s_fv_ev, 1, 1),
                    "mlp_down": (s_x_res, 3, 3)}
        for a in range(2):
            freed_by |= {f"query{a}": (s_q_ev, 2, a + 1), f"key{a}": (s_k_ev, 2, a + 1), f"value{a}": (s_v_ev, 2, a + 1),
                         f"scores{a}": (s_masked, 8, 4 * a + 1), f"weighed{a}": (s_o_norm, 4, 2 * a + 1),
                         f"oT{a}": (s_oT_ev, 2, a + 1), f"attention_out{a}": (s_x_res, 3, a + 1), f"norm{a + 3}": (s_l1_h, 2, a + 1)}
        freed_by |= {f"norm{i}": (s_l0_h, 3, i + 1) for i in range(3)}
        freed_by |= {f"probsT{i}": (s_pt_ev, 8, i + 1) for i in range(8)}
        freed_by |= {f"hidden{m}": (s_gelu, 4, m + 1) for m in range(4)}
        freed_by |= {f"mix{i}": (s_mixed, MIX, i + 1) for i in range(MIX)}
        freed_by |= {f"kvr{i}": (s_kvr_ev, 3, i + 1) for i in range(3)}
        freed_by |= {f"spread{j}": (s_kv, S2, j + 1) for j in range(S2)}

        @block.sync
        def _(sp):
            def load(n):
                if n:
                    sp.wait_ge(s_x_biased, 3 * n - 2)
                    sp.wait_ge(s_l0_norm, 3 * n - 2)
                sp.dma_start(x_in[:, :, :], x[n * T:(n + 1) * T, :].rearrange("(t p) d -> p t d", p=P)).then_inc(s_x_loaded, 16)

            def load_ctx(n):
                if n:
                    sp.wait_ge(s_k_mm, 2 * n)
                    sp.wait_ge(s_v_mm, 2 * n)
                sp.dma_start(ctx_in[:, :, :], ctxT[:, :, n * T:(n + 1) * T]).then_inc(s_ctx_loaded, 16)

            def store(n):
                sp.wait_ge(s_result, n + 1)
                sp.dma_start(out[n * T:(n + 1) * T, :].rearrange("(t p) d -> p t d", p=P), result[:, :, :]).then_inc(s_out_stored, 16)

            def load_weights(i):
                a = W_AT[W_PIECES[i]][0]
                b = W_AT[W_PIECES[i + 1]][0] if i + 1 < len(W_PIECES) else W_COLS
                sp.dma_start(W[:, a:b], weights[:, a:b]).then_inc(s_w_loaded[i], 16)

            load(0)
            sp.dma_start(C[:, 0:C_HEADS], consts[:, 0:C_HEADS]).then_inc(s_ident_loaded, 16)
            sp.dma_start(V[:, :], vectors).then_inc(s_v_loaded, 16)
            load_weights(0)
            sp.dma_start(mask1[0:SEQ, :], self_mask).then_inc(s_masks_loaded, 16)
            sp.dma_start(mask1[SEQ:P, :], self_mask).then_inc(s_masks_loaded, 16)
            sp.dma_start(mask2[:, :, :], cross_mask.rearrange("(t b) q k -> (b q) t k", b=2)).then_inc(s_masks_loaded, 16)
            load_ctx(0)
            sp.wait_ge(s_w_loaded[0], 16)
            sp.dma_start(R[:, :, :], rows.partition_broadcast(P)).then_inc(s_rows_loaded, 16)
            for i in range(1, len(W_PIECES)):
                sp.wait_ge(s_w_loaded[i - 1], 16)
                load_weights(i)
                if i == 2:
                    sp.dma_start(s0_sb[:, :, :, :], s0).then_inc(s_s_loaded, 16)
                    sp.dma_start(edge[:, :, :, :], state01).then_inc(s_s_loaded, 16)
                    sp.dma_start(C[:, C_HEADS:], consts[:, C_HEADS:]).then_inc(s_consts_loaded, 16)
            for n in range(GROUPS):
                if n + 1 < GROUPS:
                    load(n + 1)
                    load_ctx(n + 1)
                if n:
                    store(n - 1)
            store(GROUPS - 1)
            sp.wait_ge(s_out_stored, 16 * GROUPS)

        @block.tensor
        def _(pe):
            holder = {}

            def claim(use, n, i=0):
                bank = BANKS[use, n][i]
                if bank in holder:
                    signal, value = holder[bank]
                    pe.wait_ge(signal, value)
                signal, per, k = freed_by[use]
                holder[bank] = (signal, per * n + k + i)
                return banks[bank][:, :]

            def mm(o, lhsT, rhs, start=True, stop=True, **kw):
                return nc.tensor.matmul(o, lhsT, rhs, start=start, stop=stop, **kw)

            def to_features(ps, src):
                ps = ps.rearrange("p (h t) -> p h t", h=HALF)
                for h in range(HALF):
                    for t in range(TT):
                        last = nc.tensor.transpose(ps[:, h, t * P:(t + 1) * P], src[:, t, h * P:(h + 1) * P], ident)
                return last

            def features_out(ps, weight, a, src, kt=HALF):
                ps = ps.rearrange("p (h t) -> p h t", h=HALF)
                for m in range(HALF):
                    for k in range(kt):
                        last = mm(ps[:, m, :], w(weight, k, a + m * P, a + (m + 1) * P), src[:, k, :], k == 0, k == kt - 1)
                return last

            def tokens_out(ps, weight, src, at=0, kt=HALF):
                ps = ps.rearrange("p (t d) -> p t d", t=TT)
                for t in range(TT):
                    for k in range(kt):
                        last = mm(ps[:, t, :], src[:, k, t * P:(t + 1) * P], w(weight, k, at, at + E), k == 0, k == kt - 1)
                return last

            def norm_turn(i, n):
                if i < 3:
                    pe.wait_ge(s_l0_norm, 3 * n + i + 1)
                    to_features(claim(f"norm{i}", n), xn[:, 0]).then_inc(s_l0_normT, 1)
                else:
                    pe.wait_ge(s_l1_norm, 2 * n + i - 2)
                    to_features(claim(f"norm{i}", n), xn[:, 1]).then_inc(s_l1_normT, 1)

            def query(a, n):
                pe.wait_ge(s_w_loaded[a], 16)
                pe.wait_ge(s_l0_h, 3 * n + a + 1)
                features_out(claim(f"query{a}", n), ("w_qkv", "w_q")[a], 0, hT).then_inc(s_q_mm, 1)

            def key(a, n):
                if a:
                    pe.wait_ge(s_w_loaded[1], 16)
                    pe.wait_ge(s_ctx_loaded, 16 * n + 16)
                    features_out(claim("key1", n), "w_kv", 0, ctx_in).then_inc(s_k_mm, 1)
                else:
                    pe.wait_ge(s_w_loaded[0], 16)
                    pe.wait_ge(s_l0_h, 3 * n + 1)
                    features_out(claim("key0", n), "w_qkv", E, hT).then_inc(s_k_mm, 1)

            def value(a, n):
                if a:
                    pe.wait_ge(s_w_loaded[1], 16)
                    pe.wait_ge(s_ctx_loaded, 16 * n + 16)
                    tokens_out(claim("value1", n), "w_kv", ctx_in, E).then_inc(s_v_mm, 1)
                else:
                    pe.wait_ge(s_w_loaded[0], 16)
                    pe.wait_ge(s_l0_h, 3 * n + 1)
                    tokens_out(claim("value0", n), "w_qkv", hT, 2 * E).then_inc(s_v_mm, 1)

            def scores(a, n):
                pe.wait_ge(s_q_ev, 2 * n + a + 1)
                pe.wait_ge(s_k_ev, 2 * n + a + 1)
                ps = [claim(f"scores{a}", n, r).rearrange("p (c k) -> p c k", k=SEQ) for r in range(RG)]
                for t in range(TT):
                    for b in range(2):
                        for h in range(HALF):
                            for r in range(RG):
                                at = slice(t * P + b * SEQ, t * P + (b + 1) * SEQ)
                                last = mm(ps[r][b * SEQ:(b + 1) * SEQ, 4 * t + 2 * h:4 * t + 2 * h + 2, :],
                                          qT[32 * r:32 * r + 32, h, at], k_bd[32 * r:32 * r + 32, a, h, :, at])
                                if t == TT - 1 and b == 1 and h == HALF - 1:
                                    last.then_inc(s_sc_mm, 1)

            def probs_turn(i, n):
                pe.wait_ge(s_exped, 8 * n + i + 1)
                ps = claim(f"probsT{i}", n)
                for c in range(4):
                    last = nc.tensor.transpose(ps[:, c * P:(c + 1) * P],
                                               probs[:, i % RG, 2 * c:2 * c + 2, :].rearrange("p c k -> p (c k)"), ident)
                last.then_inc(s_pt_mm, 1)

            def weigh(i, n):
                a, r = i // RG, i % RG
                if r == 0:
                    pe.wait_ge(s_v_ev, 2 * n + a + 1)
                    for t in range(TT):
                        weighed[a, t] = claim(f"weighed{a}", n, t)
                pe.wait_ge(s_pt_ev, 8 * n + i + 1)
                for t in range(TT):
                    for b in range(2):
                        for h in range(HALF):
                            hp = h * RG + r
                            last = mm(weighed[a, t][b * SEQ:(b + 1) * SEQ, hp * 34:(hp + 1) * 34],
                                      probsT[:, r, 2 * t + h, b * SEQ:(b + 1) * SEQ],
                                      v_bd[:, a, 2 * t + b, hp, :, :].rearrange("p q d -> p (q d)"))
                last.then_inc(s_pv_mm, 1)

            def attended_turn(a, n):
                pe.wait_ge(s_o_norm, 4 * n + 2 * a + 2)
                to_features(claim(f"oT{a}", n), o_tok).then_inc(s_oT_mm, 1)

            def attention_out(a, n):
                pe.wait_ge(s_w_loaded[1], 16)
                pe.wait_ge(s_oT_ev, 2 * n + a + 1)
                tokens_out(claim(f"attention_out{a}", n), ("w_ao", "w_co")[a], oT).then_inc(s_ao_mm, 1)

            def mlp_up(m, n):
                pe.wait_ge(s_w_loaded[2], 16)
                pe.wait_ge(s_l0_h, 3 * n + 3)
                features_out(claim(f"hidden{m}", n), "w1", m * E, hT).then_inc(s_mlp_mm, 1)

            def mlp_down(_, n):
                pe.wait_ge(s_gelu, 4 * n + 4)
                tokens_out(claim("mlp_down", n), "w2", hidden, 0, F1 // P).then_inc(s_w2_mm, 1)

            def lora_in(_, n):
                pe.wait_ge(s_w_loaded[3], 16)
                pe.wait_ge(s_l1_in, n + 1)
                ps = claim("lora", n)
                for k in range(HALF):
                    mm(ps[:, 0:T], w("maa_w1", k, 0, P), xl[:, k, :], k == 0, k == HALF - 1)
                for k in range(HALF):
                    last = mm(ps[0:DM, T:2 * T], w("maa_w1", k, P, P + DM), xl[:, k, :], k == 0, k == HALF - 1)
                last.then_inc(s_xl_mm, 1)

            def mix(i, n):
                f = MIX_ORDER[i]
                pe.wait_ge(s_xl_ev, n + 1)
                ps = claim(f"mix{i}", n)
                at, weight, src = (32 * f, "maa_w2", lora) if f < 4 else (0, "maa_w2_last", lora_last)
                for m in range(HALF):
                    last = mm(ps[:, m * T:(m + 1) * T], w(weight, 0, m * P, (m + 1) * P, slice(at, at + DM)), src[at:at + DM, :])
                last.then_inc(s_mix_mm, 1)

            def decay_in(_, n):
                pe.wait_ge(s_mix_done, MIX * n + MIX_ORDER.index(1) + 1)
                ps = claim("decay_in", n)
                for k in range(HALF):
                    last = mm(ps[0:DD, 0:T], w("td_w1", k, 0, DD), xm[:, 1, k, :], k == 0, k == HALF - 1)
                last.then_inc(s_td1_mm, 1)

            def decay_out(_, n):
                pe.wait_ge(s_td_ev, n + 1)
                ps = claim("decay_out", n)
                for m in range(HALF):
                    last = mm(ps[:, m * T:(m + 1) * T], w("td_w2", 0, m * P, (m + 1) * P, slice(0, DD)), td_h[:, :])
                last.then_inc(s_td2_mm, 1)

            def kvr(i, n):
                f = (0, 2, 3)[i]
                pe.wait_ge(s_w_loaded[4], 16)
                pe.wait_ge(s_mix_done, MIX * n + MIX_ORDER.index(f) + 1)
                features_out(claim(f"kvr{i}", n), ("Wk", "Wv", "Wr")[i], 0, xm[:, f]).then_inc(s_kvr_mm, 1)

            def gate_in(_, n):
                pe.wait_ge(s_mix_done, MIX * n + MIX_ORDER.index(4) + 1)
                tokens_out(claim("gate", n), "Wg", xm[:, 4]).then_inc(s_g_mm, 1)

            def bonus(_, n):
                pe.wait_ge(s_init_heads, 1)
                pe.wait_ge(s_rk, n + 1)
                ps = claim("bonus", n)
                for m in range(HALF):
                    last = mm(ps[:, m * T:(m + 1) * T], u_heads[:, m, :], rk[:, m, :])
                last.then_inc(s_bonus_mm, 1)

            def spread(j, n):
                pe.wait_ge(s_consts_loaded, 16)
                pe.wait_ge(s_kvr_ev, 3 * n + 2)
                ps = claim(f"spread{j}", n)
                for m in range(HALF):
                    last = mm(ps[:, m * T:(m + 1) * T], C[:, C_SEL + j * P:C_SEL + (j + 1) * P], vT[:, m, :])
                last.then_inc(s_vb_mm, 1)

            def head_out(n):
                return banks[BANKS["wkv", n][0]][:, :].rearrange("p (t h d) -> p t h d", t=TT, h=HALF)

            def wkv_sum(j, n):
                pe.wait_ge(s_prod, S2 * n + j + 1)
                if j == 0:
                    claim("wkv", n)
                for t in range(TT):
                    for m in range(HALF):
                        last = mm(head_out(n)[:, t, m, :].rearrange("p (h j) -> p h j", j=S2)[:, :, j],
                                  wkv[:, j, m * GB + 2 * t:m * GB + 2 * t + 2, :].rearrange("p b t -> p (b t)"), heads,
                                  j == 0 and t == 0 and m == 0, False, skip_group_check=True)
                last.then_inc(s_wkv_mm, 1)

            def wkv_bonus(_, n):
                pe.wait_ge(s_bonus_v, n + 1)
                for t in range(TT):
                    for m in range(HALF):
                        last = mm(head_out(n)[:, t, m, :], rk[:, m, t * P:(t + 1) * P], ident, False, True, skip_group_check=True)
                last.then_inc(s_bonus_in, 1)

            def y_turn(_, n):
                pe.wait_ge(s_y, n + 1)
                to_features(claim("yT", n), y_tok).then_inc(s_yT_mm, 1)

            def wkv_out(_, n):
                pe.wait_ge(s_w_loaded[5], 16)
                pe.wait_ge(s_yT_ev, n + 1)
                tokens_out(claim("wkv_out", n), "Wo", yT).then_inc(s_wo_mm, 1)

            def ffn_key(_, n):
                pe.wait_ge(s_shift2, n + 1)
                features_out(claim("ffn_key", n), "Wfk", 0, xk).then_inc(s_fk_mm, 1)

            def ffn_gate(_, n):
                pe.wait_ge(s_shift2, n + 1)
                tokens_out(claim("ffn_gate", n), "Wfr", xr).then_inc(s_fr_mm, 1)

            def ffn_value(_, n):
                pe.wait_ge(s_kk, n + 1)
                tokens_out(claim("ffn_value", n), "Wfv", kk).then_inc(s_fv_mm, 1)

            weighed = {}
            steps = dict(norm_turn=norm_turn, query=query, key=key, value=value, scores=scores, probs_turn=probs_turn, weigh=weigh,
                         attended_turn=attended_turn, attention_out=attention_out, mlp_up=mlp_up, mlp_down=mlp_down,
                         lora_in=lora_in, mix=mix, decay_in=decay_in, decay_out=decay_out, kvr=kvr, gate_in=gate_in, bonus=bonus,
                         spread=spread, wkv_sum=wkv_sum, wkv_bonus=wkv_bonus, y_turn=y_turn, wkv_out=wkv_out,
                         ffn_key=ffn_key, ffn_gate=ffn_gate, ffn_value=ffn_value)
            pe.wait_ge(s_ident_loaded, 16)
            for name, i, n, _given in order("pe"):
                steps[name](i, n)

        @block.scalar
        def _(act):
            A = nc.scalar.activation

            def bank(use, n, i=0):
                return banks[BANKS[use, n][i]][:, :]

            def halves(ps):
                return ps.rearrange("p (h t) -> p h t", h=HALF)

            def flat(ap):
                return ap.rearrange("p t d -> p (t d)")

            def normed(i, n):
                if i < 3:
                    act.wait_ge(s_l0_normT, 3 * n + i + 1)
                    if i == 0 and n:
                        act.wait_ge(s_mlp_mm, 4 * n)
                    elif i == 1:
                        act.wait_ge(s_v_mm, 2 * n + 1)
                        act.wait_ge(s_q_mm, 2 * n + 1)
                        act.wait_ge(s_k_mm, 2 * n + 1)
                    elif i == 2:
                        act.wait_ge(s_q_mm, 2 * n + 2)
                    for h in range(HALF):
                        last = A(hT[:, h, :], halves(bank(f"norm{i}", n))[:, h, :], ACT.Identity,
                                 scale=vec(f"ln{i + 1}_s", h), bias=vec(f"ln{i + 1}_b", h))
                    last.then_inc(s_l0_h, 1)
                else:
                    act.wait_ge(s_l1_normT, 2 * n + i - 2)
                    if i == 3 and n:
                        act.wait_ge(s_l1_in, n)
                        act.wait_ge(s_mix_done, MIX * n)
                    if i == 4 and n:
                        act.wait_ge(s_shift2, n)
                    ln = ("r_ln1", "r_ln2")[i - 3]
                    for h in range(HALF):
                        last = A(xe[:, i - 3, h * GB:(h + 1) * GB, 1:], tokens(halves(bank(f"norm{i}", n)))[:, h * GB:(h + 1) * GB, :],
                                 ACT.Identity, scale=vec(f"{ln}_w", h), bias=vec(f"{ln}_b", h))
                    last.then_inc(s_l1_h, 1)

            def query_out(a, n):
                act.wait_ge(s_q_mm, 2 * n + a + 1)
                if a or n:
                    act.wait_ge(s_sc_mm, 8 * n + 4 * a)
                for h in range(HALF):
                    last = A(qT[:, h, :], halves(bank(f"query{a}", n))[:, h, :], ACT.Identity, bias=vec(("b_qkv", "b_q")[a], h))
                last.then_inc(s_q_ev, 1)

            def key_out(a, n):
                act.wait_ge(s_init_keys, 1)
                act.wait_ge(s_k_mm, 2 * n + a + 1)
                if n:
                    act.wait_ge(s_sc_mm, 8 * n - 4 + 4 * a)
                for h in range(HALF):
                    for q in range(2):
                        last = A(k_bd[:, a, h, q, :], halves(bank(f"key{a}", n))[:, h, :], ACT.Identity,
                                 scale=C[:, C_PAR + q:C_PAR + q + 1], bias=key_bias[:, a, h, q:q + 1])
                last.then_inc(s_k_ev, 1)

            def value_out(a, n):
                act.wait_ge(s_init_g, 1)
                act.wait_ge(s_v_mm, 2 * n + a + 1)
                if n:
                    act.wait_ge(s_pv_mm, 8 * n - 4 + 4 * a)
                src = bank(f"value{a}", n).rearrange("p (t h q d) -> p t h q d", t=TT, h=HP, q=2)
                dst = v_bd[:, a].rearrange("p (t b) h q d -> p t b h q d", b=2)
                for b in range(2):
                    for q in range(2):
                        last = A(dst[q * SEQ:(q + 1) * SEQ, :, b, :, q, 0:HD], src[b * SEQ:(b + 1) * SEQ, :, :, q, :], ACT.Copy)
                last.then_inc(s_v_ev, 1)

            def probs_exp(i, n):
                act.wait_ge(s_shifted, 8 * n + i + 1)
                A(probs[:, i % RG], probs[:, i % RG], ACT.Exp).then_inc(s_exped, 1)

            def probs_out(i, n):
                act.wait_ge(s_pt_mm, 8 * n + i + 1)
                if i >= RG or n:
                    act.wait_ge(s_pv_mm, 8 * n + i - RG + 1)
                A(probsT[:, i % RG].rearrange("p c q -> p (c q)"), bank(f"probsT{i}", n), ACT.Copy).then_inc(s_pt_ev, 1)

            def attended(a, n):
                act.wait_ge(s_oT_mm, 2 * n + a + 1)
                if a or n:
                    act.wait_ge(s_ao_mm, 2 * n + a)
                name, at = (("b_qkv", 4), ("b_kv", 2))[a]
                for h in range(HALF):
                    last = A(oT[:, h, :], halves(bank(f"oT{a}", n))[:, h, :], ACT.Identity, bias=vec(name, at + h))
                last.then_inc(s_oT_ev, 1)

            def gelu(m, n):
                act.wait_ge(s_mlp_mm, 4 * n + m + 1)
                if n:
                    act.wait_ge(s_w2_mm, n)
                for h in range(HALF):
                    last = A(hidden[:, 2 * m + h, :], halves(bank(f"hidden{m}", n))[:, h, :], ACT.Gelu_apprx_tanh,
                             bias=vec("b1", 2 * m + h))
                last.then_inc(s_gelu, 1)

            def lora_out(_, n):
                act.wait_ge(s_xl_mm, n + 1)
                if n:
                    act.wait_ge(s_mix_mm, MIX * n)
                A(lora[:, :], bank("lora", n)[:, 0:T], ACT.Tanh)
                A(lora_last[:, :], bank("lora", n)[0:DM, T:2 * T], ACT.Tanh).then_inc(s_xl_ev, 1)

            def decay_tanh(_, n):
                act.wait_ge(s_td1_mm, n + 1)
                if n:
                    act.wait_ge(s_td2_mm, n)
                A(td_h[:, :], bank("decay_in", n)[0:DD, 0:T], ACT.Tanh).then_inc(s_td_ev, 1)

            def decay_exp(_, n):
                act.wait_ge(s_td2_mm, n + 1)
                if n:
                    act.wait_ge(s_decay, 2 * n)
                for h in range(HALF):
                    last = A(dec_e[:, h * GB:(h + 1) * GB, :], tokens(halves(bank("decay_out", n)))[:, h * GB:(h + 1) * GB, :],
                             ACT.Exp, bias=vec("time_decay", h))
                last.then_inc(s_decay, 1)
                act.wait_ge(s_init_g, 1)
                act.wait_ge(s_decay, 2 * n + 1)
                if n:
                    act.wait_ge(s_scanned, S2 * n)
                A(dec[:, :, 1:], dec_e[:, :, 0:SEQ - 1], ACT.Exp, scale=-1.0).then_inc(s_decay, 1)

            def kvr_out(i, n):
                act.wait_ge(s_kvr_mm, 3 * n + i + 1)
                if n and i == 0:
                    act.wait_ge(s_kv, S2 * n)
                    act.wait_ge(s_rk, n)
                if n and i == 1:
                    act.wait_ge(s_vb_mm, S2 * n)
                    act.wait_ge(s_bonus_v, n)
                if n and i == 2:
                    act.wait_ge(s_prod, S2 * n)
                    act.wait_ge(s_rk, n)
                A((kT, vT, rT)[i][:, :, :], halves(bank(f"kvr{i}", n)), ACT.Copy).then_inc(s_kvr_ev, 1)

            def gate_tanh(_, n):
                act.wait_ge(s_g_mm, n + 1)
                if n:
                    act.wait_ge(s_gate, n)
                A(flat(g_t[:, :, :]), bank("gate", n), ACT.Tanh, scale=0.5).then_inc(s_g_tanh, 1)

            def square(_, n):
                act.wait_ge(s_centred, n + 1)
                if n:
                    act.wait_ge(s_yT_mm, n)
                A(flat(y_tok[:, :, :]), centred[:, :, :].rearrange("p h d -> p (h d)"), ACT.Square).then_inc(s_squared, 1)

            def y_out(_, n):
                act.wait_ge(s_yT_mm, n + 1)
                if n:
                    act.wait_ge(s_wo_mm, n)
                A(yT[:, :, :], halves(bank("yT", n)), ACT.Copy).then_inc(s_yT_ev, 1)

            def ffn_square(_, n):
                act.wait_ge(s_fk_mm, n + 1)
                if n:
                    act.wait_ge(s_fv_mm, n)
                A(kk[:, :, :], halves(bank("ffn_key", n)), ACT.Relu).then_inc(s_fk_ev, 1)
                act.wait_ge(s_fk_ev, n + 1)
                A(kk[:, :, :], kk[:, :, :], ACT.Square).then_inc(s_kk, 1)

            def ffn_tanh(_, n):
                act.wait_ge(s_fr_mm, n + 1)
                if n:
                    act.wait_ge(s_fv_ev, n)
                A(flat(fr_t[:, :, :]), bank("ffn_gate", n), ACT.Tanh, scale=0.5).then_inc(s_fr_ev, 1)

            steps = dict(normed=normed, query_out=query_out, key_out=key_out, value_out=value_out, probs_exp=probs_exp,
                         probs_out=probs_out, attended=attended, gelu=gelu, lora_out=lora_out, decay_tanh=decay_tanh,
                         decay_exp=decay_exp, kvr_out=kvr_out, gate_tanh=gate_tanh, square=square, y_out=y_out,
                         ffn_square=ffn_square, ffn_tanh=ffn_tanh)
            act.wait_ge(s_v_loaded, 16)
            for name, i, n, _given in order("act"):
                steps[name](i, n)

        @block.vector
        def _(dve):
            v = nc.vector
            chain = [0]

            def link(ins):
                chain[0] += 1
                ins.then_inc(s_chain_v, 1)
                dve.wait_ge(s_chain_v, chain[0])

            def bank(use, n, i=0):
                return banks[BANKS[use, n][i]][:, :]

            def flat(ap):
                return ap.rearrange("p t d -> p (t d)")

            def norm_stats(i, n):
                which = int(i >= 3)
                if i == 0:
                    dve.wait_ge(s_x_loaded, 16 * n + 16)
                elif i < 4:
                    dve.wait_ge(s_x_res, 3 * n + i)
                else:
                    dve.wait_ge(s_x1_done, n + 1)
                src = (x_in, x_res, x_res, x_mid, x1)[i]
                for t in range(TT):
                    last = v.bn_stats(stats[:, which, t, :], src[:, t, :])
                link(last)
                for t in range(TT):
                    last = v.bn_aggr(moments[:, which, t, :], stats[:, which, t, :])
                link(last)
                if i >= 3:
                    if i == 4 or n:
                        dve.wait_ge(s_l1_rstd, 2 * n + i - 3)
                    v.tensor_scalar(var_eps[:, 1, :], moments[:, 1, :, 1], EPS, None, ALU.add).then_inc(s_l1_var, 1)
                else:
                    if i or n:
                        dve.wait_ge(s_l0_rstd, 3 * n + i)
                    v.tensor_scalar(var_eps[:, 0, :], moments[:, 0, :, 1], EPS, None, ALU.add).then_inc(s_l0_var, 1)

            def norm(i, n):
                which = int(i >= 3)
                if i >= 3:
                    dve.wait_ge(s_l1_rstd, 2 * n + i - 2)
                    if i == 4 or n:
                        dve.wait_ge(s_l1_normT, 2 * n + i - 3)
                else:
                    dve.wait_ge(s_l0_rstd, 3 * n + i + 1)
                    if i or n:
                        dve.wait_ge(s_l0_normT, 3 * n + i)
                src = (x_in, x_res, x_res, x_mid, x1)[i]
                for t in range(TT):
                    last = v.tensor_scalar(xn[:, which, t, :], src[:, t, :], moments[:, which, t, 0:1], rstd[:, which, t:t + 1],
                                           ALU.subtract, ALU.mult)
                last.then_inc(s_l1_norm if which else s_l0_norm, 1)

            def masking(i, n):
                a, r = i // RG, i % RG
                dve.wait_ge(s_masks_loaded, 3 * 16)
                dve.wait_ge(s_sc_mm, 8 * n + i + 1)
                if a or n:
                    dve.wait_ge(s_pt_mm, 8 * n + i - RG + 1)
                ps = bank(f"scores{a}", n, r).rearrange("p (t c k) -> p t c k", t=TT, c=4)
                pr = probs[:, r].rearrange("p (t c) k -> p t c k", t=TT)
                v.tensor_tensor(pr, ps, mask_of(a, n, mask1, mask2), ALU.mult).then_inc(s_masked, 1)

            def shifting(i, n):
                r = i % RG
                dve.wait_ge(s_biased, 8 * n + i + 1)
                link(v.tensor_reduce(row_max[:, r, :], probs[:, r], AX_X, ALU.max))
                v.tensor_tensor(probs[:, r], probs[:, r], row_max[:, r, :].unsqueeze(2).broadcast_to([P, 8, SEQ]),
                                ALU.subtract).then_inc(s_shifted, 1)

            def attended_norm(a, n):
                dve.wait_ge(s_pv_mm, 8 * n + 4 * a + 4)
                if a or n:
                    dve.wait_ge(s_oT_mm, 2 * n + a)
                ps = [bank(f"weighed{a}", n, t)[:, 0:NH * (HD + 1)].rearrange("p (h d) -> p h d", h=NH) for t in range(TT)]
                for t in range(TT):
                    last = v.reciprocal(rden[:, t, :], ps[t][:, :, HD])
                link(last)
                for t in range(TT):
                    v.tensor_tensor(o_tok[:, t, :].rearrange("p (h d) -> p h d", h=NH), ps[t][:, :, 0:HD],
                                    rden[:, t, :].unsqueeze(2).broadcast_to([P, NH, HD]), ALU.mult).then_inc(s_o_norm, 1)

            def residual(i, n):
                if i == 2:
                    dve.wait_ge(s_w2_mm, n + 1)
                    if n:
                        dve.wait_ge(s_x1_done, n)
                else:
                    dve.wait_ge(s_ao_mm, 2 * n + i + 1)
                dve.wait_ge(s_x_biased, 3 * n + i + 1)
                use, dst = (("attention_out0", x_res), ("attention_out1", x_res), ("mlp_down", x_mid))[i]
                v.tensor_tensor(flat(dst[:, :, :]), bank(use, n), flat(x_bias[:, :, :]), ALU.add).then_inc(s_x_res, 1)

            def lerp(dst, i, name):
                for h in range(HALF):
                    at = slice(h * GB, (h + 1) * GB)
                    last = v.scalar_tensor_tensor(tokens(dst)[:, at, :], tokens(sx[:, i])[:, at, :], vec(name, h),
                                                  xe[:, i, at, 1:], ALU.mult, ALU.add)
                return last

            def shift(i, n):
                dve.wait_ge(s_l1_h, 2 * n + i + 1)
                dve.wait_ge(s_l1_edge, 2 * n + i + 1)
                link(v.tensor_tensor(tokens(sx[:, i]), xe[:, i, :, 0:SEQ], xe[:, i, :, 1:], ALU.subtract))
                if i == 0:
                    if n:
                        dve.wait_ge(s_xl_mm, n)
                    lerp(xl[:, :, :], 0, "maa_x").then_inc(s_l1_in, 1)
                else:
                    if n:
                        dve.wait_ge(s_fk_mm, n)
                        dve.wait_ge(s_fr_mm, n)
                    lerp(xk[:, :, :], 1, "mix_k")
                    lerp(xr[:, :, :], 1, "mix_r").then_inc(s_shift2, 1)

            def mixing(i, n):
                f = MIX_ORDER[i]
                dve.wait_ge(s_mix_mm, MIX * n + i + 1)
                if n:
                    if f == 1:
                        dve.wait_ge(s_td1_mm, n)
                    elif f == 4:
                        dve.wait_ge(s_g_mm, n)
                    else:
                        dve.wait_ge(s_kvr_mm, 3 * n)
                ps = bank(f"mix{i}", n).rearrange("p (h t) -> p h t", h=HALF)
                for h in range(HALF):
                    last = v.scalar_tensor_tensor(xm[:, f, h, :], ps[:, h, :], vec("maa_stack", 2 * f + h), sx[:, 0, h, :],
                                                  ALU.add, ALU.mult)
                last.then_inc(s_mixed, 1)

            def gating(_, n):
                dve.wait_ge(s_g_tanh, n + 1)
                if n:
                    dve.wait_ge(s_y, n)
                v.scalar_tensor_tensor(flat(gate[:, :, :]), flat(g_t[:, :, :]), 1.0, bank("gate", n), ALU.add, ALU.mult).then_inc(s_gate, 1)

            def bonus_value(_, n):
                dve.wait_ge(s_bonus_mm, n + 1)
                dve.wait_ge(s_kvr_ev, 3 * n + 2)
                v.tensor_tensor(rk[:, :, :], bank("bonus", n).rearrange("p (h t) -> p h t", h=HALF), vT[:, :, :],
                                ALU.mult).then_inc(s_bonus_v, 1)

            def recur(j, n):
                if j == 0:
                    dve.wait_ge(s_s0_in, n + 1)
                    dve.wait_ge(s_decay, 2 * n + 2)
                    dve.wait_ge(s_kvr_ev, 3 * n + 3)
                dve.wait_ge(s_vb_mm, S2 * n + j + 1)
                vb = bank(f"spread{j}", n).rearrange("p (c t) -> p c t", t=SEQ)
                v.tensor_tensor(wkv[:, j, :, 1:], vb[:, :, 0:SEQ - 1], tokens(kT[:, :, :])[:, :, 0:SEQ - 1], ALU.mult).then_inc(s_kv, 1)
                dve.wait_ge(s_kv, S2 * n + j + 1)
                line = wkv[:, j, :, :].rearrange("p c t -> p (c t)")
                v.tensor_tensor_scan(line, dec[:, :, :].rearrange("p c t -> p (c t)"), line, 0.0, ALU.mult, ALU.add).then_inc(s_scanned, 1)
                dve.wait_ge(s_scanned, S2 * n + j + 1)
                v.tensor_tensor(wkv[:, j, :, :], wkv[:, j, :, :], tokens(rT[:, :, :]), ALU.mult).then_inc(s_prod, 1)

            def centre(_, n):
                dve.wait_ge(s_bonus_in, n + 1)
                ps = bank("wkv", n).rearrange("p (h d) -> p h d", d=S2)
                link(v.tensor_reduce(head_sum[:, :], ps, AX_X, ALU.add))
                if n:
                    dve.wait_ge(s_y, n)
                v.scalar_tensor_tensor(centred[:, :, :], head_sum[:, :].unsqueeze(2).broadcast_to([P, TT * H2, S2]), -1.0 / S2,
                                       ps, ALU.mult, ALU.add).then_inc(s_centred, 1)

            def head_norm(_, n):
                dve.wait_ge(s_squared, n + 1)
                y, q, t, h = (nw[:, i, :] for i in range(4))
                link(v.tensor_reduce(t, y_tok[:, :, :].rearrange("p t (h d) -> p (t h) d", d=S2), AX_X, ALU.add))
                link(v.tensor_scalar(q, t, 1.0 / S2, EPS, ALU.mult, ALU.add))
                link(v.tensor_scalar(t.bitcast(I32), q.bitcast(I32), 1, None, ALU.logical_shift_right))
                link(v.tensor_scalar(y.bitcast(I32), t.bitcast(I32), -1.0, float(0x5F3759DF), ALU.mult, ALU.add))
                link(v.tensor_scalar(h, q, -0.5, None, ALU.mult))
                for _i in range(3):
                    link(v.tensor_tensor(t, y, y, ALU.mult))
                    link(v.tensor_tensor(t, t, h, ALU.mult))
                    link(v.scalar_tensor_tensor(y, t, 1.5, y, ALU.add, ALU.mult))
                v.tensor_tensor(centred[:, :, :], centred[:, :, :], y.unsqueeze(2).broadcast_to([P, TT * H2, S2]),
                                ALU.mult).then_inc(s_normed, 1)

            def gated(_, n):
                dve.wait_ge(s_gn_out, 2 * n + 2)
                dve.wait_ge(s_gate, n + 1)
                v.scalar_tensor_tensor(flat(y_tok[:, :, :]), centred[:, :, :].rearrange("p h d -> p (h d)"), 0.5, flat(gate[:, :, :]),
                                       ALU.mult, ALU.mult).then_inc(s_y, 1)

            def wkv_residual(_, n):
                dve.wait_ge(s_wo_mm, n + 1)
                if n:
                    dve.wait_ge(s_result, n)
                v.tensor_tensor(flat(x1[:, :, :]), bank("wkv_out", n), flat(x_mid[:, :, :]), ALU.add).then_inc(s_x1_done, 1)

            def finish(_, n):
                dve.wait_ge(s_fv_mm, n + 1)
                dve.wait_ge(s_fr_ev, n + 1)
                if n:
                    dve.wait_ge(s_out_stored, 16 * n)
                v.scalar_tensor_tensor(flat(result[:, :, :]), flat(fr_t[:, :, :]), 1.0, bank("ffn_value", n), ALU.add, ALU.mult).then_inc(s_fv_ev, 1)
                dve.wait_ge(s_fv_ev, n + 1)
                v.scalar_tensor_tensor(flat(result[:, :, :]), flat(result[:, :, :]), 0.5, flat(x1[:, :, :]), ALU.mult, ALU.add).then_inc(s_result, 1)

            def init_keys(_, n):
                dve.wait_ge(s_v_loaded, 16)
                dve.wait_ge(s_ident_loaded, 16)
                for a, (name, at) in enumerate((("b_qkv", 2), ("b_kv", 0))):
                    for h in range(HALF):
                        last = v.tensor_scalar(key_bias[:, a, h, :], C[:, C_PAR:C_PAR + 2], vec(name, at + h), None, ALU.mult)
                last.then_inc(s_init_keys, 1)

            def init_masks(_, n):
                dve.wait_ge(s_masks_loaded, 3 * 16)
                v.tensor_scalar(mask1b[:, :], mask1[:, :], -1.0, 10000.0, ALU.add, ALU.mult)
                v.tensor_scalar(mask2b[:, :, :], mask2[:, :, :], -1.0, 10000.0, ALU.add, ALU.mult).then_inc(s_init_masks, 1)

            def init_heads(_, n):
                dve.wait_ge(s_consts_loaded, 16)
                for h in range(HALF):
                    last = v.tensor_scalar(u_heads[:, h, :], head_ones, vec("u", h), None, ALU.mult)
                last.then_inc(s_init_heads, 1)

            steps = dict(norm_stats=norm_stats, norm=norm, masking=masking, shifting=shifting, attended_norm=attended_norm,
                         residual=residual, init_keys=init_keys, init_masks=init_masks, init_heads=init_heads, shift=shift, mixing=mixing, gating=gating, bonus_value=bonus_value, recur=recur,
                         centre=centre, head_norm=head_norm, gated=gated, wkv_residual=wkv_residual, finish=finish)
            for name, i, n, _given in order("dve"):
                steps[name](i, n)

        @block.gpsimd
        def _(pool):
            g = nc.gpsimd

            def rsqrt(i, n):
                if i >= 3:
                    pool.wait_ge(s_l1_var, 2 * n + i - 2)
                    if i == 4 or n:
                        pool.wait_ge(s_l1_norm, 2 * n + i - 3)
                    g.tensor_tensor(rstd[:, 1, :], var_eps[:, 1, :], minus_half[:, :], ALU.pow).then_inc(s_l1_rstd, 1)
                else:
                    pool.wait_ge(s_l0_var, 3 * n + i + 1)
                    if i or n:
                        pool.wait_ge(s_l0_norm, 3 * n + i)
                    g.tensor_tensor(rstd[:, 0, :], var_eps[:, 0, :], minus_half[:, :], ALU.pow).then_inc(s_l0_rstd, 1)

            def bias_residual(i, n):
                if i:
                    pool.wait_ge(s_x_res, 3 * n + i)
                else:
                    pool.wait_ge(s_x_loaded, 16 * n + 16)
                    if n:
                        pool.wait_ge(s_x_res, 3 * n)
                pool.wait_ge(s_rows_loaded, 16)
                src = x_in if i == 0 else x_res
                g.tensor_tensor(x_bias[:, :, :], src[:, :, :], row(("b_ao", "b_co", "b2")[i]), ALU.add).then_inc(s_x_biased, 1)

            def mask_bias(i, n):
                a, r = i // RG, i % RG
                pool.wait_ge(s_init_masks, 1)
                pool.wait_ge(s_masked, 8 * n + i + 1)
                pr = probs[:, r].rearrange("p (t c) k -> p t c k", t=TT)
                g.tensor_tensor(pr, pr, mask_of(a, n, mask1b, mask2b), ALU.add).then_inc(s_biased, 1)

            def edge_in(i, n):
                pool.wait_ge(s_s_loaded, 2 * 16)
                if n and i == 0:
                    pool.wait_ge(s_l1_in, n)
                if n and i == 1:
                    pool.wait_ge(s_shift2, n)
                g.tensor_copy(xe[:, i, :, 0].rearrange("p (h b) -> p h b", h=HALF), edge[:, i, :, n * GB:(n + 1) * GB]).then_inc(s_l1_edge, 1)

            def mix_add(i, n):
                f = MIX_ORDER[i]
                pool.wait_ge(s_mixed, MIX * n + i + 1)
                g.tensor_tensor(tokens(xm[:, f]), tokens(xm[:, f]), xe[:, 0, :, 1:], ALU.add).then_inc(s_mix_done, 1)

            def rk_product(_, n):
                pool.wait_ge(s_kvr_ev, 3 * n + 3)
                if n:
                    pool.wait_ge(s_bonus_in, n)
                g.tensor_tensor(rk[:, :, :], kT[:, :, :], rT[:, :, :], ALU.mult).then_inc(s_rk, 1)

            def state_in(_, n):
                pool.wait_ge(s_s_loaded, 2 * 16)
                if n:
                    pool.wait_ge(s_wkv_mm, S2 * n)
                g.tensor_copy(wkv[:, :, :, 0], s0_sb[:, n, :, :]).then_inc(s_s0_in, 1)

            def group_norm(_, n):
                pool.wait_ge(s_normed, n + 1)
                c = centred[:, :, :].rearrange("p (t h) d -> p t (h d)", t=TT)
                g.tensor_tensor(c, c, row("gn_w"), ALU.mult).then_inc(s_gn_out, 1)
                pool.wait_ge(s_gn_out, 2 * n + 1)
                g.tensor_tensor(c, c, row("gn_b"), ALU.add).then_inc(s_gn_out, 1)

            g.memset(v_bd[:, :, :, :, :, :], 0.0)
            g.memset(dec[:, :, 0:1], 0.0)
            g.memset(minus_half[:, :], -0.5)
            g.drain()
            for q in range(2):
                last = g.memset(v_bd[q * SEQ:(q + 1) * SEQ, :, :, :, q, HD:HD + 1], 1.0)
            last.then_inc(s_init_g, 1)
            pool.wait_ge(s_init_g, 1)
            steps = dict(rsqrt=rsqrt, bias_residual=bias_residual, mask_bias=mask_bias, edge_in=edge_in, mix_add=mix_add,
                         rk_product=rk_product, state_in=state_in, group_norm=group_norm)
            for name, i, n, _given in order("pool"):
                steps[name](i, n)


def kernel(**inputs):
    import numpy as np
    import concourse.bacc as bacc
    from concourse.bass_utils import run_bass_kernel_spmd as run

    def a(name):
        return np.asarray(inputs[name])

    l0 = {k[len("L0_xattn_"):]: np.asarray(v) for k, v in inputs.items() if k.startswith("L0_xattn_")}
    l1 = {k[len("L1_xattn_"):]: np.asarray(v) for k, v in inputs.items() if k.startswith("L1_xattn_")}

    src = {n: l0[n] for n in ("w_qkv", "w_ao", "w_q", "w_kv", "w_co", "w1", "w2")}
    src |= {n: l1[n] for n in ("maa_w1", "td_w1", "td_w2")}
    src |= {n: l1[n].T for n in ("Wk", "Wv", "Wr", "Wg", "Wo", "Wfk", "Wfr", "Wfv")}
    src["maa_w2"] = l1["maa_w2"][:4].reshape(4 * DM, E)
    src["maa_w2_last"] = l1["maa_w2"][4]
    W = np.zeros((P, W_COLS), np.float32)
    for name, (at, kt, n) in W_AT.items():
        m = src[name]
        for k in range(kt):
            part = m[k * P:(k + 1) * P]
            W[:part.shape[0], at + k * n:at + (k + 1) * n] = part

    vsrc = {n: l0[n] for n in ("ln1_s", "ln1_b", "ln2_s", "ln2_b", "ln3_s", "ln3_b", "b_qkv", "b_q", "b_kv", "b1")}
    vsrc |= {"r_ln1_w": l1["ln1_w"], "r_ln1_b": l1["ln1_b"], "r_ln2_w": l1["ln2_w"], "r_ln2_b": l1["ln2_b"],
             "maa_x": l1["maa_x"], "maa_stack": l1["maa_stack"], "time_decay": l1["time_decay"], "u": l1["u"],
             "mix_k": l1["ffn_maa_k"], "mix_r": l1["ffn_maa_r"]}
    V = np.concatenate([vsrc[name].reshape(n, P).T for name, n in VECTORS], axis=1)
    R = np.stack([l0["b_ao"], l0["b_co"], l0["b2"], l1["gn_w"], l1["gn_b"]])

    C = np.zeros((P, C_COLS), np.float32)
    at = np.arange(P)
    C[at, C_IDENT + at] = 1
    for j in range(S2):
        for i in range(S2):
            C[at[::S2] + j, C_SEL + j * P + at[::S2] + i] = 1
    C[at, C_HEADS + at // S2] = 1
    C[:, C_ONES:C_ONES + P] = at[:, None] // S2 == at[None, :] // S2
    for q in range(2):
        C[:, C_PAR + q] = (at // HD % 2 == q) * HD ** -0.5

    ctx = a("ctx_2048")
    s0 = ctx[:, 2:2 + S2].reshape(GROUPS, GB, HALF, P, S2).transpose(3, 0, 4, 2, 1).reshape(P, GROUPS, S2, HALF * GB)
    state01 = ctx[:, 1::-1].reshape(NB, 2, HALF, P).transpose(3, 1, 2, 0)
    arrays = {
        "x_in_dram": a("x").reshape(NB * SEQ, E),
        "ctxT_dram": ctx.reshape(NB * SEQ, HALF, P).transpose(2, 1, 0),
        "s0_dram": s0,
        "state01_dram": state01,
        "self_mask_dram": a("mask_1x1xSxS2_fc1").reshape(SEQ, SEQ),
        "cross_mask_dram": a("mask_Bx1xSxS2_ff1").reshape(NB, SEQ, SEQ),
        "weights_dram": W, "vectors_dram": V, "rows_dram": R, "consts_dram": C,
    }
    arrays = {k: np.ascontiguousarray(v) for k, v in arrays.items()}
    nc = bacc.Bacc("TRN2", target_bir_lowering=False, num_devices=1)
    args = [nc.dram_tensor(k, v.shape, F32, kind="ExternalInput").ap() for k, v in arrays.items()]
    args.append(nc.dram_tensor("out_dram", (NB * SEQ, E), F32, kind="ExternalOutput").ap())
    build(nc, *args)
    r = run(nc, [arrays], core_ids=[0])
    return r.results[0]["out_dram"].reshape(NB, SEQ, E)
```

```python
from contextlib import ExitStack

import concourse.bass as bass
from concourse import mybir

P = 128
E = 256
HALF = E // P
NB, SEQ = 16, 64
GB = 4
GROUPS = NB // GB
T = GB * SEQ
TT = T // P
NH, HD = 16, 16
HP = NH // 2
RG = P // 32
F1 = 4 * E
H2, S2 = 32, 8
HH = P // S2
MIX, DM, DD = 5, 32, 64
SLOTS = 4
EPS = 1e-5

F32 = mybir.dt.float32
I32 = mybir.dt.int32
ALU = mybir.AluOpType
ACT = mybir.ActivationFunctionType
AX_X = mybir.AxisListType.X

WEIGHTS = [("w_qkv", 2, 3 * E), ("w_ao", 2, E), ("w_q", 2, E), ("w_kv", 2, 2 * E), ("w_co", 2, E),
           ("w1", 2, F1), ("w2", 8, E),
           ("maa_w1", 2, MIX * DM), ("maa_w2", 1, E), ("maa_w2_last", 1, E), ("td_w1", 2, DD), ("td_w2", 1, E),
           ("Wk", 2, E), ("Wv", 2, E), ("Wr", 2, E), ("Wg", 2, E), ("Wo", 2, E),
           ("Wfk", 2, E), ("Wfr", 2, E), ("Wfv", 2, E)]
W_AT, W_COLS = {}, 0
for _name, _kt, _n in WEIGHTS:
    W_AT[_name] = (W_COLS, _kt, _n)
    W_COLS += _kt * _n
W_PIECES = ["w_qkv", "w_ao", "w1", "maa_w1", "Wk", "Wo"]

VECTORS = [("ln1_s", 2), ("ln1_b", 2), ("ln2_s", 2), ("ln2_b", 2), ("ln3_s", 2), ("ln3_b", 2),
           ("b_qkv", 6), ("b_q", 2), ("b_kv", 4), ("b1", 8),
           ("r_ln1_w", 2), ("r_ln1_b", 2), ("r_ln2_w", 2), ("r_ln2_b", 2),
           ("maa_x", 2), ("maa_stack", 2 * MIX), ("time_decay", 2), ("u", 2), ("mix_k", 2), ("mix_r", 2)]
V_AT, V_COLS = {}, 0
for _name, _n in VECTORS:
    V_AT[_name] = V_COLS
    V_COLS += _n

ROWS = ["b_ao", "b_co", "b2", "gn_w", "gn_b"]

C_IDENT, C_PAR, C_HEADS, C_ONES, C_SEL = 0, P, P + 2, P + 2 + HH, 2 * P + 2 + HH
C_COLS = C_SEL + S2 * P

MIX_ORDER = [1, 0, 2, 3, 4]

ORDER = {
    "pe": """
    norm_turn.0.0:0 norm_turn.0.1:1 key.0.0:0 query.0.0:1 value.0.0:2 scores.0.0:1034 scores_rest.0.0 key.1.0:2 key.0.1:4
    value.1.0:2 probs_turn.0.0:3 probs_turn.1.0:0 probs_turn.2.0:1 probs_turn.3.0:5 weigh.0.0:36 weigh.1.0 weigh.2.0
    weigh.3.0 query.0.1:5 attended_turn.0.0:3 value.0.1:2 attention_out.0.0:3 scores.0.1:2564 key.1.1:3 norm_turn.1.0:1
    scores_rest.0.1 query.1.0:1 value.1.1:5 scores.1.0:1462 probs_turn.0.1:0 scores_rest.1.0 weigh.0.1:07 probs_turn.1.1:1
    probs_turn.2.1:4 probs_turn.3.1:3 weigh.1.1 weigh.2.1 weigh.3.1 probs_turn.4.0:3 probs_turn.5.0:4 weigh.4.0:31 weigh.5.0
    probs_turn.6.0:4 probs_turn.7.0:2 attended_turn.0.1:0 weigh.6.0 weigh.7.0 attention_out.0.1:0 attended_turn.1.0:1
    attention_out.1.0:1 norm_turn.1.1:0 query.1.1:0 norm_turn.2.0:1 scores.1.1:0352 mlp_up.0.0:1 mlp_up.1.0:4 mlp_up.2.0:7
    mlp_up.3.0:4 scores_rest.1.1 mlp_down.0.0:4 probs_turn.4.1:2 probs_turn.5.1:5 probs_turn.6.1:3 weigh.4.1:20
    probs_turn.7.1:4 weigh.5.1 weigh.6.1 weigh.7.1 norm_turn.0.2:4 norm_turn.3.0:3 attended_turn.1.1:0 query.0.2:4
    attention_out.1.1:0 lora_in.0.0:4 key.0.2:0 mix.0.0:4 mix.1.0:3 norm_turn.2.1:2 mix.2.0:5 mix.3.0:4 decay_in.0.0:2
    kvr.0.0:4 decay_out.0.0:2 kvr.1.0:5 kvr.2.0:4 spread.0.0:5 spread.1.0:2 spread.2.0:4 mlp_up.0.1:3 wkv_sum.0.0:5
    spread.3.0:0 wkv_sum.1.0 spread.4.0:2 spread.5.0:3 spread.6.0:4 bonus.0.0:7 spread.7.0:0 wkv_sum.2.0 wkv_sum.3.0
    wkv_sum.4.0 mlp_up.1.1:2 wkv_sum.5.0 mlp_up.2.1:3 wkv_sum.6.0 wkv_sum.7.0 wkv_bonus.0.0 mix.4.0:7 mlp_up.3.1:3
    scores.0.2:7502 gate_in.0.0:3 scores_rest.0.2 value.0.2:4 y_turn.0.0:3 key.1.2:7 wkv_out.0.0:2 mlp_down.0.1:3
    probs_turn.0.2:2 probs_turn.1.2:7 norm_turn.4.0:4 probs_turn.2.2:3 probs_turn.3.2:2 weigh.0.2:70 weigh.1.2 weigh.2.2
    weigh.3.2 value.1.2:2 attended_turn.0.2:0 ffn_gate.0.0:7 norm_turn.3.1:2 ffn_key.0.0:0 attention_out.0.2:2 lora_in.0.1:0
    norm_turn.0.3:2 ffn_value.0.0:7 norm_turn.1.2:2 mix.0.1:0 mix.1.1:3 mix.2.1:2 query.1.2:0 mix.3.1:2 kvr.0.1:3
    scores.1.2:2074 kvr.1.1:3 scores_rest.1.2 decay_in.0.1:3 mix.4.1:5 decay_out.0.1:0 kvr.2.1:7 spread.0.1:4 spread.1.1:0
    spread.2.1:7 probs_turn.4.2:3 probs_turn.5.2:2 probs_turn.6.2:1 weigh.4.2:36 weigh.5.2 wkv_sum.0.1:1 weigh.6.2
    spread.3.1:4 spread.4.1:2 probs_turn.7.2:0 wkv_sum.1.1 weigh.7.2 spread.5.1:0 wkv_sum.2.1 spread.6.1:7 spread.7.1:4
    attended_turn.1.2:3 wkv_sum.3.1 bonus.0.1:6 attention_out.1.2:2 wkv_sum.4.1 wkv_sum.5.1 key.0.3:6 gate_in.0.1:5
    wkv_sum.6.1 value.0.3:6 query.0.3:2 wkv_sum.7.1 norm_turn.2.2:6 wkv_bonus.0.1 scores.0.3:2547 mlp_up.0.2:1 mlp_up.1.2:6
    mlp_up.2.2:0 mlp_up.3.2:6 y_turn.0.1:0 scores_rest.0.3 mlp_down.0.2:0 wkv_out.0.1:7 probs_turn.0.3:4 probs_turn.1.3:5
    probs_turn.2.3:2 weigh.0.3:47 probs_turn.3.3:5 weigh.1.3 weigh.2.3 norm_turn.4.1:5 key.1.3:0 weigh.3.3 norm_turn.3.2:5
    value.1.3:2 ffn_gate.0.1:0 attended_turn.0.3:2 ffn_key.0.1:4 attention_out.0.3:2 lora_in.0.2:4 ffn_value.0.1:2 mix.0.2:4
    norm_turn.1.3:0 mix.1.2:7 mix.2.2:2 query.1.3:0 mix.3.2:2 kvr.0.2:7 scores.1.3:2045 scores_rest.1.3 kvr.1.2:7
    decay_in.0.2:0 kvr.2.2:4 decay_out.0.2:0 probs_turn.4.3:5 spread.0.2:4 probs_turn.5.3:7 spread.1.2:2 spread.2.2:0
    weigh.4.3:56 probs_turn.6.3:1 probs_turn.7.3:7 weigh.5.3 weigh.6.3 weigh.7.3 spread.3.2:7 bonus.0.2:2
    attended_turn.1.3:5 wkv_sum.0.2:6 wkv_sum.1.2 attention_out.1.3:5 wkv_sum.2.2 mix.4.2:2 wkv_sum.3.2 spread.4.2:5
    spread.5.2:7 spread.6.2:2 norm_turn.2.3:0 spread.7.2:1 gate_in.0.2:4 wkv_sum.4.2 wkv_sum.5.2 mlp_up.0.3:7 wkv_sum.6.2
    mlp_up.1.3:2 wkv_sum.7.2 wkv_bonus.0.2 mlp_up.2.3:2 mlp_up.3.3:7 mlp_down.0.3:7 y_turn.0.2:2 wkv_out.0.2:2
    norm_turn.4.2:7 norm_turn.3.3:7 ffn_gate.0.2:7 lora_in.0.3:2 ffn_key.0.2:6 mix.0.3:2 mix.1.3:7 mix.2.3:6 mix.3.3:2
    decay_in.0.3:7 kvr.0.3:2 decay_out.0.3:7 kvr.1.3:6 kvr.2.3:2 spread.0.3:6 spread.1.3:7 spread.2.3:2 spread.3.3:4
    wkv_sum.0.3:6 spread.4.3:1 bonus.0.3:0 wkv_sum.1.3 mix.4.3:7 ffn_value.0.2:5 wkv_sum.2.3 spread.5.3:4 wkv_sum.3.3
    spread.6.3:0 wkv_sum.4.3 spread.7.3:1 gate_in.0.3:7 wkv_sum.5.3 wkv_sum.6.3 wkv_sum.7.3 wkv_bonus.0.3 y_turn.0.3:6
    wkv_out.0.3:6 norm_turn.4.3:6 ffn_key.0.3:6 ffn_gate.0.3:7 ffn_value.0.3:6""",
    "act": """
    normed.0.0 normed.0.1 key_out.0.0 query_out.0.0 value_out.0.0 key_out.1.0 probs_exp.0.0 probs_exp.1.0 probs_exp.2.0
    probs_exp.3.0 probs_out.0.0 probs_out.1.0 probs_out.2.0 probs_out.3.0 key_out.0.1 value_out.1.0 query_out.0.1
    attended.0.0 value_out.0.1 normed.1.0 query_out.1.0 probs_exp.0.1 probs_exp.1.1 probs_out.0.1 probs_exp.2.1
    probs_exp.3.1 key_out.1.1 probs_out.1.1 probs_out.2.1 probs_out.3.1 probs_exp.4.0 probs_exp.5.0 probs_out.4.0
    probs_out.5.0 probs_exp.6.0 probs_exp.7.0 probs_out.6.0 probs_out.7.0 attended.0.1 value_out.1.1 attended.1.0 normed.1.1
    query_out.1.1 normed.2.0 gelu.0.0 gelu.1.0 gelu.2.0 gelu.3.0 probs_exp.4.1 probs_exp.5.1 probs_exp.6.1 probs_out.4.1
    probs_exp.7.1 probs_out.5.1 probs_out.6.1 probs_out.7.1 normed.0.2 normed.3.0 attended.1.1 query_out.0.2 lora_out.0.0
    key_out.0.2 normed.2.1 decay_tanh.0.0 kvr_out.0.0 decay_exp.0.0 kvr_out.1.0 kvr_out.2.0 gelu.0.1 gelu.1.1 gelu.2.1
    square.0.0 gelu.3.1 gate_tanh.0.0 value_out.0.2 y_out.0.0 key_out.1.2 probs_exp.0.2 probs_exp.1.2 probs_exp.2.2
    probs_exp.3.2 probs_out.0.2 probs_out.1.2 normed.4.0 probs_out.2.2 probs_out.3.2 value_out.1.2 attended.0.2 ffn_tanh.0.0
    normed.3.1 ffn_square.0.0 lora_out.0.1 normed.0.3 normed.1.2 query_out.1.2 kvr_out.0.1 kvr_out.1.1 decay_tanh.0.1
    decay_exp.0.1 probs_exp.4.2 kvr_out.2.1 probs_exp.5.2 probs_exp.6.2 probs_out.4.2 probs_out.5.2 probs_out.6.2
    probs_exp.7.2 probs_out.7.2 attended.1.2 key_out.0.3 gate_tanh.0.1 value_out.0.3 query_out.0.3 normed.2.2 square.0.1
    gelu.0.2 gelu.1.2 gelu.2.2 gelu.3.2 y_out.0.1 probs_exp.0.3 probs_exp.1.3 probs_exp.2.3 probs_exp.3.3 probs_out.0.3
    probs_out.1.3 probs_out.2.3 probs_out.3.3 normed.4.1 key_out.1.3 normed.3.2 value_out.1.3 ffn_tanh.0.1 attended.0.3
    ffn_square.0.1 lora_out.0.2 normed.1.3 query_out.1.3 kvr_out.0.2 kvr_out.1.2 decay_tanh.0.2 probs_exp.4.3 kvr_out.2.2
    probs_exp.5.3 decay_exp.0.2 probs_exp.6.3 probs_out.4.3 probs_exp.7.3 probs_out.5.3 probs_out.6.3 probs_out.7.3
    attended.1.3 normed.2.3 gate_tanh.0.2 gelu.0.3 gelu.1.3 square.0.2 gelu.2.3 gelu.3.3 y_out.0.2 normed.4.2 normed.3.3
    ffn_tanh.0.2 lora_out.0.3 ffn_square.0.2 decay_tanh.0.3 kvr_out.0.3 decay_exp.0.3 kvr_out.1.3 kvr_out.2.3 gate_tanh.0.3
    square.0.3 y_out.0.3 normed.4.3 ffn_square.0.3 ffn_tanh.0.3""",
    "dve": """
    norm_stats.0.0 init_keys.0.0 norm_stats.0.1 norm.0.0 norm.0.1 init_masks.0.0 masking.0.0 masking.1.0 masking.2.0
    masking.3.0 shifting.0.0 shifting.1.0 shifting.2.0 shifting.3.0 init_heads.0.0 attended_norm.0.0 residual.0.0
    norm_stats.1.0 norm.1.0 masking.0.1 masking.1.1 masking.2.1 masking.3.1 shifting.0.1 shifting.1.1 shifting.2.1
    shifting.3.1 masking.4.0 masking.5.0 masking.6.0 masking.7.0 shifting.4.0 shifting.5.0 shifting.6.0 shifting.7.0
    attended_norm.0.1 attended_norm.1.0 residual.0.1 norm_stats.1.1 norm.1.1 residual.1.0 norm_stats.2.0 norm.2.0
    norm_stats.0.2 norm.0.2 masking.4.1 masking.5.1 masking.6.1 masking.7.1 shifting.4.1 shifting.5.1 shifting.6.1
    shifting.7.1 residual.2.0 norm_stats.3.0 norm.3.0 attended_norm.1.1 shift.0.0 residual.1.1 norm_stats.2.1 norm.2.1
    norm_stats.0.3 mixing.0.0 mixing.1.0 norm.0.3 mixing.2.0 mixing.3.0 recur.0.0 recur.1.0 recur.2.0 recur.3.0 recur.4.0
    recur.5.0 recur.6.0 recur.7.0 bonus_value.0.0 centre.0.0 mixing.4.0 head_norm.0.0 group_norm.0.0 gating.0.0 gated.0.0
    masking.0.2 masking.1.2 masking.2.2 masking.3.2 shifting.0.2 shifting.1.2 wkv_residual.0.0 shifting.2.2 shifting.3.2
    norm_stats.4.0 norm.4.0 residual.2.1 norm_stats.3.1 shift.1.0 attended_norm.0.2 norm.3.1 shift.0.1 residual.0.2
    norm_stats.1.2 norm.1.2 finish.0.0 mixing.0.1 mixing.1.1 mixing.2.1 mixing.3.1 masking.4.2 masking.5.2 masking.6.2
    masking.7.2 shifting.4.2 shifting.5.2 shifting.6.2 recur.0.1 shifting.7.2 recur.1.1 recur.2.1 recur.3.1
    attended_norm.1.2 recur.4.1 recur.5.1 bonus_value.0.1 mixing.4.1 recur.6.1 recur.7.1 residual.1.2 norm_stats.2.2
    gating.0.1 norm.2.2 centre.0.1 head_norm.0.1 group_norm.0.1 gated.0.1 masking.0.3 masking.1.3 masking.2.3 masking.3.3
    shifting.0.3 shifting.1.3 shifting.2.3 shifting.3.3 wkv_residual.0.1 norm_stats.4.1 residual.2.2 norm.4.1 norm_stats.3.2
    norm.3.2 shift.1.1 attended_norm.0.3 shift.0.2 residual.0.3 norm_stats.1.3 norm.1.3 finish.0.1 mixing.0.2 mixing.1.2
    mixing.2.2 mixing.3.2 masking.4.3 masking.5.3 masking.6.3 masking.7.3 shifting.4.3 shifting.5.3 shifting.6.3
    shifting.7.3 recur.0.2 recur.1.2 attended_norm.1.3 recur.2.2 bonus_value.0.2 recur.3.2 residual.1.3 norm_stats.2.3
    mixing.4.2 norm.2.3 recur.4.2 recur.5.2 recur.6.2 recur.7.2 gating.0.2 centre.0.2 head_norm.0.2 group_norm.0.2 gated.0.2
    wkv_residual.0.2 norm_stats.4.2 residual.2.3 norm.4.2 norm_stats.3.3 norm.3.3 shift.1.2 shift.0.3 mixing.0.3 mixing.1.3
    mixing.2.3 mixing.3.3 recur.0.3 recur.1.3 recur.2.3 recur.3.3 bonus_value.0.3 recur.4.3 mixing.4.3 recur.5.3 recur.6.3
    recur.7.3 finish.0.2 gating.0.3 centre.0.3 head_norm.0.3 group_norm.0.3 gated.0.3 wkv_residual.0.3 norm_stats.4.3
    norm.4.3 shift.1.3 finish.0.3""",
    "pool": """
    rsqrt.0.0 rsqrt.0.1 bias_residual.0.1 bias_residual.0.0 mask_bias.0.0 edge_in.0.0 mask_bias.1.0 mask_bias.2.0
    mask_bias.3.0 edge_in.1.0 bias_residual.1.0 rsqrt.1.0 mask_bias.0.1 mask_bias.1.1 mask_bias.2.1 mask_bias.3.1
    mask_bias.4.0 mask_bias.5.0 mask_bias.6.0 mask_bias.7.0 bias_residual.1.1 rsqrt.1.1 bias_residual.2.0 rsqrt.2.0
    rsqrt.0.2 mask_bias.4.1 mask_bias.5.1 mask_bias.6.1 mask_bias.7.1 bias_residual.0.2 rsqrt.3.0 edge_in.0.1
    bias_residual.2.1 rsqrt.2.1 rsqrt.0.3 mix_add.0.0 mix_add.1.0 mix_add.2.0 mix_add.3.0 rk_product.0.0 mix_add.4.0
    mask_bias.0.2 mask_bias.1.2 mask_bias.2.2 mask_bias.3.2 rsqrt.4.0 bias_residual.0.3 rsqrt.3.1 edge_in.1.1 edge_in.0.2
    bias_residual.1.2 rsqrt.1.2 mix_add.0.1 mix_add.1.1 mix_add.2.1 mix_add.3.1 mask_bias.4.2 mask_bias.5.2 mask_bias.6.2
    mask_bias.7.2 rk_product.0.1 mix_add.4.1 bias_residual.2.2 rsqrt.2.2 mask_bias.0.3 mask_bias.1.3 mask_bias.2.3
    mask_bias.3.3 rsqrt.4.1 rsqrt.3.2 edge_in.1.2 edge_in.0.3 bias_residual.1.3 rsqrt.1.3 mix_add.0.2 mix_add.1.2
    mix_add.2.2 mix_add.3.2 mask_bias.4.3 mask_bias.5.3 mask_bias.6.3 mask_bias.7.3 rk_product.0.2 bias_residual.2.3
    rsqrt.2.3 mix_add.4.2 rsqrt.4.2 rsqrt.3.3 edge_in.1.3 mix_add.0.3 mix_add.1.3 mix_add.2.3 mix_add.3.3 rk_product.0.3
    mix_add.4.3 rsqrt.4.3""",
}


def order(engine):
    for word in ORDER[engine].split():
        step, _, given = word.partition(":")
        name, i, n = step.split(".")
        yield name, int(i), int(n), [int(bank) for bank in given]


def bank_uses():
    named = {"norm_turn": "norm{}", "query": "query{}", "key": "key{}", "value": "value{}", "scores": "scores{}",
             "probs_turn": "probsT{}", "attended_turn": "oT{}", "attention_out": "attention_out{}", "mlp_up": "hidden{}",
             "mlp_down": "mlp_down", "lora_in": "lora", "mix": "mix{}", "decay_in": "decay_in", "decay_out": "decay_out",
             "kvr": "kvr{}", "gate_in": "gate", "bonus": "bonus", "spread": "spread{}", "wkv_sum": "wkv", "y_turn": "yT",
             "wkv_out": "wkv_out", "ffn_key": "ffn_key", "ffn_gate": "ffn_gate", "ffn_value": "ffn_value"}
    out = {}
    for name, i, n, given in order("pe"):
        if name == "weigh" and given:
            out[f"weighed{i // RG}", n] = given
        elif given:
            out[named[name].format(i), n] = given
    return out


BANKS = bank_uses()


def build(nc, x, ctxT, s0, state01, self_mask, cross_mask, weights, vectors, rows, consts, out):
    with ExitStack() as ctx:
        def sb(name, *shape):
            return ctx.enter_context(nc.sbuf_tensor(name, list(shape), F32))

        def sem(name):
            return ctx.enter_context(nc.semaphore(name))

        s_l0_norm = [sem("l0_norm_even"), sem("l0_norm_odd")]
        s_l0_normT = [sem("l0_normT_even"), sem("l0_normT_odd")]
        s_l0_h = [sem("l0_h_even"), sem("l0_h_odd")]
        s_q_mm = [sem("q_mm_even"), sem("q_mm_odd")]
        s_k_mm = [sem("k_mm_even"), sem("k_mm_odd")]
        s_v_mm = [sem("v_mm_even"), sem("v_mm_odd")]
        s_q_ev = [sem("q_ev_even"), sem("q_ev_odd")]
        s_k_ev = [sem("k_ev_even"), sem("k_ev_odd")]
        s_sc_mm = [sem("sc_mm_even"), sem("sc_mm_odd")]
        s_exped = [sem("exped_even"), sem("exped_odd")]
        s_pt_mm = [sem("pt_mm_even"), sem("pt_mm_odd")]
        s_v_ev = [sem("v_ev_even"), sem("v_ev_odd")]
        s_pt_ev = [sem("pt_ev_even"), sem("pt_ev_odd")]
        s_pv_mm = [sem("pv_mm_even"), sem("pv_mm_odd")]
        s_o_norm = [sem("o_norm_even"), sem("o_norm_odd")]
        s_oT_mm = [sem("oT_mm_even"), sem("oT_mm_odd")]
        s_oT_ev = [sem("oT_ev_even"), sem("oT_ev_odd")]
        s_ao_mm = [sem("ao_mm_even"), sem("ao_mm_odd")]
        s_mlp_mm = [sem("mlp_mm_even"), sem("mlp_mm_odd")]
        s_gelu = [sem("gelu_even"), sem("gelu_odd")]
        s_w2_mm = [sem("w2_mm_even"), sem("w2_mm_odd")]
        s_shifted = [sem("shifted_even"), sem("shifted_odd")]
        s_x_res = [sem("x_res_even"), sem("x_res_odd")]
        s_l0_rstd = [sem("l0_rstd_even"), sem("l0_rstd_odd")]
        s_l0_var = [sem("l0_var_even"), sem("l0_var_odd")]
        s_masked = [sem("masked_even"), sem("masked_odd")]
        s_biased = [sem("biased_even"), sem("biased_odd")]
        s_x_biased = [sem("x_biased_even"), sem("x_biased_odd")]
        s_x_loaded = [sem("x_loaded_even"), sem("x_loaded_odd")]
        s_l1_norm = sem("l1_norm")
        s_l1_normT = sem("l1_normT")
        s_ctx_loaded = sem("ctx_loaded")
        s_l1_in = sem("l1_in")
        s_xl_mm = sem("xl_mm")
        s_xl_ev = sem("xl_ev")
        s_mix_mm = sem("mix_mm")
        s_mix_done = sem("mix_done")
        s_td1_mm = sem("td1_mm")
        s_td_ev = sem("td_ev")
        s_td2_mm = sem("td2_mm")
        s_kv = sem("kv")
        s_kvr_mm = sem("kvr_mm")
        s_g_mm = sem("g_mm")
        s_init_heads = sem("init_heads")
        s_rk = sem("rk")
        s_bonus_mm = sem("bonus_mm")
        s_consts_loaded = sem("consts_loaded")
        s_kvr_ev = sem("kvr_ev")
        s_vb_mm = sem("vb_mm")
        s_prod = sem("prod")
        s_wkv_mm = sem("wkv_mm")
        s_bonus_v = sem("bonus_v")
        s_bonus_in = sem("bonus_in")
        s_y = sem("y")
        s_yT_mm = sem("yT_mm")
        s_yT_ev = sem("yT_ev")
        s_wo_mm = sem("wo_mm")
        s_shift2 = sem("shift2")
        s_fk_mm = sem("fk_mm")
        s_fr_mm = sem("fr_mm")
        s_kk = sem("kk")
        s_fv_mm = sem("fv_mm")
        s_ident_loaded = sem("ident_loaded")
        s_l1_h = sem("l1_h")
        s_init_keys = sem("init_keys")
        s_init_g = sem("init_g")
        s_decay = sem("decay")
        s_scanned = sem("scanned")
        s_g_tanh = sem("g_tanh")
        s_centred = sem("centred")
        s_squared = sem("squared")
        s_fk_ev = sem("fk_ev")
        s_out_stored = sem("out_stored")
        s_fr_ev = sem("fr_ev")
        s_v_loaded = sem("v_loaded")
        s_chain_v = sem("chain_v")
        s_x1_done = sem("x1_done")
        s_l1_rstd = sem("l1_rstd")
        s_l1_var = sem("l1_var")
        s_masks_loaded = sem("masks_loaded")
        s_l1_edge = sem("l1_edge")
        s_mixed = sem("mixed")
        s_gate = sem("gate")
        s_s_loaded = sem("s_loaded")
        s_normed = sem("normed")
        s_rows_loaded = sem("rows_loaded")
        s_gn_out = sem("gn_out")
        s_result = sem("result")
        s_fv_ev = sem("fv_ev")
        s_init_masks = sem("init_masks")
        s_w_loaded = [sem(f"w_loaded{i}") for i in range(len(W_PIECES))]
        banks = [ctx.enter_context(nc.psum_tensor(f"bank{i}", [P, 512], F32)) for i in range(8)]

        W = sb("W", P, W_COLS)
        V = sb("V", P, V_COLS)
        R = sb("R", P, len(ROWS), E)
        C = sb("C", P, C_COLS)
        ident = C[:, C_IDENT:C_IDENT + P]
        heads = C[:, C_HEADS:C_HEADS + HH]
        head_ones = C[:, C_ONES:C_ONES + P]
        mask1 = sb("mask1", P, SEQ)
        mask1b = sb("mask1b", P, SEQ)
        mask2 = sb("mask2", P, GROUPS * TT, SEQ)
        mask2b = sb("mask2b", P, GROUPS * TT, SEQ)
        key_bias = sb("key_bias", P, 2, HALF, 2)
        minus_half = sb("minus_half", P, TT)
        u_heads = sb("u_heads", P, HALF, P)

        x_in = sb("x_in", P, 2, TT, E)
        x_res = sb("x_res", P, 2, TT, E)
        x_mid = sb("x_mid", P, TT, E)
        x_bias = sb("x_bias", P, 2, TT, E)
        ctx_in = sb("ctx_in", P, HALF, T)
        stats = sb("stats", P, 3, TT, 6)
        moments = sb("moments", P, 3, TT, 2)
        var_eps = sb("var_eps", P, 3, TT)
        rstd = sb("rstd", P, 3, TT)
        xn = sb("xn", P, 3, TT, E)
        hT = sb("hT", P, 2, HALF, T)
        qT = sb("qT", P, 2, HALF, T)
        k_bd = sb("k_bd", P, 2, HALF, 2, T)
        v_bd = sb("v_bd", P, 2, GB, HP, 2, HD + 1)
        probs = sb("probs", P, 2, RG, 8, SEQ)
        row_max = sb("row_max", P, 2, RG, 8)
        rden = sb("rden", P, 2, TT, NH)
        o_tok = sb("o_tok", P, 2, TT, E)
        oT = sb("oT", P, 2, HALF, T)
        hidden = sb("hidden", P, F1 // P, T)

        xe = sb("xe", P, 2, HALF * GB, SEQ + 1)
        edge = sb("edge", P, 2, HALF, NB)
        sx = sb("sx", P, HALF, T)
        xl = sb("xl", P, HALF, T)
        lora = sb("lora", P, T)
        lora_last = sb("lora_last", DM, T)
        xm = sb("xm", P, MIX, HALF, T)
        td_h = sb("td_h", DD, T)
        dec_e = sb("dec_e", P, HALF * GB, SEQ)
        dec = sb("dec", P, HALF * GB, SEQ)
        kT = sb("kT", P, HALF, T)
        vT = sb("vT", P, HALF, T)
        rT = sb("rT", P, HALF, T)
        rk = sb("rk", P, HALF, T)
        gate = sb("gate", P, TT, E)
        s0_sb = sb("s0_sb", P, GROUPS, S2, HALF * GB)
        wkv = sb("wkv", P, SLOTS, HALF * GB, SEQ)
        head_sum = sb("head_sum", P, TT * H2)
        centred = sb("centred", P, TT * H2, S2)
        nw = sb("nw", P, 4, TT * H2)
        x1 = sb("x1", P, TT, E)
        xk = sb("xk", P, HALF, T)
        xr = sb("xr", P, HALF, T)
        kk = sb("kk", P, HALF, T)
        result = sb("result", P, TT, E)
        y_tok, yT, sx_ffn = xr, xk, kk

        block = ctx.enter_context(nc.Block())

        def w(name, kt, a, b, rows_=slice(0, P)):
            at, _, n = W_AT[name]
            return W[rows_, at + kt * n + a:at + kt * n + b]

        def vec(name, i):
            return V[:, V_AT[name] + i:V_AT[name] + i + 1]

        def row(name):
            return R[:, ROWS.index(name), :].unsqueeze(1).broadcast_to([P, TT, E])

        def tok(n):
            return bass.ds(n * T, T)

        def tokens(ap):
            return ap.rearrange("p h (b t) -> p (h b) t", t=SEQ)

        def mask_of(a, n, own, cross):
            if a == 0:
                return own[:, :].unsqueeze(1).unsqueeze(1).broadcast_to([P, TT, 4, SEQ])
            return cross[:, bass.ds(n * TT, TT), :].unsqueeze(2).broadcast_to([P, TT, 4, SEQ])

        freed_by = {"lora": (s_xl_ev, 1, 1), "decay_in": (s_td_ev, 1, 1), "decay_out": (s_decay, 2, 1), "gate": (s_gate, 1, 1),
                    "bonus": (s_bonus_v, 1, 1), "wkv": (s_centred, 1, 1), "yT": (s_yT_ev, 1, 1), "wkv_out": (s_x1_done, 1, 1),
                    "ffn_key": (s_fk_ev, 1, 1), "ffn_gate": (s_fr_ev, 1, 1), "ffn_value": (s_fv_ev, 1, 1),
                    "mlp_down": (s_x_res, 3, 3)}
        for a in range(2):
            freed_by |= {f"query{a}": (s_q_ev, 2, a + 1), f"key{a}": (s_k_ev, 2, a + 1), f"value{a}": (s_v_ev, 2, a + 1),
                         f"scores{a}": (s_masked, 8, 4 * a + 1), f"weighed{a}": (s_o_norm, 4, 2 * a + 1),
                         f"oT{a}": (s_oT_ev, 2, a + 1), f"attention_out{a}": (s_x_res, 3, a + 1), f"norm{a + 3}": (s_l1_h, 2, a + 1)}
        freed_by |= {f"norm{i}": (s_l0_h, 3, i + 1) for i in range(3)}
        freed_by |= {f"probsT{i}": (s_pt_ev, 8, i + 1) for i in range(8)}
        freed_by |= {f"hidden{m}": (s_gelu, 4, m + 1) for m in range(4)}
        freed_by |= {f"mix{i}": (s_mixed, MIX, i + 1) for i in range(MIX)}
        freed_by |= {f"kvr{i}": (s_kvr_ev, 3, i + 1) for i in range(3)}
        freed_by |= {f"spread{j}": (s_kv, S2, j + 1) for j in range(S2)}

        @block.sync
        def _(sp):
            def load(n):
                if n > 1:
                    sp.wait_ge(s_x_biased[n % 2], 3 * (n // 2) - 2)
                    sp.wait_ge(s_l0_norm[n % 2], 3 * (n // 2) - 2)
                sp.dma_start(x_in[:, n % 2, :, :], x[n * T:(n + 1) * T, :].rearrange("(t p) d -> p t d", p=P)).then_inc(s_x_loaded[n % 2], 16)

            def load_ctx(n):
                if n:
                    sp.wait_ge(s_k_mm[1 - n % 2], 2 * ((n + 1) // 2))
                    sp.wait_ge(s_v_mm[1 - n % 2], 2 * ((n + 1) // 2))
                sp.dma_start(ctx_in[:, :, :], ctxT[:, :, n * T:(n + 1) * T]).then_inc(s_ctx_loaded, 16)

            def store(n):
                sp.wait_ge(s_result, n + 1)
                sp.dma_start(out[n * T:(n + 1) * T, :].rearrange("(t p) d -> p t d", p=P), result[:, :, :]).then_inc(s_out_stored, 16)

            def load_weights(i):
                a = W_AT[W_PIECES[i]][0]
                b = W_AT[W_PIECES[i + 1]][0] if i + 1 < len(W_PIECES) else W_COLS
                sp.dma_start(W[:, a:b], weights[:, a:b]).then_inc(s_w_loaded[i], 16)

            load(0)
            load(1)
            sp.dma_start(C[:, 0:C_HEADS], consts[:, 0:C_HEADS]).then_inc(s_ident_loaded, 16)
            sp.dma_start(V[:, :], vectors).then_inc(s_v_loaded, 16)
            load_weights(0)
            sp.dma_start(mask1[0:SEQ, :], self_mask).then_inc(s_masks_loaded, 16)
            sp.dma_start(mask1[SEQ:P, :], self_mask).then_inc(s_masks_loaded, 16)
            sp.dma_start(mask2[:, :, :], cross_mask.rearrange("(t b) q k -> (b q) t k", b=2)).then_inc(s_masks_loaded, 16)
            load_ctx(0)
            sp.wait_ge(s_w_loaded[0], 16)
            sp.dma_start(R[:, :, :], rows.partition_broadcast(P)).then_inc(s_rows_loaded, 16)
            for i in range(1, len(W_PIECES)):
                sp.wait_ge(s_w_loaded[i - 1], 16)
                load_weights(i)
                if i == 2:
                    sp.dma_start(s0_sb[:, :, :, :], s0).then_inc(s_s_loaded, 16)
                    sp.dma_start(edge[:, :, :, :], state01).then_inc(s_s_loaded, 16)
                    sp.dma_start(C[:, C_HEADS:], consts[:, C_HEADS:]).then_inc(s_consts_loaded, 16)
            for n in range(GROUPS):
                if n + 2 < GROUPS:
                    load(n + 2)
                if n + 1 < GROUPS:
                    load_ctx(n + 1)
                if n:
                    store(n - 1)
            store(GROUPS - 1)
            sp.wait_ge(s_out_stored, 16 * GROUPS)

        @block.tensor
        def _(pe):
            holder = {}

            def claim(use, n, i=0):
                bank = BANKS[use, n][i]
                if bank in holder:
                    signal, value = holder[bank]
                    pe.wait_ge(signal, value)
                signal, per, k = freed_by[use]
                holder[bank] = (signal[n % 2], per * (n // 2) + k + i) if isinstance(signal, list) else (signal, per * n + k + i)
                return banks[bank][:, :]

            def mm(o, lhsT, rhs, start=True, stop=True, **kw):
                return nc.tensor.matmul(o, lhsT, rhs, start=start, stop=stop, **kw)

            def to_features(ps, src):
                ps = ps.rearrange("p (h t) -> p h t", h=HALF)
                for h in range(HALF):
                    for t in range(TT):
                        last = nc.tensor.transpose(ps[:, h, t * P:(t + 1) * P], src[:, t, h * P:(h + 1) * P], ident)
                return last

            def features_out(ps, weight, a, src, kt=HALF):
                ps = ps.rearrange("p (h t) -> p h t", h=HALF)
                for m in range(HALF):
                    for k in range(kt):
                        last = mm(ps[:, m, :], w(weight, k, a + m * P, a + (m + 1) * P), src[:, k, :], k == 0, k == kt - 1)
                return last

            def tokens_out(ps, weight, src, at=0, kt=HALF):
                ps = ps.rearrange("p (t d) -> p t d", t=TT)
                for t in range(TT):
                    for k in range(kt):
                        last = mm(ps[:, t, :], src[:, k, t * P:(t + 1) * P], w(weight, k, at, at + E), k == 0, k == kt - 1)
                return last

            def norm_turn(i, n):
                if i < 3:
                    pe.wait_ge(s_l0_norm[n % 2], 3 * (n // 2) + i + 1)
                    to_features(claim(f"norm{i}", n), xn[:, n % 2]).then_inc(s_l0_normT[n % 2], 1)
                else:
                    pe.wait_ge(s_l1_norm, 2 * n + i - 2)
                    to_features(claim(f"norm{i}", n), xn[:, 2]).then_inc(s_l1_normT, 1)

            def query(a, n):
                pe.wait_ge(s_w_loaded[a], 16)
                pe.wait_ge(s_l0_h[n % 2], 3 * (n // 2) + a + 1)
                features_out(claim(f"query{a}", n), ("w_qkv", "w_q")[a], 0, hT[:, n % 2]).then_inc(s_q_mm[n % 2], 1)

            def key(a, n):
                if a:
                    pe.wait_ge(s_w_loaded[1], 16)
                    pe.wait_ge(s_ctx_loaded, 16 * n + 16)
                    features_out(claim("key1", n), "w_kv", 0, ctx_in).then_inc(s_k_mm[n % 2], 1)
                else:
                    pe.wait_ge(s_w_loaded[0], 16)
                    pe.wait_ge(s_l0_h[n % 2], 3 * (n // 2) + 1)
                    features_out(claim("key0", n), "w_qkv", E, hT[:, n % 2]).then_inc(s_k_mm[n % 2], 1)

            def value(a, n):
                if a:
                    pe.wait_ge(s_w_loaded[1], 16)
                    pe.wait_ge(s_ctx_loaded, 16 * n + 16)
                    tokens_out(claim("value1", n), "w_kv", ctx_in, E).then_inc(s_v_mm[n % 2], 1)
                else:
                    pe.wait_ge(s_w_loaded[0], 16)
                    pe.wait_ge(s_l0_h[n % 2], 3 * (n // 2) + 1)
                    tokens_out(claim("value0", n), "w_qkv", hT[:, n % 2], 2 * E).then_inc(s_v_mm[n % 2], 1)

            def scores(a, n):
                pe.wait_ge(s_q_ev[n % 2], 2 * (n // 2) + a + 1)
                pe.wait_ge(s_k_ev[n % 2], 2 * (n // 2) + a + 1)
                scored[a, n] = [claim(f"scores{a}", n, r).rearrange("p (c k) -> p c k", k=SEQ) for r in range(RG)]
                for b in range(2):
                    for h in range(HALF):
                        for r in range(RG):
                            score(a, n, 0, b, h, r)

            def scores_rest(a, n):
                for b in range(2):
                    for h in range(HALF):
                        for r in range(RG):
                            last = score(a, n, 1, b, h, r)
                            if b == 1 and h == HALF - 1:
                                last.then_inc(s_sc_mm[n % 2], 1)

            def score(a, n, t, b, h, r):
                at = slice(t * P + b * SEQ, t * P + (b + 1) * SEQ)
                return mm(scored[a, n][r][b * SEQ:(b + 1) * SEQ, 4 * t + 2 * h:4 * t + 2 * h + 2, :],
                          qT[32 * r:32 * r + 32, n % 2, h, at], k_bd[32 * r:32 * r + 32, a, h, :, at])

            def probs_turn(i, n):
                pe.wait_ge(s_exped[n % 2], 8 * (n // 2) + i + 1)
                ps = claim(f"probsT{i}", n)
                for c in range(4):
                    last = nc.tensor.transpose(ps[:, c * P:(c + 1) * P],
                                               probs[:, n % 2, i % RG, 2 * c:2 * c + 2, :].rearrange("p c k -> p (c k)"), ident)
                last.then_inc(s_pt_mm[n % 2], 1)

            def weigh(i, n):
                a, r = i // RG, i % RG
                if r == 0:
                    pe.wait_ge(s_v_ev[n % 2], 2 * (n // 2) + a + 1)
                    for t in range(TT):
                        weighed[a, n, t] = claim(f"weighed{a}", n, t)
                pe.wait_ge(s_pt_ev[n % 2], 8 * (n // 2) + i + 1)
                turned = probs[:, n % 2, r].rearrange("p c k -> p (c k)").rearrange("p (c q) -> p c q", q=P)
                for t in range(TT):
                    for b in range(2):
                        for h in range(HALF):
                            hp = h * RG + r
                            last = mm(weighed[a, n, t][b * SEQ:(b + 1) * SEQ, hp * 34:(hp + 1) * 34],
                                      turned[:, 2 * t + h, b * SEQ:(b + 1) * SEQ],
                                      v_bd[:, a, 2 * t + b, hp, :, :].rearrange("p q d -> p (q d)"))
                last.then_inc(s_pv_mm[n % 2], 1)

            def attended_turn(a, n):
                pe.wait_ge(s_o_norm[n % 2], 4 * (n // 2) + 2 * a + 2)
                to_features(claim(f"oT{a}", n), o_tok[:, n % 2]).then_inc(s_oT_mm[n % 2], 1)

            def attention_out(a, n):
                pe.wait_ge(s_w_loaded[1], 16)
                pe.wait_ge(s_oT_ev[n % 2], 2 * (n // 2) + a + 1)
                tokens_out(claim(f"attention_out{a}", n), ("w_ao", "w_co")[a], oT[:, n % 2]).then_inc(s_ao_mm[n % 2], 1)

            def mlp_up(m, n):
                pe.wait_ge(s_w_loaded[2], 16)
                pe.wait_ge(s_l0_h[n % 2], 3 * (n // 2) + 3)
                features_out(claim(f"hidden{m}", n), "w1", m * E, hT[:, n % 2]).then_inc(s_mlp_mm[n % 2], 1)

            def mlp_down(_, n):
                pe.wait_ge(s_gelu[n % 2], 4 * (n // 2) + 4)
                tokens_out(claim("mlp_down", n), "w2", hidden, 0, F1 // P).then_inc(s_w2_mm[n % 2], 1)

            def lora_in(_, n):
                pe.wait_ge(s_w_loaded[3], 16)
                pe.wait_ge(s_l1_in, n + 1)
                ps = claim("lora", n)
                for k in range(HALF):
                    mm(ps[:, 0:T], w("maa_w1", k, 0, P), xl[:, k, :], k == 0, k == HALF - 1)
                for k in range(HALF):
                    last = mm(ps[0:DM, T:2 * T], w("maa_w1", k, P, P + DM), xl[:, k, :], k == 0, k == HALF - 1)
                last.then_inc(s_xl_mm, 1)

            def mix(i, n):
                f = MIX_ORDER[i]
                pe.wait_ge(s_xl_ev, n + 1)
                ps = claim(f"mix{i}", n)
                at, weight, src = (32 * f, "maa_w2", lora) if f < 4 else (0, "maa_w2_last", lora_last)
                for m in range(HALF):
                    last = mm(ps[:, m * T:(m + 1) * T], w(weight, 0, m * P, (m + 1) * P, slice(at, at + DM)), src[at:at + DM, :])
                last.then_inc(s_mix_mm, 1)

            def decay_in(_, n):
                pe.wait_ge(s_mix_done, MIX * n + MIX_ORDER.index(1) + 1)
                ps = claim("decay_in", n)
                for k in range(HALF):
                    last = mm(ps[0:DD, 0:T], w("td_w1", k, 0, DD), xm[:, 1, k, :], k == 0, k == HALF - 1)
                last.then_inc(s_td1_mm, 1)

            def decay_out(_, n):
                pe.wait_ge(s_td_ev, n + 1)
                ps = claim("decay_out", n)
                for m in range(HALF):
                    last = mm(ps[:, m * T:(m + 1) * T], w("td_w2", 0, m * P, (m + 1) * P, slice(0, DD)), td_h[:, :])
                last.then_inc(s_td2_mm, 1)

            def kvr(i, n):
                f = (0, 2, 3)[i]
                pe.wait_ge(s_w_loaded[4], 16)
                pe.wait_ge(s_mix_done, MIX * n + MIX_ORDER.index(f) + 1)
                features_out(claim(f"kvr{i}", n), ("Wk", "Wv", "Wr")[i], 0, xm[:, f]).then_inc(s_kvr_mm, 1)

            def gate_in(_, n):
                pe.wait_ge(s_mix_done, MIX * n + MIX_ORDER.index(4) + 1)
                tokens_out(claim("gate", n), "Wg", xm[:, 4]).then_inc(s_g_mm, 1)

            def bonus(_, n):
                pe.wait_ge(s_init_heads, 1)
                pe.wait_ge(s_rk, n + 1)
                ps = claim("bonus", n)
                for m in range(HALF):
                    last = mm(ps[:, m * T:(m + 1) * T], u_heads[:, m, :], rk[:, m, :])
                last.then_inc(s_bonus_mm, 1)

            def spread(j, n):
                pe.wait_ge(s_consts_loaded, 16)
                pe.wait_ge(s_kvr_ev, 3 * n + 2)
                ps = claim(f"spread{j}", n)
                for m in range(HALF):
                    last = mm(ps[:, m * T:(m + 1) * T], C[:, C_SEL + j * P:C_SEL + (j + 1) * P], vT[:, m, :])
                last.then_inc(s_vb_mm, 1)

            def head_out(n):
                return banks[BANKS["wkv", n][0]][:, :].rearrange("p (t h d) -> p t h d", t=TT, h=HALF)

            def wkv_sum(j, n):
                pe.wait_ge(s_prod, S2 * n + j + 1)
                if j == 0:
                    claim("wkv", n)
                for t in range(TT):
                    for m in range(HALF):
                        last = mm(head_out(n)[:, t, m, :].rearrange("p (h j) -> p h j", j=S2)[:, :, j],
                                  wkv[:, j % SLOTS, m * GB + 2 * t:m * GB + 2 * t + 2, :].rearrange("p b t -> p (b t)"), heads,
                                  j == 0 and t == 0 and m == 0, False, skip_group_check=True)
                last.then_inc(s_wkv_mm, 1)

            def wkv_bonus(_, n):
                pe.wait_ge(s_bonus_v, n + 1)
                for t in range(TT):
                    for m in range(HALF):
                        last = mm(head_out(n)[:, t, m, :], rk[:, m, t * P:(t + 1) * P], ident, False, True, skip_group_check=True)
                last.then_inc(s_bonus_in, 1)

            def y_turn(_, n):
                pe.wait_ge(s_y, n + 1)
                to_features(claim("yT", n), y_tok).then_inc(s_yT_mm, 1)

            def wkv_out(_, n):
                pe.wait_ge(s_w_loaded[5], 16)
                pe.wait_ge(s_yT_ev, n + 1)
                tokens_out(claim("wkv_out", n), "Wo", yT).then_inc(s_wo_mm, 1)

            def ffn_key(_, n):
                pe.wait_ge(s_shift2, n + 1)
                features_out(claim("ffn_key", n), "Wfk", 0, xk).then_inc(s_fk_mm, 1)

            def ffn_gate(_, n):
                pe.wait_ge(s_shift2, n + 1)
                tokens_out(claim("ffn_gate", n), "Wfr", xr).then_inc(s_fr_mm, 1)

            def ffn_value(_, n):
                pe.wait_ge(s_kk, n + 1)
                tokens_out(claim("ffn_value", n), "Wfv", kk).then_inc(s_fv_mm, 1)

            weighed, scored = {}, {}
            steps = dict(norm_turn=norm_turn, query=query, key=key, value=value, scores=scores, scores_rest=scores_rest, probs_turn=probs_turn, weigh=weigh,
                         attended_turn=attended_turn, attention_out=attention_out, mlp_up=mlp_up, mlp_down=mlp_down,
                         lora_in=lora_in, mix=mix, decay_in=decay_in, decay_out=decay_out, kvr=kvr, gate_in=gate_in, bonus=bonus,
                         spread=spread, wkv_sum=wkv_sum, wkv_bonus=wkv_bonus, y_turn=y_turn, wkv_out=wkv_out,
                         ffn_key=ffn_key, ffn_gate=ffn_gate, ffn_value=ffn_value)
            pe.wait_ge(s_ident_loaded, 16)
            for name, i, n, _given in order("pe"):
                steps[name](i, n)

        @block.scalar
        def _(act):
            A = nc.scalar.activation

            def bank(use, n, i=0):
                return banks[BANKS[use, n][i]][:, :]

            def halves(ps):
                return ps.rearrange("p (h t) -> p h t", h=HALF)

            def flat(ap):
                return ap.rearrange("p t d -> p (t d)")

            def normed(i, n):
                if i < 3:
                    act.wait_ge(s_l0_normT[n % 2], 3 * (n // 2) + i + 1)
                    if i == 0 and n > 1:
                        act.wait_ge(s_mlp_mm[n % 2], 4 * (n // 2))
                    elif i == 1:
                        act.wait_ge(s_v_mm[n % 2], 2 * (n // 2) + 1)
                        act.wait_ge(s_q_mm[n % 2], 2 * (n // 2) + 1)
                        act.wait_ge(s_k_mm[n % 2], 2 * (n // 2) + 1)
                    elif i == 2:
                        act.wait_ge(s_q_mm[n % 2], 2 * (n // 2) + 2)
                    for h in range(HALF):
                        last = A(hT[:, n % 2, h, :], halves(bank(f"norm{i}", n))[:, h, :], ACT.Identity,
                                 scale=vec(f"ln{i + 1}_s", h), bias=vec(f"ln{i + 1}_b", h))
                    last.then_inc(s_l0_h[n % 2], 1)
                else:
                    act.wait_ge(s_l1_normT, 2 * n + i - 2)
                    if i == 3 and n:
                        act.wait_ge(s_l1_in, n)
                        act.wait_ge(s_mix_done, MIX * n)
                    if i == 4 and n:
                        act.wait_ge(s_shift2, n)
                    ln = ("r_ln1", "r_ln2")[i - 3]
                    for h in range(HALF):
                        last = A(xe[:, i - 3, h * GB:(h + 1) * GB, 1:], tokens(halves(bank(f"norm{i}", n)))[:, h * GB:(h + 1) * GB, :],
                                 ACT.Identity, scale=vec(f"{ln}_w", h), bias=vec(f"{ln}_b", h))
                    last.then_inc(s_l1_h, 1)

            def query_out(a, n):
                act.wait_ge(s_q_mm[n % 2], 2 * (n // 2) + a + 1)
                if a or n > 1:
                    act.wait_ge(s_sc_mm[n % 2], 8 * (n // 2) + 4 * a)
                for h in range(HALF):
                    last = A(qT[:, n % 2, h, :], halves(bank(f"query{a}", n))[:, h, :], ACT.Identity, bias=vec(("b_qkv", "b_q")[a], h))
                last.then_inc(s_q_ev[n % 2], 1)

            def key_out(a, n):
                act.wait_ge(s_init_keys, 1)
                act.wait_ge(s_k_mm[n % 2], 2 * (n // 2) + a + 1)
                if n:
                    act.wait_ge(s_sc_mm[1 - n % 2], 8 * ((n + 1) // 2) - 4 + 4 * a)
                for h in range(HALF):
                    for q in range(2):
                        last = A(k_bd[:, a, h, q, :], halves(bank(f"key{a}", n))[:, h, :], ACT.Identity,
                                 scale=C[:, C_PAR + q:C_PAR + q + 1], bias=key_bias[:, a, h, q:q + 1])
                last.then_inc(s_k_ev[n % 2], 1)

            def value_out(a, n):
                act.wait_ge(s_init_g, 1)
                act.wait_ge(s_v_mm[n % 2], 2 * (n // 2) + a + 1)
                if n:
                    act.wait_ge(s_pv_mm[1 - n % 2], 8 * ((n + 1) // 2) - 4 + 4 * a)
                src = bank(f"value{a}", n).rearrange("p (t h q d) -> p t h q d", t=TT, h=HP, q=2)
                dst = v_bd[:, a].rearrange("p (t b) h q d -> p t b h q d", b=2)
                for b in range(2):
                    for q in range(2):
                        last = A(dst[q * SEQ:(q + 1) * SEQ, :, b, :, q, 0:HD], src[b * SEQ:(b + 1) * SEQ, :, :, q, :], ACT.Copy)
                last.then_inc(s_v_ev[n % 2], 1)

            def probs_exp(i, n):
                act.wait_ge(s_shifted[n % 2], 8 * (n // 2) + i + 1)
                A(probs[:, n % 2, i % RG], probs[:, n % 2, i % RG], ACT.Exp).then_inc(s_exped[n % 2], 1)

            def probs_out(i, n):
                act.wait_ge(s_pt_mm[n % 2], 8 * (n // 2) + i + 1)
                A(probs[:, n % 2, i % RG].rearrange("p c k -> p (c k)"), bank(f"probsT{i}", n), ACT.Copy).then_inc(s_pt_ev[n % 2], 1)

            def attended(a, n):
                act.wait_ge(s_oT_mm[n % 2], 2 * (n // 2) + a + 1)
                if a or n > 1:
                    act.wait_ge(s_ao_mm[n % 2], 2 * (n // 2) + a)
                name, at = (("b_qkv", 4), ("b_kv", 2))[a]
                for h in range(HALF):
                    last = A(oT[:, n % 2, h, :], halves(bank(f"oT{a}", n))[:, h, :], ACT.Identity, bias=vec(name, at + h))
                last.then_inc(s_oT_ev[n % 2], 1)

            def gelu(m, n):
                act.wait_ge(s_mlp_mm[n % 2], 4 * (n // 2) + m + 1)
                if n:
                    act.wait_ge(s_w2_mm[1 - n % 2], (n + 1) // 2)
                for h in range(HALF):
                    last = A(hidden[:, 2 * m + h, :], halves(bank(f"hidden{m}", n))[:, h, :], ACT.Gelu_apprx_tanh,
                             bias=vec("b1", 2 * m + h))
                last.then_inc(s_gelu[n % 2], 1)

            def lora_out(_, n):
                act.wait_ge(s_xl_mm, n + 1)
                if n:
                    act.wait_ge(s_mix_mm, MIX * n)
                A(lora[:, :], bank("lora", n)[:, 0:T], ACT.Tanh)
                A(lora_last[:, :], bank("lora", n)[0:DM, T:2 * T], ACT.Tanh).then_inc(s_xl_ev, 1)

            def decay_tanh(_, n):
                act.wait_ge(s_td1_mm, n + 1)
                if n:
                    act.wait_ge(s_td2_mm, n)
                A(td_h[:, :], bank("decay_in", n)[0:DD, 0:T], ACT.Tanh).then_inc(s_td_ev, 1)

            def decay_exp(_, n):
                act.wait_ge(s_td2_mm, n + 1)
                if n:
                    act.wait_ge(s_decay, 2 * n)
                for h in range(HALF):
                    last = A(dec_e[:, h * GB:(h + 1) * GB, :], tokens(halves(bank("decay_out", n)))[:, h * GB:(h + 1) * GB, :],
                             ACT.Exp, bias=vec("time_decay", h))
                last.then_inc(s_decay, 1)
                act.wait_ge(s_init_g, 1)
                act.wait_ge(s_decay, 2 * n + 1)
                if n:
                    act.wait_ge(s_scanned, S2 * n)
                A(dec[:, :, 1:], dec_e[:, :, 0:SEQ - 1], ACT.Exp, scale=-1.0).then_inc(s_decay, 1)

            def kvr_out(i, n):
                act.wait_ge(s_kvr_mm, 3 * n + i + 1)
                if n and i == 0:
                    act.wait_ge(s_kv, S2 * n)
                    act.wait_ge(s_rk, n)
                if n and i == 1:
                    act.wait_ge(s_vb_mm, S2 * n)
                    act.wait_ge(s_bonus_v, n)
                if n and i == 2:
                    act.wait_ge(s_prod, S2 * n)
                    act.wait_ge(s_rk, n)
                A((kT, vT, rT)[i][:, :, :], halves(bank(f"kvr{i}", n)), ACT.Copy).then_inc(s_kvr_ev, 1)

            def gate_tanh(_, n):
                act.wait_ge(s_g_mm, n + 1)
                if n:
                    act.wait_ge(s_y, n)
                A(flat(gate[:, :, :]), bank("gate", n), ACT.Tanh, scale=0.5).then_inc(s_g_tanh, 1)

            def square(_, n):
                act.wait_ge(s_centred, n + 1)
                if n:
                    act.wait_ge(s_yT_mm, n)
                    act.wait_ge(s_fr_mm, n)
                A(flat(y_tok[:, :, :]), centred[:, :, :].rearrange("p h d -> p (h d)"), ACT.Square).then_inc(s_squared, 1)

            def y_out(_, n):
                act.wait_ge(s_yT_mm, n + 1)
                if n:
                    act.wait_ge(s_wo_mm, n)
                    act.wait_ge(s_fk_mm, n)
                A(yT[:, :, :], halves(bank("yT", n)), ACT.Copy).then_inc(s_yT_ev, 1)

            def ffn_square(_, n):
                act.wait_ge(s_fk_mm, n + 1)
                if n:
                    act.wait_ge(s_fv_mm, n)
                A(kk[:, :, :], halves(bank("ffn_key", n)), ACT.Relu).then_inc(s_fk_ev, 1)
                act.wait_ge(s_fk_ev, n + 1)
                A(kk[:, :, :], kk[:, :, :], ACT.Square).then_inc(s_kk, 1)

            def ffn_tanh(_, n):
                act.wait_ge(s_fr_mm, n + 1)
                if n:
                    act.wait_ge(s_out_stored, 16 * n)
                A(flat(result[:, :, :]), bank("ffn_gate", n), ACT.Tanh, scale=0.5).then_inc(s_fr_ev, 1)

            steps = dict(normed=normed, query_out=query_out, key_out=key_out, value_out=value_out, probs_exp=probs_exp,
                         probs_out=probs_out, attended=attended, gelu=gelu, lora_out=lora_out, decay_tanh=decay_tanh,
                         decay_exp=decay_exp, kvr_out=kvr_out, gate_tanh=gate_tanh, square=square, y_out=y_out,
                         ffn_square=ffn_square, ffn_tanh=ffn_tanh)
            act.wait_ge(s_v_loaded, 16)
            for name, i, n, _given in order("act"):
                steps[name](i, n)

        @block.vector
        def _(dve):
            v = nc.vector
            chain = [0]

            def link(ins):
                chain[0] += 1
                ins.then_inc(s_chain_v, 1)
                dve.wait_ge(s_chain_v, chain[0])

            def bank(use, n, i=0):
                return banks[BANKS[use, n][i]][:, :]

            def flat(ap):
                return ap.rearrange("p t d -> p (t d)")

            def norm_stats(i, n):
                which = 2 if i >= 3 else n % 2
                if i == 0:
                    dve.wait_ge(s_x_loaded[n % 2], 16 * (n // 2) + 16)
                elif i < 4:
                    dve.wait_ge(s_x_res[n % 2], 3 * (n // 2) + i)
                else:
                    dve.wait_ge(s_x1_done, n + 1)
                src = (x_in[:, n % 2], x_res[:, n % 2], x_res[:, n % 2], x_mid, x1)[i]
                for t in range(TT):
                    last = v.bn_stats(stats[:, which, t, :], src[:, t, :])
                link(last)
                for t in range(TT):
                    last = v.bn_aggr(moments[:, which, t, :], stats[:, which, t, :])
                link(last)
                if i >= 3:
                    if i == 4 or n:
                        dve.wait_ge(s_l1_rstd, 2 * n + i - 3)
                    v.tensor_scalar(var_eps[:, 2, :], moments[:, 2, :, 1], EPS, None, ALU.add).then_inc(s_l1_var, 1)
                else:
                    if i or n > 1:
                        dve.wait_ge(s_l0_rstd[n % 2], 3 * (n // 2) + i)
                    v.tensor_scalar(var_eps[:, n % 2, :], moments[:, n % 2, :, 1], EPS, None, ALU.add).then_inc(s_l0_var[n % 2], 1)

            def norm(i, n):
                which = 2 if i >= 3 else n % 2
                if i >= 3:
                    dve.wait_ge(s_l1_rstd, 2 * n + i - 2)
                    if i == 4 or n:
                        dve.wait_ge(s_l1_normT, 2 * n + i - 3)
                else:
                    dve.wait_ge(s_l0_rstd[n % 2], 3 * (n // 2) + i + 1)
                    if i or n > 1:
                        dve.wait_ge(s_l0_normT[n % 2], 3 * (n // 2) + i)
                src = (x_in[:, n % 2], x_res[:, n % 2], x_res[:, n % 2], x_mid, x1)[i]
                for t in range(TT):
                    last = v.tensor_scalar(xn[:, which, t, :], src[:, t, :], moments[:, which, t, 0:1], rstd[:, which, t:t + 1],
                                           ALU.subtract, ALU.mult)
                last.then_inc(s_l1_norm if which == 2 else s_l0_norm[n % 2], 1)

            def masking(i, n):
                a, r = i // RG, i % RG
                dve.wait_ge(s_masks_loaded, 3 * 16)
                dve.wait_ge(s_sc_mm[n % 2], 8 * (n // 2) + i + 1)
                if a or n > 1:
                    dve.wait_ge(s_pv_mm[n % 2], 8 * (n // 2) + i - RG + 1)
                ps = bank(f"scores{a}", n, r).rearrange("p (t c k) -> p t c k", t=TT, c=4)
                pr = probs[:, n % 2, r].rearrange("p (t c) k -> p t c k", t=TT)
                v.tensor_tensor(pr, ps, mask_of(a, n, mask1, mask2), ALU.mult).then_inc(s_masked[n % 2], 1)

            def shifting(i, n):
                r = i % RG
                dve.wait_ge(s_biased[n % 2], 8 * (n // 2) + i + 1)
                link(v.tensor_reduce(row_max[:, n % 2, r, :], probs[:, n % 2, r], AX_X, ALU.max))
                v.tensor_tensor(probs[:, n % 2, r], probs[:, n % 2, r], row_max[:, n % 2, r, :].unsqueeze(2).broadcast_to([P, 8, SEQ]),
                                ALU.subtract).then_inc(s_shifted[n % 2], 1)

            def attended_norm(a, n):
                dve.wait_ge(s_pv_mm[n % 2], 8 * (n // 2) + 4 * a + 4)
                if a or n > 1:
                    dve.wait_ge(s_oT_mm[n % 2], 2 * (n // 2) + a)
                ps = [bank(f"weighed{a}", n, t)[:, 0:NH * (HD + 1)].rearrange("p (h d) -> p h d", h=NH) for t in range(TT)]
                for t in range(TT):
                    last = v.reciprocal(rden[:, n % 2, t, :], ps[t][:, :, HD])
                link(last)
                for t in range(TT):
                    v.tensor_tensor(o_tok[:, n % 2, t, :].rearrange("p (h d) -> p h d", h=NH), ps[t][:, :, 0:HD],
                                    rden[:, n % 2, t, :].unsqueeze(2).broadcast_to([P, NH, HD]), ALU.mult).then_inc(s_o_norm[n % 2], 1)

            def residual(i, n):
                if i == 2:
                    dve.wait_ge(s_w2_mm[n % 2], (n // 2) + 1)
                    if n:
                        dve.wait_ge(s_x1_done, n)
                else:
                    dve.wait_ge(s_ao_mm[n % 2], 2 * (n // 2) + i + 1)
                dve.wait_ge(s_x_biased[n % 2], 3 * (n // 2) + i + 1)
                use, dst = (("attention_out0", x_res[:, n % 2]), ("attention_out1", x_res[:, n % 2]), ("mlp_down", x_mid))[i]
                v.tensor_tensor(flat(dst[:, :, :]), bank(use, n), flat(x_bias[:, n % 2, :, :]), ALU.add).then_inc(s_x_res[n % 2], 1)

            def lerp(dst, i, name):
                for h in range(HALF):
                    at = slice(h * GB, (h + 1) * GB)
                    last = v.scalar_tensor_tensor(tokens(dst)[:, at, :], tokens((sx, sx_ffn)[i][:, :, :])[:, at, :], vec(name, h),
                                                  xe[:, i, at, 1:], ALU.mult, ALU.add)
                return last

            def shift(i, n):
                dve.wait_ge(s_l1_h, 2 * n + i + 1)
                dve.wait_ge(s_l1_edge, 2 * n + i + 1)
                if i and n:
                    dve.wait_ge(s_fv_mm, n)
                link(v.tensor_tensor(tokens((sx, sx_ffn)[i][:, :, :]), xe[:, i, :, 0:SEQ], xe[:, i, :, 1:], ALU.subtract))
                if i == 0:
                    if n:
                        dve.wait_ge(s_xl_mm, n)
                    lerp(xl[:, :, :], 0, "maa_x").then_inc(s_l1_in, 1)
                else:
                    if n:
                        dve.wait_ge(s_fk_mm, n)
                        dve.wait_ge(s_fr_mm, n)
                    lerp(xk[:, :, :], 1, "mix_k")
                    lerp(xr[:, :, :], 1, "mix_r").then_inc(s_shift2, 1)

            def mixing(i, n):
                f = MIX_ORDER[i]
                dve.wait_ge(s_mix_mm, MIX * n + i + 1)
                if n:
                    if f == 1:
                        dve.wait_ge(s_td1_mm, n)
                    elif f == 4:
                        dve.wait_ge(s_g_mm, n)
                    else:
                        dve.wait_ge(s_kvr_mm, 3 * n)
                ps = bank(f"mix{i}", n).rearrange("p (h t) -> p h t", h=HALF)
                for h in range(HALF):
                    last = v.scalar_tensor_tensor(xm[:, f, h, :], ps[:, h, :], vec("maa_stack", 2 * f + h), sx[:, h, :],
                                                  ALU.add, ALU.mult)
                last.then_inc(s_mixed, 1)

            def gating(_, n):
                dve.wait_ge(s_g_tanh, n + 1)
                v.scalar_tensor_tensor(flat(gate[:, :, :]), flat(gate[:, :, :]), 1.0, bank("gate", n), ALU.add, ALU.mult).then_inc(s_gate, 1)

            def bonus_value(_, n):
                dve.wait_ge(s_bonus_mm, n + 1)
                dve.wait_ge(s_kvr_ev, 3 * n + 2)
                v.tensor_tensor(rk[:, :, :], bank("bonus", n).rearrange("p (h t) -> p h t", h=HALF), vT[:, :, :],
                                ALU.mult).then_inc(s_bonus_v, 1)

            def recur(j, n):
                at = j % SLOTS
                if j == 0:
                    dve.wait_ge(s_s_loaded, 2 * 16)
                    dve.wait_ge(s_decay, 2 * n + 2)
                    dve.wait_ge(s_kvr_ev, 3 * n + 3)
                dve.wait_ge(s_vb_mm, S2 * n + j + 1)
                if n or j >= SLOTS:
                    dve.wait_ge(s_wkv_mm, S2 * n + j - SLOTS + 1)
                v.tensor_copy(wkv[:, at, :, 0], s0_sb[:, n, j, :])
                vb = bank(f"spread{j}", n).rearrange("p (c t) -> p c t", t=SEQ)
                v.tensor_tensor(wkv[:, at, :, 1:], vb[:, :, 0:SEQ - 1], tokens(kT[:, :, :])[:, :, 0:SEQ - 1], ALU.mult).then_inc(s_kv, 1)
                dve.wait_ge(s_kv, S2 * n + j + 1)
                line = wkv[:, at, :, :].rearrange("p c t -> p (c t)")
                v.tensor_tensor_scan(line, dec[:, :, :].rearrange("p c t -> p (c t)"), line, 0.0, ALU.mult, ALU.add).then_inc(s_scanned, 1)
                dve.wait_ge(s_scanned, S2 * n + j + 1)
                v.tensor_tensor(wkv[:, at, :, :], wkv[:, at, :, :], tokens(rT[:, :, :]), ALU.mult).then_inc(s_prod, 1)

            def centre(_, n):
                dve.wait_ge(s_bonus_in, n + 1)
                ps = bank("wkv", n).rearrange("p (h d) -> p h d", d=S2)
                link(v.tensor_reduce(head_sum[:, :], ps, AX_X, ALU.add))
                if n:
                    dve.wait_ge(s_y, n)
                v.scalar_tensor_tensor(centred[:, :, :], head_sum[:, :].unsqueeze(2).broadcast_to([P, TT * H2, S2]), -1.0 / S2,
                                       ps, ALU.mult, ALU.add).then_inc(s_centred, 1)

            def head_norm(_, n):
                dve.wait_ge(s_squared, n + 1)
                y, q, t, h = (nw[:, i, :] for i in range(4))
                link(v.tensor_reduce(t, y_tok[:, :, :].rearrange("p t (h d) -> p (t h) d", d=S2), AX_X, ALU.add))
                link(v.tensor_scalar(q, t, 1.0 / S2, EPS, ALU.mult, ALU.add))
                link(v.tensor_scalar(t.bitcast(I32), q.bitcast(I32), 1, None, ALU.logical_shift_right))
                link(v.tensor_scalar(y.bitcast(I32), t.bitcast(I32), -1.0, float(0x5F3759DF), ALU.mult, ALU.add))
                link(v.tensor_scalar(h, q, -0.5, None, ALU.mult))
                for _i in range(3):
                    link(v.tensor_tensor(t, y, y, ALU.mult))
                    link(v.tensor_tensor(t, t, h, ALU.mult))
                    link(v.scalar_tensor_tensor(y, t, 1.5, y, ALU.add, ALU.mult))
                v.tensor_tensor(centred[:, :, :], centred[:, :, :], y.unsqueeze(2).broadcast_to([P, TT * H2, S2]),
                                ALU.mult).then_inc(s_normed, 1)

            def group_norm(_, n):
                dve.wait_ge(s_rows_loaded, 16)
                dve.wait_ge(s_normed, n + 1)
                c = centred[:, :, :].rearrange("p (t h) d -> p t (h d)", t=TT)
                v.tensor_tensor(c, c, row("gn_w"), ALU.mult).then_inc(s_gn_out, 1)
                dve.wait_ge(s_gn_out, 2 * n + 1)
                v.tensor_tensor(c, c, row("gn_b"), ALU.add).then_inc(s_gn_out, 1)

            def gated(_, n):
                dve.wait_ge(s_gn_out, 2 * n + 2)
                dve.wait_ge(s_gate, n + 1)
                v.scalar_tensor_tensor(flat(y_tok[:, :, :]), centred[:, :, :].rearrange("p h d -> p (h d)"), 0.5, flat(gate[:, :, :]),
                                       ALU.mult, ALU.mult).then_inc(s_y, 1)

            def wkv_residual(_, n):
                dve.wait_ge(s_wo_mm, n + 1)
                if n:
                    dve.wait_ge(s_result, n)
                v.tensor_tensor(flat(x1[:, :, :]), bank("wkv_out", n), flat(x_mid[:, :, :]), ALU.add).then_inc(s_x1_done, 1)

            def finish(_, n):
                dve.wait_ge(s_fv_mm, n + 1)
                dve.wait_ge(s_fr_ev, n + 1)
                v.scalar_tensor_tensor(flat(result[:, :, :]), flat(result[:, :, :]), 1.0, bank("ffn_value", n), ALU.add, ALU.mult).then_inc(s_fv_ev, 1)
                dve.wait_ge(s_fv_ev, n + 1)
                v.scalar_tensor_tensor(flat(result[:, :, :]), flat(result[:, :, :]), 0.5, flat(x1[:, :, :]), ALU.mult, ALU.add).then_inc(s_result, 1)

            def init_keys(_, n):
                dve.wait_ge(s_v_loaded, 16)
                dve.wait_ge(s_ident_loaded, 16)
                for a, (name, at) in enumerate((("b_qkv", 2), ("b_kv", 0))):
                    for h in range(HALF):
                        last = v.tensor_scalar(key_bias[:, a, h, :], C[:, C_PAR:C_PAR + 2], vec(name, at + h), None, ALU.mult)
                last.then_inc(s_init_keys, 1)

            def init_masks(_, n):
                dve.wait_ge(s_masks_loaded, 3 * 16)
                v.tensor_scalar(mask1b[:, :], mask1[:, :], -1.0, 10000.0, ALU.add, ALU.mult)
                v.tensor_scalar(mask2b[:, :, :], mask2[:, :, :], -1.0, 10000.0, ALU.add, ALU.mult).then_inc(s_init_masks, 1)

            def init_heads(_, n):
                dve.wait_ge(s_consts_loaded, 16)
                for h in range(HALF):
                    last = v.tensor_scalar(u_heads[:, h, :], head_ones, vec("u", h), None, ALU.mult)
                last.then_inc(s_init_heads, 1)

            steps = dict(init_keys=init_keys, init_masks=init_masks, init_heads=init_heads, norm_stats=norm_stats, norm=norm,
                         masking=masking, shifting=shifting, attended_norm=attended_norm, residual=residual, shift=shift,
                         mixing=mixing, gating=gating, bonus_value=bonus_value, recur=recur, centre=centre,
                         head_norm=head_norm, group_norm=group_norm, gated=gated, wkv_residual=wkv_residual, finish=finish)
            for name, i, n, _given in order("dve"):
                steps[name](i, n)

        @block.gpsimd
        def _(pool):
            g = nc.gpsimd

            def rsqrt(i, n):
                if i >= 3:
                    pool.wait_ge(s_l1_var, 2 * n + i - 2)
                    if i == 4 or n:
                        pool.wait_ge(s_l1_norm, 2 * n + i - 3)
                    g.tensor_tensor(rstd[:, 2, :], var_eps[:, 2, :], minus_half[:, :], ALU.pow).then_inc(s_l1_rstd, 1)
                else:
                    pool.wait_ge(s_l0_var[n % 2], 3 * (n // 2) + i + 1)
                    if i or n > 1:
                        pool.wait_ge(s_l0_norm[n % 2], 3 * (n // 2) + i)
                    g.tensor_tensor(rstd[:, n % 2, :], var_eps[:, n % 2, :], minus_half[:, :], ALU.pow).then_inc(s_l0_rstd[n % 2], 1)

            def bias_residual(i, n):
                if i:
                    pool.wait_ge(s_x_res[n % 2], 3 * (n // 2) + i)
                else:
                    pool.wait_ge(s_x_loaded[n % 2], 16 * (n // 2) + 16)
                    if n > 1:
                        pool.wait_ge(s_x_res[n % 2], 3 * (n // 2))
                pool.wait_ge(s_rows_loaded, 16)
                src = (x_in if i == 0 else x_res)[:, n % 2]
                g.tensor_tensor(x_bias[:, n % 2, :, :], src[:, :, :], row(("b_ao", "b_co", "b2")[i]), ALU.add).then_inc(s_x_biased[n % 2], 1)

            def mask_bias(i, n):
                a, r = i // RG, i % RG
                pool.wait_ge(s_init_masks, 1)
                pool.wait_ge(s_masked[n % 2], 8 * (n // 2) + i + 1)
                pr = probs[:, n % 2, r].rearrange("p (t c) k -> p t c k", t=TT)
                g.tensor_tensor(pr, pr, mask_of(a, n, mask1b, mask2b), ALU.add).then_inc(s_biased[n % 2], 1)

            def edge_in(i, n):
                pool.wait_ge(s_s_loaded, 2 * 16)
                if n and i == 0:
                    pool.wait_ge(s_l1_in, n)
                if n and i == 1:
                    pool.wait_ge(s_shift2, n)
                g.tensor_copy(xe[:, i, :, 0].rearrange("p (h b) -> p h b", h=HALF), edge[:, i, :, n * GB:(n + 1) * GB]).then_inc(s_l1_edge, 1)

            def mix_add(i, n):
                f = MIX_ORDER[i]
                pool.wait_ge(s_mixed, MIX * n + i + 1)
                g.tensor_tensor(tokens(xm[:, f]), tokens(xm[:, f]), xe[:, 0, :, 1:], ALU.add).then_inc(s_mix_done, 1)

            def rk_product(_, n):
                pool.wait_ge(s_kvr_ev, 3 * n + 3)
                if n:
                    pool.wait_ge(s_bonus_in, n)
                g.tensor_tensor(rk[:, :, :], kT[:, :, :], rT[:, :, :], ALU.mult).then_inc(s_rk, 1)

            g.memset(v_bd[:, :, :, :, :, :], 0.0)
            g.memset(dec[:, :, 0:1], 0.0)
            g.memset(minus_half[:, :], -0.5)
            g.drain()
            for q in range(2):
                last = g.memset(v_bd[q * SEQ:(q + 1) * SEQ, :, :, :, q, HD:HD + 1], 1.0)
            last.then_inc(s_init_g, 1)
            pool.wait_ge(s_init_g, 1)
            steps = dict(rsqrt=rsqrt, bias_residual=bias_residual, mask_bias=mask_bias, edge_in=edge_in, mix_add=mix_add,
                         rk_product=rk_product)
            for name, i, n, _given in order("pool"):
                steps[name](i, n)


def kernel(**inputs):
    import numpy as np
    import concourse.bacc as bacc
    from concourse.bass_utils import run_bass_kernel_spmd as run

    def a(name):
        return np.asarray(inputs[name])

    l0 = {k[len("L0_xattn_"):]: np.asarray(v) for k, v in inputs.items() if k.startswith("L0_xattn_")}
    l1 = {k[len("L1_xattn_"):]: np.asarray(v) for k, v in inputs.items() if k.startswith("L1_xattn_")}

    src = {n: l0[n] for n in ("w_qkv", "w_ao", "w_q", "w_kv", "w_co", "w1", "w2")}
    src |= {n: l1[n] for n in ("maa_w1", "td_w1", "td_w2")}
    src |= {n: l1[n].T for n in ("Wk", "Wv", "Wr", "Wg", "Wo", "Wfk", "Wfr", "Wfv")}
    src["maa_w2"] = l1["maa_w2"][:4].reshape(4 * DM, E)
    src["maa_w2_last"] = l1["maa_w2"][4]
    W = np.zeros((P, W_COLS), np.float32)
    for name, (at, kt, n) in W_AT.items():
        m = src[name]
        for k in range(kt):
            part = m[k * P:(k + 1) * P]
            W[:part.shape[0], at + k * n:at + (k + 1) * n] = part

    vsrc = {n: l0[n] for n in ("ln1_s", "ln1_b", "ln2_s", "ln2_b", "ln3_s", "ln3_b", "b_qkv", "b_q", "b_kv", "b1")}
    vsrc |= {"r_ln1_w": l1["ln1_w"], "r_ln1_b": l1["ln1_b"], "r_ln2_w": l1["ln2_w"], "r_ln2_b": l1["ln2_b"],
             "maa_x": l1["maa_x"], "maa_stack": l1["maa_stack"], "time_decay": l1["time_decay"], "u": l1["u"],
             "mix_k": l1["ffn_maa_k"], "mix_r": l1["ffn_maa_r"]}
    V = np.concatenate([vsrc[name].reshape(n, P).T for name, n in VECTORS], axis=1)
    R = np.stack([l0["b_ao"], l0["b_co"], l0["b2"], l1["gn_w"], l1["gn_b"]])

    C = np.zeros((P, C_COLS), np.float32)
    at = np.arange(P)
    C[at, C_IDENT + at] = 1
    for j in range(S2):
        for i in range(S2):
            C[at[::S2] + j, C_SEL + j * P + at[::S2] + i] = 1
    C[at, C_HEADS + at // S2] = 1
    C[:, C_ONES:C_ONES + P] = at[:, None] // S2 == at[None, :] // S2
    for q in range(2):
        C[:, C_PAR + q] = (at // HD % 2 == q) * HD ** -0.5

    ctx = a("ctx_2048")
    s0 = ctx[:, 2:2 + S2].reshape(GROUPS, GB, HALF, P, S2).transpose(3, 0, 4, 2, 1).reshape(P, GROUPS, S2, HALF * GB)
    state01 = ctx[:, 1::-1].reshape(NB, 2, HALF, P).transpose(3, 1, 2, 0)
    arrays = {
        "x_in_dram": a("x").reshape(NB * SEQ, E),
        "ctxT_dram": ctx.reshape(NB * SEQ, HALF, P).transpose(2, 1, 0),
        "s0_dram": s0,
        "state01_dram": state01,
        "self_mask_dram": a("mask_1x1xSxS2_fc1").reshape(SEQ, SEQ),
        "cross_mask_dram": a("mask_Bx1xSxS2_ff1").reshape(NB, SEQ, SEQ),
        "weights_dram": W, "vectors_dram": V, "rows_dram": R, "consts_dram": C,
    }
    arrays = {k: np.ascontiguousarray(v) for k, v in arrays.items()}
    nc = bacc.Bacc("TRN2", target_bir_lowering=False, num_devices=1)
    args = [nc.dram_tensor(k, v.shape, F32, kind="ExternalInput").ap() for k, v in arrays.items()]
    args.append(nc.dram_tensor("out_dram", (NB * SEQ, E), F32, kind="ExternalOutput").ap())
    build(nc, *args)
    r = run(nc, [arrays], core_ids=[0])
    return r.results[0]["out_dram"].reshape(NB, SEQ, E)
```
